# Optimizing a Trainium2 kernel written in Bass

```python
import numpy as np
import jax
import jax.numpy as jnp

def _softmax(x, axis=-1):
    return jax.nn.softmax(x, axis=axis)

def _gelu(x):
    return jax.nn.gelu(x, approximate=True)

def _silu(x):
    return jax.nn.silu(x)

def _sigmoid(x):
    return jax.nn.sigmoid(x)

def _layernorm(x, axis=-1, eps=1e-05):
    m = jnp.mean(x, axis=axis, keepdims=True)
    v = jnp.var(x, axis=axis, keepdims=True)
    return (x - m) / jnp.sqrt(v + eps)

def _scatter_add(tgt, idx, src, axis=0):
    return tgt.at[idx].add(src)

def _segment_sum(src, seg, n):
    return jax.ops.segment_sum(src, seg, n)
kernel_name = 'mk_gnn_resnorm_d2_gnn_r8_3cdf98'

def setup_inputs(seed: int=0):
    np.random.seed(seed)
    _w = jnp.asarray

    def _rec_inputs():
        import jax
        import jax.numpy as jnp
        _gk = jax.random.key(seed)
        x = -0.0003713 + 1 * jax.random.normal(jax.random.fold_in(_gk, 1), (12500, 256), jnp.float32)
        src = jax.random.randint(jax.random.fold_in(_gk, 2), (200000,), 0, 12500, jnp.int32)
        dst = jax.random.randint(jax.random.fold_in(_gk, 3), (200000,), 0, 12500, jnp.int32)
        _o = jnp.argsort(dst, stable=True)
        src = src[_o]
        dst = dst[_o]
        edge_type_64 = jax.random.randint(jax.random.fold_in(_gk, 12), (200000,), 0, 64, jnp.int32)
        return (x, src, dst, edge_type_64)
    x, src, dst, edge_type_64 = _rec_inputs()

    def _L0_gnn_setup():
        import jax, jax.numpy as jnp
        import numpy as np
        N_NODES = 6250
        N_EDGES = 62500
        IN_DIM = 256
        HID = 64
        HEADS = 4
        N_REL = 64
        key = jax.random.key(seed)
        ks = jax.random.split(key, 16)
        s = 0.02
        return {'node_features': jax.random.normal(ks[0], (N_NODES, IN_DIM), jnp.float32), 'edge_index': jax.random.randint(ks[1], (2, N_EDGES), 0, N_NODES, jnp.int32), 'edge_relations': jax.random.randint(ks[2], (N_EDGES,), 0, N_REL, jnp.int32), 'query_emb': jax.random.normal(ks[3], (IN_DIM,), jnp.float32), 'Wq': jax.random.normal(ks[4], (IN_DIM, HID * HEADS), jnp.float32) * s, 'bq': jnp.zeros((HID * HEADS,), jnp.float32), 'Wk': jax.random.normal(ks[5], (IN_DIM, HID * HEADS), jnp.float32) * s, 'bk': jnp.zeros((HID * HEADS,), jnp.float32), 'Wv': jax.random.normal(ks[6], (IN_DIM, HID * HEADS), jnp.float32) * s, 'bv': jnp.zeros((HID * HEADS,), jnp.float32), 'rel_w': jax.random.normal(ks[7], (N_REL, HID), jnp.float32) * s, 'Wo': jax.random.normal(ks[8], (HID * HEADS, IN_DIM), jnp.float32) * s, 'bo': jnp.zeros((IN_DIM,), jnp.float32), 'gamma': jnp.ones((IN_DIM,), jnp.float32), 'beta': jnp.zeros((IN_DIM,), jnp.float32)}
    _L0_gnn_all = _L0_gnn_setup()
    _L0_gnn_in = {k: v for k, v in _L0_gnn_all.items() if k in ('query_emb', 'Wq', 'bq', 'Wk', 'bk', 'Wv', 'bv', 'rel_w', 'Wo', 'bo', 'gamma', 'beta')}
    del _L0_gnn_all

    def _L1_gnn_setup():
        import jax, jax.numpy as jnp
        import numpy as np
        N = 1250
        E = 40000
        D = 256
        key = jax.random.key(seed)
        ks = jax.random.split(key, 10)
        s = 1.0 / np.sqrt(D)
        return {'x0': jax.random.normal(ks[0], (N, D), jnp.float32), 'edge_index': jax.random.randint(ks[1], (2, E), 0, N, jnp.int32), 'W1': jax.random.normal(ks[2], (D, D), jnp.float32) * s, 'b1': jax.random.normal(ks[3], (D,), jnp.float32) * s, 'W2': jax.random.normal(ks[4], (D, D), jnp.float32) * s, 'b2': jax.random.normal(ks[5], (D,), jnp.float32) * s, 'wa1': jax.random.normal(ks[6], (D,), jnp.float32) * s, 'ba1': jax.random.normal(ks[7], (1,), jnp.float32) * s, 'wa2': jax.random.normal(ks[8], (D,), jnp.float32) * s, 'ba2': jax.random.normal(ks[9], (1,), jnp.float32) * s}
    _L1_gnn_all = _L1_gnn_setup()
    _L1_gnn_in = {k: v for k, v in _L1_gnn_all.items() if k in ('W1', 'b1', 'W2', 'b2', 'wa1', 'ba1', 'wa2', 'ba2')}
    del _L1_gnn_all
    return {'x': x, 'src': src, 'dst': dst, 'edge_type_64': edge_type_64, 'L0_gnn_query_emb': _L0_gnn_in['query_emb'], 'L0_gnn_Wq': _L0_gnn_in['Wq'], 'L0_gnn_bq': _L0_gnn_in['bq'], 'L0_gnn_Wk': _L0_gnn_in['Wk'], 'L0_gnn_bk': _L0_gnn_in['bk'], 'L0_gnn_Wv': _L0_gnn_in['Wv'], 'L0_gnn_bv': _L0_gnn_in['bv'], 'L0_gnn_rel_w': _L0_gnn_in['rel_w'], 'L0_gnn_Wo': _L0_gnn_in['Wo'], 'L0_gnn_bo': _L0_gnn_in['bo'], 'L0_gnn_gamma': _L0_gnn_in['gamma'], 'L0_gnn_beta': _L0_gnn_in['beta'], 'L1_gnn_W1': _L1_gnn_in['W1'], 'L1_gnn_b1': _L1_gnn_in['b1'], 'L1_gnn_W2': _L1_gnn_in['W2'], 'L1_gnn_b2': _L1_gnn_in['b2'], 'L1_gnn_wa1': _L1_gnn_in['wa1'], 'L1_gnn_ba1': _L1_gnn_in['ba1'], 'L1_gnn_wa2': _L1_gnn_in['wa2'], 'L1_gnn_ba2': _L1_gnn_in['ba2']}

def reference(x, src, dst, edge_type_64, L0_gnn_query_emb, L0_gnn_Wq, L0_gnn_bq, L0_gnn_Wk, L0_gnn_bk, L0_gnn_Wv, L0_gnn_bv, L0_gnn_rel_w, L0_gnn_Wo, L0_gnn_bo, L0_gnn_gamma, L0_gnn_beta, L1_gnn_W1, L1_gnn_b1, L1_gnn_W2, L1_gnn_b2, L1_gnn_wa1, L1_gnn_ba1, L1_gnn_wa2, L1_gnn_ba2):
    import jax
    import jax.numpy as jnp

    def _L0_gnn_ref(node_features, edge_index, edge_relations, query_emb, Wq, bq, Wk, bk, Wv, bv, rel_w, Wo, bo, gamma, beta):
        import jax, jax.numpy as jnp
        import numpy as np
        N_NODES = 6250
        N_EDGES = 62500
        IN_DIM = 256
        HID = 64
        HEADS = 4
        N_REL = 64
        N = node_features.shape[0]
        D = rel_w.shape[1]
        H = Wq.shape[1] // D
        enh = node_features + 0.1 * query_emb[None, :]
        Q = (enh @ Wq + bq).reshape(N, H, D)
        K = (enh @ Wk + bk).reshape(N, H, D)
        V = (enh @ Wv + bv).reshape(N, H, D)
        src, dst = (edge_index[0], edge_index[1])
        rel = rel_w[edge_relations]
        mod_k = K[src] + 0.2 * rel[:, None, :]
        scores = jnp.einsum('ehd,ehd->eh', Q[dst], mod_k) / D ** 0.5
        seg_max = jax.ops.segment_max(scores, dst, num_segments=N)
        ex = jnp.exp(scores - seg_max[dst])
        denom = jax.ops.segment_sum(ex, dst, num_segments=N)
        w = ex / denom[dst]
        agg = jax.ops.segment_sum(w[:, :, None] * V[src], dst, num_segments=N)
        deg = jax.ops.segment_sum(jnp.ones((src.shape[0],), jnp.float32), dst, num_segments=N)
        msgs = jnp.where(deg[:, None, None] > 0, agg, V)
        out = msgs.reshape(N, H * D) @ Wo + bo
        x = out + node_features
        mu = jnp.mean(x, axis=-1, keepdims=True)
        var = jnp.var(x, axis=-1, keepdims=True)
        return (x - mu) / jnp.sqrt(var + 1e-05) * gamma + beta

    def _L1_gnn_ref(x0, edge_index, W1, b1, W2, b2, wa1, ba1, wa2, ba2):
        import jax, jax.numpy as jnp
        import numpy as np
        N = 1250
        E = 40000
        D = 256
        n = x0.shape[0]
        leaky = lambda v: jax.nn.leaky_relu(v, 0.2)
        x0_i = leaky(x0 @ W1 + b1)
        x0_j = leaky(x0 @ W2 + b2)
        a1 = x0_i @ wa1 + ba1[0]
        a2 = x0_j @ wa2 + ba2[0]
        row, col = (edge_index[0], edge_index[1])
        att = jax.nn.sigmoid(a1[row] + a2[col])
        msg = att[:, None] * x0_j[col]
        out = jax.ops.segment_sum(msg, row, num_segments=n)
        return out + x0
    edge_index = jnp.stack([src, dst])
    x = _layernorm(x + _L0_gnn_ref(x, edge_index, edge_type_64, L0_gnn_query_emb, L0_gnn_Wq, L0_gnn_bq, L0_gnn_Wk, L0_gnn_bk, L0_gnn_Wv, L0_gnn_bv, L0_gnn_rel_w, L0_gnn_Wo, L0_gnn_bo, L0_gnn_gamma, L0_gnn_beta), axis=-1)
    x = _layernorm(x + _L1_gnn_ref(x, edge_index, L1_gnn_W1, L1_gnn_b1, L1_gnn_W2, L1_gnn_b2, L1_gnn_wa1, L1_gnn_ba1, L1_gnn_wa2, L1_gnn_ba2), axis=-1)
    return x

_drawn_inputs = setup_inputs


def setup_inputs(seed=0):
    import zlib

    import numpy as np

    out = dict(_drawn_inputs(seed))
    spreads = {'L0_gnn_bq': (0.0, 0.8),
     'L0_gnn_bk': (0.0, 2.0),
     'L0_gnn_bv': (0.0, 0.1),
     'L0_gnn_bo': (0.0, 0.1),
     'L0_gnn_gamma': (1.0, 0.2),
     'L0_gnn_beta': (0.0, 0.1)}
    factors = {'L0_gnn_query_emb': 5.262,
     'L0_gnn_Wq': 8.0,
     'L0_gnn_Wk': 8.0,
     'L0_gnn_Wv': 2.92,
     'L0_gnn_rel_w': 64.0,
     'L1_gnn_b1': 8.0}
    for name, (base, spread) in spreads.items():
        noise = np.random.default_rng([zlib.crc32(name.encode()), seed]).standard_normal(out[name].shape)
        drawn = base * np.exp(spread * noise) if base else spread * noise
        out[name] = jnp.asarray(drawn.astype(out[name].dtype))
    for name, factor in factors.items():
        out[name] = (out[name] * factor).astype(out[name].dtype)
    return out
```

```python
import concourse.bass as bass
from concourse import mybir
from contextlib import ExitStack

fp32 = mybir.dt.float32
bf16 = mybir.dt.bfloat16
i32 = mybir.dt.int32
ALU = mybir.AluOpType
ACT = mybir.ActivationFunctionType
AX = mybir.AxisListType

P = 128
N = 12500
E = 200000
D = 256
H = 4
DH = D // H
R = 64
NB = -(-N // P)
LAST_ROWS = N - (NB - 1) * P
T = -(-E // P)
U = 4
V = 4
TURN = U * V
LAG = 2
G = -(-(T + NB - 1) // TURN) * V
S = G * U
C = S // P
AW = D + H
XW = D + 4
LOGN = 18
F = (1 << LOGN) // P
NODE_BITS = 14
NODE_MASK = (1 << NODE_BITS) - 1
KEY_BIAS = 1 << 30
PAD_NODE = NB * P - 1
EPS = 1e-5
LOWEST = -1.0e30
assert S % P == 0 and C * P >= T and PAD_NODE >= N and PAD_NODE < (1 << NODE_BITS) and NB <= P


class Serial:

    def __init__(self, eng, sem, per_loop=0):
        self.eng, self.sem, self.per_loop, self.n, self.turn = eng, sem, per_loop, 0, 0

    def __call__(self, ins):
        self.n += 1
        ins.then_inc(self.sem, 1)
        self.eng.wait_ge(self.sem, self.turn + self.n)

    def enter(self, i, per_turn):
        self.turn, self.start, self.per = i * per_turn, self.n, per_turn

    def leave(self, turns):
        assert self.n - self.start == self.per, (self.n, self.start, self.per)
        self.n, self.turn = self.start + self.per * turns, 0


def block_pairs(eng, body):
    body(0, 0)
    body(1, 1)
    with eng.Fori(1, NB // 2 - 1) as i:
        body(2 * i, 0)
        body(2 * i + 1, 1)
    body(NB - 2, 0)
    body(NB - 1, 1)


def early(b, n=2):
    return isinstance(b, int) and b < n


def skewed(eng, stages, step=None):
    deepest = max(lag for lag, _ in stages)
    first = -(-(deepest + 4) // 4) * 4
    last = first + (NB - 1 - first) // 4 * 4

    def turn(i, w):
        for lag, stage in stages:
            if not isinstance(i, int) or 0 <= i - lag < NB:
                stage(i - lag, (w - lag) % 4)

    for i in range(first):
        turn(i, i % 4)
    with eng.Fori(first // 4, last // 4) as i:
        if step:
            step.enter(i - first // 4, step.per_loop)
        for w in range(4):
            turn(4 * i + w, w)
        if step:
            step.leave(last // 4 - first // 4)
    for i in range(last, NB + deepest):
        turn(i, i % 4)


def rows_of(b):
    return LAST_ROWS if isinstance(b, int) and b == NB - 1 else P


def group_turns(eng, turn):
    turn(0)
    with eng.Fori(1, G // V - 1) as i:
        turn(i)
    turn(G // V - 1)


def blocks_of(eng, packed, i):
    v = eng.value_load(packed[0:1, bass.ds(i, 1)], min_val=0, max_val=(P << (TURN - 1)) - 1)
    blocks = [eng.snap((v & (P - 1)).with_bounds(min_val=0, max_val=NB - 1))]
    for k in range(1, TURN):
        blocks.append(eng.snap((blocks[-1] + ((v >> (6 + k)) & 1)).with_bounds(min_val=0, max_val=NB - 1)))
    return blocks


def gnn_kernel(nc, x, src, dst, edge_type, query, wq, bq, wk, bk, wv, bv, rel_w, wo, bo, gamma, beta,
               w1, b1, w2, b2, wa1, ba1, wa2, ba2, out):
    with ExitStack() as ctx:
        def sb(name, shape, dt=fp32):
            return ctx.enter_context(nc.sbuf_tensor(name, shape, dt))

        def dram(name, shape, dt=fp32):
            return nc.dram_tensor(name, shape, dt, kind="Internal").ap()

        t = {}
        t["k_rows"] = dram("k_rows", (N, D))
        t["v_rows"] = dram("v_rows", (N, D))
        t["x1_rows"] = dram("x1_rows", (N, D))
        t["xj_rows"] = dram("xj_rows", (N, XW))
        t["sorted_keys"] = dram("sorted_keys", (1 << LOGN,), i32)

        t["node_tab"] = sb("node_tab", [P, NB * AW])
        t["ident"] = sb("ident", [P, P])
        t["ident_h"] = sb("ident_h", [P, P], bf16)
        t["iota"] = sb("iota", [P, P])
        t["ones"] = sb("ones", [P, P])
        for layer in range(2):
            t[f"other{layer}"] = sb(f"other{layer}", [P, S], i32)
            t[f"local{layer}"] = sb(f"local{layer}", [P, S])
            t[f"packed_late{layer}"] = sb(f"packed_late{layer}", [1, S // TURN + 1], i32)
            t[f"packed{layer}"] = sb(f"packed{layer}", [1, S // TURN], i32)
        t["rel"] = sb("rel", [P, S])
        t["score"] = sb("score", [P, S * H])
        t["a1_tab"] = sb("a1_tab", [P, NB])

        t["x"], t["src"], t["dst"], t["edge_type"], t["out"] = x, src, dst, edge_type, out
        project_and_sort(nc, t, query, wq, bq, wk, bk, wv, bv)
        build_steps(nc, t)
        edge_scores(nc, t, rel_w)
        softmax_numerators(nc, t)
        aggregate(nc, t)
        update_nodes(nc, t, query, wo, bo, gamma, beta, w1, b1, w2, b2, wa1, ba1, wa2, ba2)
        attend(nc, t)
        finish(nc, t)


def project_and_sort(nc, t, query, wq, bq, wk, bk, wv, bv):
    x, tab, ident, ones = t["x"], t["node_tab"], t["ident"], t["ones"]
    with ExitStack() as ctx:
        def sb(name, shape, dt=fp32):
            return ctx.enter_context(nc.sbuf_tensor(name, shape, dt))

        def sem(name):
            return ctx.enter_context(nc.semaphore(name))

        x_in = [sb(f"x_in{u}", [P, D]) for u in range(2)]
        enh = [sb(f"enh{u}", [P, 2, P]) for u in range(2)]
        kv_out = [sb(f"kv_out{u}", [P, 2 * D]) for u in range(2)]
        w_qkv = sb("w_qkv", [P, 2, 3 * D])
        b_qkv = sb("b_qkv", [1, 3 * D])
        q_col = sb("q_col", [P, 2])
        q01 = sb("q01", [P, 2])
        keys = [sb(f"keys{u}", [P, F], i32) for u in range(2)]
        sign = sb("sign", [P, 8])
        pbit = sb("pbit", [P, 8], i32)
        pid = sb("pid", [P, 1], i32)
        ps_xt = ctx.enter_context(nc.psum_tensor("ps_xt", [P, 2, P], fp32))
        ps4 = ctx.enter_context(nc.psum_tensor("ps4", [P, 4, 512], fp32))

        consts_set, weights_in, x_loaded = sem("consts_set"), sem("weights_in"), [sem("x_loaded0"), sem("x_loaded1")]
        xt_ready, enh_ready, mm_done = sem("xt_ready"), sem("enh_ready"), sem("mm_done")
        evacuated = sem("evacuated")
        kv_stored, q01_ready = [sem("kv_stored0"), sem("kv_stored1")], sem("q01_ready")
        pool_step, dve_step = sem("pool_step"), sem("dve_step")
        keys_in, pads_set = sem("keys_in"), sem("pads_set")
        to_flip, flipped, flip_copied, keys_out = sem("to_flip"), sem("flipped"), sem("flip_copied"), sem("keys_out")
        sorted_ready = sem("sorted_ready")
        full_p = E // F
        rest = E - full_p * F
        block = ctx.enter_context(nc.Block())

        @block.sync
        def _(sp):
            sp.wait_ge(pads_set, 1)
            for n, a in enumerate((t["src"], t["dst"])):
                sp.dma_start(keys[n][0:full_p, :], a[0:full_p * F].rearrange("(p f) -> p f", f=F)).then_inc(keys_in, 16)
                sp.dma_start(keys[n][full_p:full_p + 1, 0:rest],
                             a[full_p * F:E].rearrange("(p f) -> p f", p=1)).then_inc(keys_in, 16)
            for n, (w, b) in enumerate(((wq, bq), (wk, bk), (wv, bv))):
                sp.dma_start(w_qkv[:, :, n * D:(n + 1) * D], w.rearrange("(c p) n -> p c n", p=P)).then_inc(weights_in, 16)
                sp.dma_start(b_qkv[:, n * D:(n + 1) * D], b.rearrange("(a n) -> a n", a=1)).then_inc(weights_in, 16)
            with nc.allow_non_contiguous_dma(reason="256 numbers, once"):
                sp.dma_start(q_col[:, :], query.rearrange("(c p) -> p c", p=P)).then_inc(weights_in, 16)

            def load(b, u):
                r = rows_of(b)
                sp.dma_start(x_in[u][0:r, :], x[bass.ds(b * P, r), :]).then_inc(x_loaded[u], 16)

            load(0, 0)
            load(1, 1)

            def body(b, u):
                sp.wait_ge(xt_ready, b + 1)
                if not (isinstance(b, int) and b + 2 >= NB):
                    load(b + 2, u)

            with sp.Fori(0, NB // 2 - 2) as i:
                body(2 * i, 0)
                body(2 * i + 1, 1)
            body(NB - 4, 0)
            body(NB - 3, 1)
            sp.wait_ge(sorted_ready, 1)
            sp.dma_start(t["sorted_keys"].rearrange("(p f) -> p f", f=F), keys[0][:, :]).then_inc(keys_out, 16)
            sp.wait_ge(keys_out, 16)

        @block.gpsimd
        def _(pool):
            step = Serial(pool, pool_step)
            step(nc.gpsimd.memset(keys[0][96:P, :], PAD_NODE))
            nc.gpsimd.memset(keys[1][96:P, :], 0).then_inc(pads_set, 1)
            pool.wait_ge(pads_set, 1)
            for m, base in ((t["ident"], 0.0), (t["ident_h"], 0.0), (ones, 1.0)):
                step(nc.gpsimd.memset(m[:, :], base))
            for m in (t["ident"], t["ident_h"]):
                step(nc.gpsimd.affine_select(out=m[:, :], in_=m[:, :], compare_op=ALU.not_equal, fill=1.0,
                                             base=0, pattern=[[-1, P]], channel_multiplier=1))
            step(nc.gpsimd.iota(t["iota"][:, :], [[1, P]], base=0, channel_multiplier=0,
                                allow_small_or_imprecise_dtypes=True))
            step(nc.gpsimd.iota(pid[:, :], [[1, 1]], base=0, channel_multiplier=1))
            step(nc.gpsimd.memset(t["a1_tab"][:, :], 0.0))
            pool.sem_inc(consts_set, 1)
            def body(b, u):
                r = rows_of(b)
                pool.wait_ge(evacuated, b + 1)
                for k, rows in enumerate((t["k_rows"], t["v_rows"])):
                    pool.dma_start(rows[bass.ds(b * P, r), :], kv_out[u][0:r, k * D:(k + 1) * D])\
                        .then_inc(kv_stored[u], 16)

            block_pairs(pool, body)
            for u in range(2):
                pool.wait_ge(kv_stored[u], NB // 2 * 32)

        @block.scalar
        def _(act):
            act.wait_ge(weights_in, 7 * 16)
            nc.scalar.mul(q01[:, :], q_col[:, :], 0.1).then_inc(q01_ready, 1)
            act.wait_ge(q01_ready, 1)

            def enhance(b, u):
                act.wait_ge(xt_ready, b + 1)
                for c in range(2):
                    last = nc.scalar.activation(enh[u][:, c, :], ps_xt[:, c, :], ACT.Identity, bias=q01[:, c:c + 1])
                last.then_inc(enh_ready, 1)

            def evacuate(b, u):
                act.wait_ge(mm_done, b + 1)
                if not early(b):
                    act.wait_ge(kv_stored[u], (b - u) * 16)
                nc.scalar.activation(tab[:, bass.ds(b * AW, D)], ps4[:, 2 * u, 0:D], ACT.Copy, scale=float(DH) ** -0.5)
                nc.scalar.activation(kv_out[u][:, :], ps4[:, 2 * u + 1, :], ACT.Copy).then_inc(evacuated, 1)

            enhance(0, 0)

            def body(b, u):
                if not (isinstance(b, int) and b == NB - 1):
                    enhance(b + 1, 1 - u)
                evacuate(b, u)

            block_pairs(act, body)
            for r in range(2 * (LOGN - 11)):
                for bank in range(4):
                    act.wait_ge(flipped, 4 * r + bank + 1)
                    last = nc.scalar.activation(keys[0][:, bank * 512:(bank + 1) * 512].bitcast(fp32),
                                                ps4[:, bank, :], ACT.Copy)
                last.then_inc(flip_copied, 1)

        @block.tensor
        def _(pe):
            pe.wait_ge(consts_set, 1)
            pe.wait_ge(weights_in, 7 * 16)

            def transpose(b, u):
                pe.wait_ge(x_loaded[u], (b - u) * 8 + 16)
                for c in range(2):
                    last = nc.tensor.transpose(ps_xt[:, c, :], x_in[u][:, c * P:(c + 1) * P], ident[:, :])
                last.then_inc(xt_ready, 1)

            def body(b, u):
                pe.wait_ge(enh_ready, b + 1)
                if not (isinstance(b, int) and b == NB - 1):
                    transpose(b + 1, 1 - u)
                if not early(b):
                    pe.wait_ge(evacuated, b - 1)
                for o, (lo, hi) in ((2 * u, (0, D)), (2 * u + 1, (D, 3 * D))):
                    for c in range(2):
                        nc.tensor.matmul(ps4[:, o, 0:hi - lo], enh[u][:, c, :], w_qkv[:, c, lo:hi], start=(c == 0), stop=False)
                    last = nc.tensor.matmul(ps4[:, o, 0:hi - lo], ones[0:1, :], b_qkv[:, lo:hi], start=False, stop=True)
                last.then_inc(mm_done, 1)

            transpose(0, 0)
            block_pairs(pe, body)
            for r in range(2 * (LOGN - 11)):
                pe.wait_ge(to_flip, r + 1)
                if r == 0:
                    pe.wait_ge(evacuated, NB)
                for bank in range(4):
                    for c in range(4):
                        col = bank * 4 + c
                        last = nc.tensor.transpose(ps4[:, bank, c * P:(c + 1) * P],
                                                   keys[0][:, col * P:(col + 1) * P].bitcast(fp32), ident[:, :])
                    last.then_inc(flipped, 1)

        @block.vector
        def _(dve):
            step = Serial(dve, dve_step)
            pair = [keys[0][:, :].bitcast(fp32), keys[1][:, :].bitcast(fp32)]
            dve.wait_ge(keys_in, 64)
            dve.wait_ge(consts_set, 1)
            step(dve.tensor_scalar(keys[0][:, :], keys[0][:, :], NODE_BITS, KEY_BIAS,
                                   ALU.logical_shift_left, ALU.bitwise_or))
            step(dve.tensor_tensor(keys[0][:, :], keys[0][:, :], keys[1][:, :], ALU.bitwise_or))
            for m in range(7):
                step(dve.tensor_scalar(pbit[:, m:m + 1], pid[:, :], m, 1, ALU.logical_shift_right, ALU.bitwise_and))
            step(dve.tensor_scalar(sign[:, 0:7], pbit[:, 0:7], -2.0, 1.0, ALU.mult, ALU.add))
            step(dve.memset(sign[:, 7:8], 1.0))
            now = 0

            def exchange(distance, now):
                a, b = (z.rearrange("p (n two d) -> p n two d", two=2, d=distance) for z in (pair[now], pair[1 - now]))
                dve.tensor_tensor(b[:, :, 0, :], a[:, :, 0, :], a[:, :, 1, :], ALU.min)
                step(dve.tensor_tensor(b[:, :, 1, :], a[:, :, 0, :], a[:, :, 1, :], ALU.max))
                return 1 - now

            rounds = 0
            for k in range(1, LOGN + 1):
                z = pair[now]
                if k == 1:
                    v = z.rearrange("p (n s w) -> p n s w", s=2, w=2)[:, :, 1, :]
                    step(dve.tensor_scalar(v, v, -1.0, None, ALU.mult))
                elif k < 11:
                    v = z.rearrange("p (n s w) -> p n s w", s=4, w=1 << (k - 1))[:, :, 1:3, :]
                    step(dve.tensor_scalar(v, v, -1.0, None, ALU.mult))
                else:
                    if k == 11:
                        v = z[:, F // 2:F]
                        step(dve.tensor_scalar(v, v, -1.0, None, ALU.mult))
                    else:
                        step(dve.tensor_scalar(z, z, sign[:, k - 12:k - 11], None, ALU.mult))
                    if k < LOGN:
                        step(dve.tensor_scalar(z, z, sign[:, k - 11:k - 10], None, ALU.mult))
                if k > 11:
                    for back in range(2):
                        if now == 1:
                            step(dve.tensor_copy(pair[0], pair[1]))
                            now = 0
                        dve.sem_inc(to_flip, 1)
                        rounds += 1
                        dve.wait_ge(flip_copied, rounds)
                        if back == 0:
                            for j in range(k - 12, -1, -1):
                                now = exchange(1 << j, now)
                for j in range(min(k, 11) - 1, -1, -1):
                    now = exchange(1 << j, now)
            if now == 1:
                step(dve.tensor_copy(keys[0][:, :], keys[1][:, :]))
            dve.sem_inc(sorted_ready, 1)


def build_steps(nc, t):
    with ExitStack() as ctx:
        def sb(name, shape, dt=fp32):
            return ctx.enter_context(nc.sbuf_tensor(name, shape, dt))

        def sem(name):
            return ctx.enter_context(nc.semaphore(name))

        names = (("dst", "src", "edge_type"), ("key",))
        raw = {n: t["score"][:, k * S:(k + 1) * S].bitcast(i32).rearrange("q (c e) -> q c e", e=P)
               for k, n in enumerate(names[0] + names[1])}
        node = [raw["dst"], sb("sorted_src", [P, C, P], i32)]
        far = [raw["src"], raw["key"]]
        arrays = [[node[0], far[0], raw["edge_type"]], [node[1], far[1]]]
        last_block = sb("last_block", [P, C], i32)
        tile_end = sb("tile_end", [P, C])
        tile_id = sb("tile_id", [P, C])
        step_id = sb("step_id", [P, S])
        tile_row = sb("tile_row", [P, S])
        block_row = sb("block_row", [P, S])
        before = sb("before", [P, 2, P])
        hit = sb("hit", [P, 2, P])
        coef = sb("coef", [1, TURN])
        late = sb("late", [1, S + TURN])
        mixed = sb("mixed", [1, S + TURN])
        packed = block_row[0:1, 0:S // TURN + 1]
        ps_tile = ctx.enter_context(nc.psum_tensor("ps_tile", [P, P], fp32))
        ps_val = ctx.enter_context(nc.psum_tensor("ps_val", [P, 3, 512], fp32))
        pads_set, edges_in, pool_step, dve_step = sem("tile_pads"), sem("edges_in"), sem("pool_step2"), sem("dve_step2")
        ids_set, before_ready, tile_ready = sem("ids_set"), sem("before_ready"), sem("tile_ready")
        hit_ready, val_ready = sem("hit_ready"), sem("val_ready")
        full_c = T // P
        full_q = E // P - full_c * P
        rest = E - (full_c * P + full_q) * P
        block = ctx.enter_context(nc.Block())

        @block.sync
        def _(sp):
            sp.wait_ge(pads_set, 1)
            for n in names[0]:
                a = t[n]
                sp.dma_start(raw[n][:, 0:full_c, :], a[0:full_c * P * P].rearrange("(c q e) -> q c e", q=P, e=P)).then_inc(edges_in, 16)
                sp.dma_start(raw[n][0:full_q, full_c, :],
                             a[full_c * P * P:(full_c * P + full_q) * P].rearrange("(q e) -> q e", e=P)).then_inc(edges_in, 16)
                sp.dma_start(raw[n][full_q:full_q + 1, full_c, 0:rest],
                             a[E - rest:E].rearrange("(q e) -> q e", q=1)).then_inc(edges_in, 16)
            sp.dma_start(raw["key"][:, :, :], t["sorted_keys"][0:C * P * P].rearrange("(c q e) -> q c e", q=P, e=P))\
                .then_inc(edges_in, 16)

        @block.gpsimd
        def _(pool):
            step = Serial(pool, pool_step)
            for n, pad in zip(names[0], (PAD_NODE, 0, 0)):
                step(nc.gpsimd.memset(raw[n][:, full_c:C, :], pad))
            pool.sem_inc(pads_set, 1)
            step(nc.gpsimd.iota(step_id[:, :], [[1, S]], base=0, channel_multiplier=0,
                                allow_small_or_imprecise_dtypes=True))
            step(nc.gpsimd.iota(tile_id[:, :], [[P, C]], base=0, channel_multiplier=1,
                                allow_small_or_imprecise_dtypes=True))
            for k in range(TURN):
                step(nc.gpsimd.memset(coef[:, k:k + 1], float(P << (k - 1)) if k else 1.0))
            pool.sem_inc(ids_set, 1)

        @block.vector
        def _(dve):
            step = Serial(dve, dve_step)
            dve.wait_ge(ids_set, 1)
            dve.wait_ge(edges_in, (3 * 3 + 1) * 16)
            step(dve.tensor_scalar(node[1][:, :, :], raw["key"][:, :, :], NODE_BITS, NODE_MASK,
                                   ALU.logical_shift_right, ALU.bitwise_and))
            step(dve.tensor_scalar(raw["key"][:, :, :], raw["key"][:, :, :], NODE_MASK, None, ALU.bitwise_and))
            seen = 0
            for layer in range(2):
                step(dve.tensor_scalar(last_block[:, :], node[layer][:, :, P - 1], 7, None, ALU.logical_shift_right))
                step(dve.tensor_tensor(tile_end[:, :], last_block[:, :], tile_id[:, :], ALU.add))
                for a in arrays[layer]:
                    step(dve.tensor_copy(a[:, :, :].bitcast(fp32), a[:, :, :]))
                for c in range(C):
                    cols = slice(c * P, (c + 1) * P)
                    near = [c - 1, c] if c else [c]
                    for k, a in enumerate(near):
                        step(dve.tensor_scalar(before[:, k, :], step_id[:, cols], tile_end[:, a:a + 1], None, ALU.is_gt))
                    dve.sem_inc(before_ready, 1)
                    dve.wait_ge(tile_ready, layer * C + c + 1)
                    step(dve.tensor_scalar(tile_row[:, cols], ps_tile[:, :], float(near[0] * P), None, ALU.add))
                    for k, a in enumerate(near):
                        step(dve.tensor_scalar(hit[:, k, :], tile_row[:, cols], tile_id[:, a:a + 1], None, ALU.is_equal))
                    dve.sem_inc(hit_ready, 1)
                    step(dve.tensor_tensor(block_row[:, cols], step_id[:, cols], tile_row[:, cols], ALU.subtract))
                    dve.wait_ge(val_ready, layer * C + c + 1)
                    step(dve.scalar_tensor_tensor(t[f"local{layer}"][:, cols], block_row[:, cols], -float(P),
                                                  ps_val[:, 0, 0:P], ALU.mult, ALU.add))
                    step(dve.tensor_copy(t[f"other{layer}"][:, cols], ps_val[:, 1, 0:P]))
                    if layer == 0:
                        step(dve.tensor_copy(t["rel"][:, cols], ps_val[:, 2, 0:P]))
                step(dve.memset(late[:, 0:LAG * U], 0.0))
                step(dve.tensor_copy(late[:, LAG * U:LAG * U + S], block_row[0:1, :]))
                step(dve.tensor_scalar(late[:, LAG * U + S:S + TURN], late[:, 0:TURN - LAG * U], 0.0, float(NB - 1), ALU.mult, ALU.add))
                for blocks, into, turns in ((block_row, "packed", S // TURN), (late, "packed_late", S // TURN + 1)):
                    by_turn, m = (z[0:1, 0:turns * TURN].rearrange("p (g k) -> p g k", k=TURN) for z in (blocks, mixed))
                    step(dve.tensor_tensor(m[:, :, 1:TURN], by_turn[:, :, 1:TURN], by_turn[:, :, 0:TURN - 1], ALU.subtract))
                    step(dve.tensor_copy(m[:, :, 0], by_turn[:, :, 0]))
                    step(dve.tensor_tensor(m, m, coef[:, :].unsqueeze(1).broadcast_to([1, turns, TURN]), ALU.mult))
                    step(dve.tensor_reduce(packed[:, 0:turns], m, AX.X, ALU.add))
                    step(dve.tensor_copy(t[f"{into}{layer}"][:, 0:turns], packed[:, 0:turns]))

        @block.tensor
        def _(pe):
            for layer in range(2):
                for c in range(C):
                    near = [c - 1, c] if c else [c]
                    pe.wait_ge(before_ready, layer * C + c + 1)
                    for k in range(len(near)):
                        last = nc.tensor.matmul(ps_tile[:, :], t["ones"][:, :], before[:, k, :],
                                                start=(k == 0), stop=(k == len(near) - 1))
                    last.then_inc(tile_ready, 1)
                    pe.wait_ge(hit_ready, layer * C + c + 1)
                    for v, vals in enumerate(arrays[layer]):
                        for k, a in enumerate(near):
                            last = nc.tensor.matmul(ps_val[:, v, 0:P], vals[:, a, :].bitcast(fp32), hit[:, k, :],
                                                    start=(k == 0), stop=(k == len(near) - 1))
                    last.then_inc(val_ready, 1)


def edge_scores(nc, t, rel_w):
    with ExitStack() as ctx:
        def sb(name, shape, dt=fp32):
            return ctx.enter_context(nc.sbuf_tensor(name, shape, dt))

        def pb(name, shape, dt=fp32):
            return ctx.enter_context(nc.psum_tensor(name, shape, dt))

        def sem(name):
            return ctx.enter_context(nc.semaphore(name))

        rel_in = sb("rel_in", [R, DH])
        rel_02 = sb("rel_02", [R, DH])
        index = [sb(f"s_index{u}", [P, U], i32) for u in range(V)]
        rows = [sb(f"s_rows{u}", [P, U, D]) for u in range(V)]
        prod = sb("prod", [P, U, D])
        hot_node = [sb(f"hot_node{u}", [P, U, P], bf16) for u in range(2)]
        hot_rel = [sb(f"hot_rel{u}", [P, U, R], bf16) for u in range(2)]
        node_hot = [sb(f"node_hot{u}", [P, U, P]) for u in range(2)]
        rel_hot = [sb(f"rel_hot{u}", [R, U, P]) for u in range(2)]
        ps_node = pb("ps_node", [P, U, P], bf16)
        ps_relh = pb("ps_relh", [P, U, P], bf16)
        ps_q = [pb(f"ps_q{u}", [P, U, D]) for u in range(2)]
        ps_rel = [pb(f"ps_rel{u}", [P, U, DH]) for u in range(2)]
        weights_in, rel_ready = sem("rel_in_sem"), sem("rel_ready")
        index_ready, rows_in, rows_used = sem("s_index_ready"), [sem(f"s_rows_in{u}") for u in range(V)], sem("s_rows_used")
        hot_ready, turned, turned_copied = sem("s_hot_ready"), sem("s_turned"), sem("s_turned_copied")
        picked, picked_used, scored = sem("s_picked"), sem("s_picked_used"), sem("s_scored")
        pool_turn = sem("s_pool_turn")
        block = ctx.enter_context(nc.Block())

        @block.sync
        def _(sp):
            sp.dma_start(rel_in[:, :], rel_w).then_inc(weights_in, 16)

        @block.gpsimd
        def _(pool):
            def turn(i):
                for u in range(V):
                    g = V * i + u
                    pool.wait_ge(index_ready, g + 1)
                    if not early(i, 1):
                        pool.wait_ge(rows_used, g - V + 1)
                    pool.sem_inc(pool_turn, 1)
                    for k in range(U):
                        pool.indirect_dma_start(out=rows[u][:, k, :], out_offset=None, in_=t["k_rows"],
                                                in_offset=bass.IndirectOffsetOnAxis(ap=index[u][:, k:k + 1], axis=0))\
                            .then_inc(rows_in[u], 16)

            group_turns(pool, turn)

        @block.scalar
        def _(act):
            act.wait_ge(weights_in, 16)
            nc.scalar.mul(rel_02[:, :], rel_in[:, :], 0.2).then_inc(rel_ready, 1)

            def turn(i):
                for u in range(V):
                    g = V * i + u
                    if not early(i, 1):
                        act.wait_ge(rows_in[u], 16 * U * i)
                    nc.scalar.copy(index[u][:, :], t["other0"][:, bass.ds(g * U, U)]).then_inc(index_ready, 1)
                    act.wait_ge(turned, g + 1)
                    if not early(g):
                        act.wait_ge(picked, g - 1)
                    nc.scalar.copy(node_hot[u % 2][:, :, :], ps_node[:, :, :])
                    nc.scalar.copy(rel_hot[u % 2][:, :, :], ps_relh[0:R, :, :]).then_inc(turned_copied, 1)

            group_turns(act, turn)

        @block.vector
        def _(dve):
            def hot(g, u):
                if not early(g):
                    dve.wait_ge(turned, g - 1)
                local = t["local0"][:, bass.ds(g * U, U)].unsqueeze(2).broadcast_to([P, U, P])
                rel = t["rel"][:, bass.ds(g * U, U)].unsqueeze(2).broadcast_to([P, U, R])
                dve.tensor_tensor(hot_node[u % 2][:, :, :], t["iota"][:, :].unsqueeze(1).broadcast_to([P, U, P]), local, ALU.is_equal)
                dve.tensor_tensor(hot_rel[u % 2][:, :, :], t["iota"][:, 0:R].unsqueeze(1).broadcast_to([P, U, R]), rel, ALU.is_equal)\
                    .then_inc(hot_ready, 1)

            def work(g, u, i):
                by_head = rows[u][:, :, :].rearrange("p k (h d) -> p k h d", h=H)
                dve.wait_ge(picked, g + 1)
                dve.wait_ge(rows_in[u], 16 * U * (i + 1))
                if not (isinstance(g, int) and g == 0):
                    dve.wait_ge(scored, g)
                dve.tensor_tensor(prod[:, :, :].rearrange("p k (h d) -> p k h d", h=H), by_head,
                                  ps_rel[u % 2][:, :, :].unsqueeze(2).broadcast_to([P, U, H, DH]), ALU.add).then_inc(rows_used, 1)
                dve.wait_ge(rows_used, g + 1)
                dve.tensor_tensor(prod[:, :, :], prod[:, :, :], ps_q[u % 2][:, :, :], ALU.mult).then_inc(picked_used, 1)
                dve.wait_ge(picked_used, g + 1)
                dve.tensor_reduce(t["score"][:, bass.ds(g * U * H, U * H)],
                                  prod[:, :, :].rearrange("p k (h d) -> p (k h) d", h=H), AX.X, ALU.add).then_inc(scored, 1)

            def turn(i):
                for u in range(V):
                    g = V * i + u
                    if not (isinstance(g, int) and g + 2 >= G):
                        hot(g + 2, u % 2)
                    work(g, u, i)

            hot(0, 0)
            hot(1, 1)
            group_turns(dve, turn)
            dve.wait_ge(scored, G)

        @block.tensor
        def _(pe):
            def turn_hot(g, u):
                pe.wait_ge(hot_ready, g + 1)
                if not (isinstance(g, int) and g == 0):
                    pe.wait_ge(turned_copied, g)
                for k in range(U):
                    nc.tensor.transpose(ps_node[:, k, :], hot_node[u % 2][:, k, :], t["ident_h"][:, :])
                for k in range(U):
                    last = nc.tensor.transpose(ps_relh[0:R, k, :], hot_rel[u % 2][:, k, :], t["ident_h"][:, :])
                last.then_inc(turned, 1)

            def turn(i):
                blocks = blocks_of(pe, t["packed0"], i)
                for u in range(V):
                    g = V * i + u
                    if not (isinstance(g, int) and g == G - 1):
                        turn_hot(g + 1, (u + 1) % 2)
                    pe.wait_ge(turned_copied, g + 1)
                    if not early(g):
                        pe.wait_ge(picked_used, g - 1)
                    for k in range(U):
                        nc.tensor.matmul(ps_rel[u % 2][:, k, :], rel_hot[u % 2][:, k, :], rel_02[:, :], start=True, stop=True)
                    for k in range(U):
                        last = nc.tensor.matmul(ps_q[u % 2][:, k, :], node_hot[u % 2][:, k, :],
                                                t["node_tab"][:, bass.ds(blocks[u * U + k] * AW, D)], start=True, stop=True)
                    last.then_inc(picked, 1)

            pe.wait_ge(rel_ready, 1)
            turn_hot(0, 0)
            group_turns(pe, turn)


def softmax_numerators(nc, t):
    with ExitStack() as ctx:
        def sb(name, shape, dt=fp32):
            return ctx.enter_context(nc.sbuf_tensor(name, shape, dt))

        def sem(name):
            return ctx.enter_context(nc.semaphore(name))

        W = S * H
        tab = t["node_tab"]
        y, fwd, bwd = tab[:, 0:W], tab[:, W:2 * W], tab[:, 2 * W:3 * W]
        loc, valid, pen = (tab[:, 3 * W + k * S:3 * W + (k + 1) * S] for k in range(3))
        score = t["score"]

        def by_edge(v):
            return v.rearrange("q (c e) -> q c e", e=P)

        def by_head(v):
            return v.rearrange("q (c h e) -> q c h e", h=H, e=P)

        def all_heads(v):
            return by_edge(v).unsqueeze(2).broadcast_to([P, C, H, P])

        restart = sb("restart", [P, W + 1])
        ends = sb("ends", [P, 4, C, H])
        rows = [score[0:H, k * S:(k + 1) * S] for k in range(4)]
        cont = sb("cont", [H, S + 1])
        reach = t["rel"][0:H, :]
        carry = [restart[0:H, k * S:(k + 1) * S] for k in range(2)]
        carry_in = sb("carry_in", [P, 2, C, H])
        ps_y = [ctx.enter_context(nc.psum_tensor(f"ps_y{u}", [P, H, P], fp32)) for u in range(2)]
        ps_rows = ctx.enter_context(nc.psum_tensor("ps_rows", [P, 4 * 512], fp32))
        ps_carry = ctx.enter_context(nc.psum_tensor("ps_carry", [P, 2, C, H], fp32))
        y_turned, y_copied, loc_turned, loc_copied = sem("y_turned"), sem("y_copied"), sem("loc_turned"), sem("loc_copied")
        ends_ready, ends_turned, ends_copied = sem("ends_ready"), sem("ends_turned"), sem("ends_copied")
        carry_ready, carry_turned = sem("carry_ready"), sem("carry_turned")
        less_max, exp_done, w_turned, w_copied = sem("less_max"), sem("exp_done"), sem("w_turned"), sem("w_copied")
        dve_step = sem("dve_step4")
        block = ctx.enter_context(nc.Block())

        @block.tensor
        def _(pe):
            ident = t["ident"]
            for c in range(C):
                last = nc.tensor.transpose(ps_rows[:, c * P:(c + 1) * P], t["local0"][:, c * P:(c + 1) * P], ident[:, :])
            last.then_inc(loc_turned, 1)
            for c in range(C):
                if c >= 2:
                    pe.wait_ge(y_copied, c - 1)
                s = score[:, c * P * H:(c + 1) * P * H].rearrange("p (s h) -> p h s", h=H)
                for h in range(H):
                    last = nc.tensor.transpose(ps_y[c % 2][:, h, :], s[:, h, :], ident[:, :])
                last.then_inc(y_turned, 1)
            pe.wait_ge(ends_ready, 1)
            pe.wait_ge(loc_copied, 1)
            for k in range(4):
                if k:
                    pe.wait_ge(ends_copied, k)
                for c in range(C):
                    last = nc.tensor.transpose(ps_rows[0:H, c * P:(c + 1) * P], ends[:, k, c, :], ident[:, :])
                last.then_inc(ends_turned, 1)
            pe.wait_ge(carry_ready, 1)
            for k in range(2):
                for c in range(C):
                    last = nc.tensor.transpose(ps_carry[:, k, c, :], carry[k][:, c * P:(c + 1) * P], ident[0:H, 0:H])
            last.then_inc(carry_turned, 1)
            pe.wait_ge(exp_done, 1)
            for c in range(C):
                if c >= 2:
                    pe.wait_ge(w_copied, c - 1)
                for h in range(H):
                    last = nc.tensor.transpose(ps_y[c % 2][:, h, :], by_head(y)[:, c, h, :], ident[:, :])
                last.then_inc(w_turned, 1)

        @block.scalar
        def _(act):
            act.wait_ge(loc_turned, 1)
            nc.scalar.copy(loc, ps_rows[:, 0:S]).then_inc(loc_copied, 1)
            for c in range(C):
                act.wait_ge(y_turned, c + 1)
                nc.scalar.copy(by_head(y)[:, c, :, :], ps_y[c % 2][:, :, :]).then_inc(y_copied, 1)
            for k in range(4):
                act.wait_ge(ends_turned, k + 1)
                nc.scalar.copy(rows[k], ps_rows[0:H, 0:S]).then_inc(ends_copied, 1)
            act.wait_ge(less_max, 1)
            nc.scalar.activation(y, y, ACT.Exp).then_inc(exp_done, 1)
            for c in range(C):
                act.wait_ge(w_turned, c + 1)
                nc.scalar.copy(score[:, c * P * H:(c + 1) * P * H].rearrange("p (s h) -> p h s", h=H), ps_y[c % 2][:, :, :])\
                    .then_inc(w_copied, 1)
            act.wait_ge(w_copied, C)

        @block.vector
        def _(dve):
            step = Serial(dve, dve_step)
            dve.wait_ge(loc_copied, 1)
            step(dve.tensor_scalar(valid, loc, 0.0, None, ALU.is_ge))
            step(dve.scalar_tensor_tensor(valid, loc, float(P - 1), valid, ALU.is_le, ALU.mult))
            step(dve.tensor_scalar(pen, valid, 1.0, -LOWEST, ALU.subtract, ALU.mult))
            dve.wait_ge(y_copied, C)
            step(dve.tensor_tensor(by_head(y), by_head(y), all_heads(pen), ALU.add))
            step(dve.memset(restart[:, :], LOWEST))
            other = by_edge(loc)
            step(dve.tensor_tensor(by_edge(pen)[:, :, 1:P], other[:, :, 1:P], other[:, :, 0:P - 1], ALU.not_equal))
            step(dve.tensor_scalar(by_head(restart[:, 0:W])[:, :, :, 1:P],
                                   by_edge(pen)[:, :, 1:P].unsqueeze(2).broadcast_to([P, C, H, P - 1]), LOWEST, None, ALU.mult))
            step(dve.tensor_tensor_scan(fwd, restart[:, 0:W], y, LOWEST, ALU.add, ALU.max))
            step(dve.tensor_tensor_scan(bwd[:, ::-1], restart[:, W:0:-1], y[:, ::-1], LOWEST, ALU.add, ALU.max))
            step(dve.tensor_copy(ends[:, 0, :, :], by_head(fwd)[:, :, :, P - 1]))
            step(dve.tensor_copy(ends[:, 1, :, :], by_head(bwd)[:, :, :, 0]))
            for k, edge, none in ((2, P - 1, 2.0), (3, 0, 1.0)):
                shape = [P, C, H]
                at = by_edge(loc)[:, :, edge:edge + 1].broadcast_to(shape)
                step(dve.tensor_scalar(ends[:, k, :, :], at, none, None, ALU.add))
                step(dve.tensor_tensor(ends[:, k, :, :], ends[:, k, :, :], by_edge(valid)[:, :, edge:edge + 1].broadcast_to(shape), ALU.mult))
                step(dve.tensor_scalar(ends[:, k, :, :], ends[:, k, :, :], none, None, ALU.subtract))
            dve.sem_inc(ends_ready, 1)
            dve.wait_ge(ends_copied, 4)
            leave_end, leave_start, last_node, first_node = rows
            step(dve.memset(cont[:, :], 0.0))
            step(dve.tensor_tensor(cont[:, 1:S], first_node[:, 1:S], last_node[:, 0:S - 1], ALU.is_equal))
            step(dve.tensor_tensor(first_node[:, :], first_node[:, :], last_node[:, :], ALU.is_equal))
            for k, shift in ((0, 0), (1, 1)):
                step(dve.tensor_tensor(reach[:, :], first_node[:, :], cont[:, shift:shift + S], ALU.mult))
                step(dve.tensor_scalar(reach[:, :], reach[:, :], 1.0, -LOWEST, ALU.subtract, ALU.mult))
                if k == 0:
                    step(dve.tensor_tensor_scan(leave_end[:, :], reach[:, :], leave_end[:, :], LOWEST, ALU.add, ALU.max))
                else:
                    step(dve.tensor_tensor_scan(leave_start[:, ::-1], reach[:, ::-1], leave_start[:, ::-1], LOWEST, ALU.add, ALU.max))
            step(dve.tensor_scalar(cont[:, :], cont[:, :], 1.0, -LOWEST, ALU.subtract, ALU.mult))
            step(dve.memset(carry[0][:, 0:1], LOWEST))
            step(dve.memset(carry[1][:, S - 1:S], LOWEST))
            step(dve.tensor_tensor(carry[0][:, 1:S], leave_end[:, 0:S - 1], cont[:, 1:S], ALU.add))
            step(dve.tensor_tensor(carry[1][:, 0:S - 1], leave_start[:, 1:S], cont[:, 1:S], ALU.add))
            dve.sem_inc(carry_ready, 1)
            step(dve.tensor_tensor(fwd, fwd, bwd, ALU.max))
            dve.wait_ge(carry_turned, 1)
            step(dve.tensor_copy(carry_in[:, :, :, :], ps_carry[:, :, :, :]))
            for k, edge in ((0, 0), (1, P - 1)):
                step(dve.tensor_tensor(by_edge(pen), by_edge(loc), by_edge(loc)[:, :, edge:edge + 1].broadcast_to([P, C, P]), ALU.is_equal))
                step(dve.tensor_scalar(pen, pen, 1.0, -LOWEST, ALU.subtract, ALU.mult))
                step(dve.tensor_tensor(by_head(bwd), all_heads(pen), carry_in[:, k, :, :].unsqueeze(3).broadcast_to([P, C, H, P]), ALU.add))
                step(dve.tensor_tensor(fwd, fwd, bwd, ALU.max))
            step(dve.tensor_tensor(y, y, fwd, ALU.subtract))
            dve.sem_inc(less_max, 1)


def aggregate(nc, t):
    with ExitStack() as ctx:
        def sb(name, shape, dt=fp32):
            return ctx.enter_context(nc.sbuf_tensor(name, shape, dt))

        def sem(name):
            return ctx.enter_context(nc.semaphore(name))

        tab = t["node_tab"]
        index = [sb(f"a_index{u}", [P, U], i32) for u in range(V)]
        rows = [sb(f"a_rows{u}", [P, U, D]) for u in range(V)]
        hot = [sb(f"a_hot{u}", [P, U, P]) for u in range(2)]
        terms = [sb(f"a_terms{u}", [P, U, AW]) for u in range(2)]
        ps_sum = [ctx.enter_context(nc.psum_tensor(f"ps_sum{u}", [P, U, 512], fp32)) for u in range(2)]
        index_ready, rows_in, rows_used = sem("a_index_ready"), [sem(f"a_rows_in{u}") for u in range(V)], sem("a_rows_used")
        hot_ready, weights_ready, summed, added = sem("a_hot_ready"), sem("a_weights_ready"), sem("a_summed"), sem("a_added")
        pool_turn, cleared = sem("a_pool_turn"), sem("a_cleared")
        block = ctx.enter_context(nc.Block())

        @block.gpsimd
        def _(pool):
            def turn(i):
                for u in range(V):
                    g = V * i + u
                    pool.wait_ge(index_ready, g + 1)
                    if not early(i, 1):
                        pool.wait_ge(rows_used, g - V + 1)
                    pool.sem_inc(pool_turn, 1)
                    for k in range(U):
                        pool.indirect_dma_start(out=rows[u][:, k, :], out_offset=None, in_=t["v_rows"],
                                                in_offset=bass.IndirectOffsetOnAxis(ap=index[u][:, k:k + 1], axis=0))\
                            .then_inc(rows_in[u], 16)

            group_turns(pool, turn)

        @block.scalar
        def _(act):
            def turn(i):
                for u in range(V):
                    g = V * i + u
                    if not early(i, 1):
                        act.wait_ge(rows_in[u], 16 * U * i)
                    nc.scalar.copy(index[u][:, :], t["other0"][:, bass.ds(g * U, U)]).then_inc(index_ready, 1)
                    if not early(g):
                        act.wait_ge(summed, g - 1)
                    nc.scalar.copy(terms[u % 2][:, :, D:AW],
                                   t["score"][:, bass.ds(g * U * H, U * H)].rearrange("p (k h) -> p k h", h=H))\
                        .then_inc(weights_ready, 1)

            group_turns(act, turn)

        @block.vector
        def _(dve):
            def weigh(g, u, i):
                if not early(g):
                    dve.wait_ge(summed, g - 1)
                local = t["local0"][:, bass.ds(g * U, U)].unsqueeze(2).broadcast_to([P, U, P])
                dve.tensor_tensor(hot[u % 2][:, :, :], t["iota"][:, :].unsqueeze(1).broadcast_to([P, U, P]), local, ALU.is_equal)\
                    .then_inc(hot_ready, 1)
                dve.wait_ge(rows_in[u], 16 * U * (i + 1))
                weight = t["score"][:, bass.ds(g * U * H, U * H)].rearrange("p (k h) -> p k h", h=H)
                dve.tensor_tensor(terms[u % 2][:, :, 0:D].rearrange("p k (h d) -> p k h d", h=H),
                                  rows[u][:, :, :].rearrange("p k (h d) -> p k h d", h=H),
                                  weight.unsqueeze(3).broadcast_to([P, U, H, DH]), ALU.mult).then_inc(rows_used, 1)

            def add(g, u, blocks):
                dve.wait_ge(summed, g + 1)
                for k in range(U):
                    acc = tab[:, bass.ds(blocks[k] * AW, AW)]
                    if not (isinstance(g, int) and g == 0 and k == 0):
                        dve.wait_ge(added, g * U + k)
                    dve.tensor_tensor(acc, acc, ps_sum[u % 2][:, k, 0:AW], ALU.add).then_inc(added, 1)

            def turn(i):
                blocks = blocks_of(dve, t["packed_late0"], i)
                for u in range(V):
                    g = V * i + u
                    if not early(g, LAG):
                        add(g - LAG, u - LAG, blocks[u * U:])
                    weigh(g, u, i)

            dve.memset(tab[:, :], 0.0).then_inc(cleared, 1)
            dve.wait_ge(cleared, 1)
            group_turns(dve, turn)
            blocks = blocks_of(dve, t["packed_late0"], G // V)
            for k in range(LAG):
                add(G - LAG + k, k, blocks[k * U:])
            dve.wait_ge(added, G * U)

        @block.tensor
        def _(pe):
            def turn(i):
                for u in range(V):
                    g = V * i + u
                    pe.wait_ge(hot_ready, g + 1)
                    pe.wait_ge(weights_ready, g + 1)
                    pe.wait_ge(rows_used, g + 1)
                    if not early(g):
                        pe.wait_ge(added, (g - 1) * U)
                    for k in range(U):
                        last = nc.tensor.matmul(ps_sum[u % 2][:, k, 0:AW], hot[u % 2][:, k, :], terms[u % 2][:, k, :],
                                                start=True, stop=True)
                    last.then_inc(summed, 1)

            group_turns(pe, turn)


def update_nodes(nc, t, query, wo, bo, gamma, beta, w1, b1, w2, b2, wa1, ba1, wa2, ba2):
    with ExitStack() as ctx:
        def sb(name, shape, dt=fp32):
            return ctx.enter_context(nc.sbuf_tensor(name, shape, dt))

        def ring(name, shape):
            return [sb(f"{name}{u}", shape) for u in range(4)]

        def pb(name, shape):
            return ctx.enter_context(nc.psum_tensor(name, shape, fp32))

        def sem(name):
            return ctx.enter_context(nc.semaphore(name))

        tab, ident, ones = t["node_tab"], t["ident"], t["ones"]
        w_o, w_12, b_row = sb("w_o", [P, 2, D]), sb("w_12", [P, 2, 2 * D]), sb("b_row", [1, 3 * D])
        wide = {n: sb(f"wide_{n}", [P, D]) for n in ("gamma", "beta", "wa1", "wa2")}
        ba = sb("ba", [P, 2])
        x_in, v_in, xj = ring("n_x", [P, D]), ring("n_v", [P, D]), ring("n_xj", [P, XW])
        msg, y, z, x1 = ([t["score"][:, (4 * k + u) * D:(4 * k + u + 1) * D] for u in range(4)] for k in range(4))
        msg_t, x1_t = ring("n_msg_t", [P, 2, P]), ring("n_x1_t", [P, 2, P])
        h02, small = ring("n_h02", [P, 2 * D]), ring("n_small", [P, 48])
        junk = sb("junk", [P, D])
        ps_t = [pb(f"ps_t{k}", [P, 2, P]) for k in range(2)]
        ps_o = [pb(f"ps_o{k}", [P, D]) for k in range(2)]
        ps_h = [pb(f"ps_h{k}", [P, 2 * D]) for k in range(2)]
        weights_in, loaded = sem("n_weights_in"), [sem(f"n_loaded{u}") for u in range(4)]
        msg_ready, msg_turned, msg_t_ready, o_ready = sem("msg_ready"), sem("msg_turned"), sem("msg_t_ready"), sem("o_ready")
        var_ready, std_ready, scale_ready, normed = ([sem(f"{n}{k}") for k in range(2)] for n in ("var_ready", "std_ready", "scale_ready", "normed"))
        z_ready, x1_turned, x1_t_ready, h_ready = sem("z_ready"), sem("x1_turned"), sem("x1_t_ready"), sem("h_ready")
        h02_ready, xj_ready, pads_set = sem("h02_ready"), sem("xj_ready"), sem("xj_pads_set")
        x1_stored, xj_stored = [sem(f"x1_stored{u}") for u in range(4)], [sem(f"xj_stored{u}") for u in range(4)]
        dve_step, pool_step = sem("dve_step6"), sem("pool_step6")
        dve_turn = sem("n_turn")
        block = ctx.enter_context(nc.Block())

        @block.sync
        def _(sp):
            sp.dma_start(w_o[:, :, :], wo.rearrange("(c p) n -> p c n", p=P)).then_inc(weights_in, 16)
            for k, (w, b) in enumerate(((w1, b1), (w2, b2))):
                sp.dma_start(w_12[:, :, k * D:(k + 1) * D], w.rearrange("(c p) n -> p c n", p=P)).then_inc(weights_in, 16)
                sp.dma_start(b_row[:, (k + 1) * D:(k + 2) * D], b.rearrange("(a n) -> a n", a=1)).then_inc(weights_in, 16)
            sp.dma_start(b_row[:, 0:D], bo.rearrange("(a n) -> a n", a=1)).then_inc(weights_in, 16)
            for n, a in (("gamma", gamma), ("beta", beta), ("wa1", wa1), ("wa2", wa2)):
                sp.dma_start(wide[n][:, :], a.partition_broadcast(P)).then_inc(weights_in, 16)
            for k, a in enumerate((ba1, ba2)):
                sp.dma_start(ba[:, k:k + 1], a.partition_broadcast(P)).then_inc(weights_in, 16)

            def load(b, s):
                if not early(b, 4):
                    sp.wait_ge(z_ready, b - 3)
                r = rows_of(b)
                sp.dma_start(x_in[s][0:r, :], t["x"][bass.ds(b * P, r), :]).then_inc(loaded[s], 16)
                sp.dma_start(v_in[s][0:r, :], t["v_rows"][bass.ds(b * P, r), :]).then_inc(loaded[s], 16)

            def store_x1(b, s):
                r = rows_of(b)
                sp.wait_ge(normed[1], b + 1)
                sp.dma_start(t["x1_rows"][bass.ds(b * P, r), :], x1[s][0:r, :]).then_inc(x1_stored[s], 16)

            def store_xj(b, s):
                r = rows_of(b)
                sp.wait_ge(xj_ready, b + 1)
                sp.dma_start(t["xj_rows"][bass.ds(b * P, r), :], xj[s][0:r, :]).then_inc(xj_stored[s], 16)

            skewed(sp, [(0, load), (4, store_x1), (5, store_xj)])
            for s in range(4):
                uses = len(range(s, NB, 4))
                sp.wait_ge(x1_stored[s], 16 * uses)
                sp.wait_ge(xj_stored[s], 16 * uses)

        @block.gpsimd
        def _(pool):
            step = Serial(pool, pool_step, 4 * 2)
            for s in range(4):
                nc.gpsimd.memset(xj[s][:, D:XW], 0.0).then_inc(pads_set, 1)
            pool.wait_ge(weights_in, 12 * 16)

            def affine(b, s):
                pool.wait_ge(normed[0], b + 1)
                step(nc.gpsimd.tensor_tensor(z[s][:, :], y[s][:, :], wide["gamma"][:, :], ALU.mult))
                step(nc.gpsimd.tensor_tensor(z[s][:, :], z[s][:, :], wide["beta"][:, :], ALU.add))
                nc.gpsimd.tensor_tensor(z[s][:, :], z[s][:, :], x_in[s][:, :], ALU.add).then_inc(z_ready, 1)

            skewed(pool, [(2, affine)], step)

        @block.scalar
        def _(act):
            def sqrt(k):
                def f(b, s):
                    act.wait_ge(var_ready[k], b + 1)
                    nc.scalar.activation(small[s][:, 16 + k:17 + k], small[s][:, 9 + 2 * k:10 + 2 * k], ACT.Sqrt).then_inc(std_ready[k], 1)
                return f

            def normalise(k):
                def f(b, s):
                    act.wait_ge(scale_ready[k], b + 1)
                    src, dst = ((y, y), (z, x1))[k]
                    if k and not early(b, 4):
                        act.wait_ge(x1_stored[s], (b - s) * 4)
                    if k and not early(b, 4):
                        act.wait_ge(x1_turned, b - 3)
                    nc.scalar.activation(dst[s][:, :], src[s][:, :], ACT.Identity, scale=small[s][:, 20 + 2 * k:21 + 2 * k],
                                         bias=small[s][:, 21 + 2 * k:22 + 2 * k]).then_inc(normed[k], 1)
                return f

            def copy_x1_t(b, s):
                act.wait_ge(x1_turned, b + 1)
                nc.scalar.copy(x1_t[s][:, :, :], ps_t[1][:, :, :]).then_inc(x1_t_ready, 1)

            def copy_msg_t(b, s):
                act.wait_ge(msg_turned, b + 1)
                nc.scalar.copy(msg_t[s][:, :, :], ps_t[0][:, :, :]).then_inc(msg_t_ready, 1)

            def fifth(b, s):
                act.wait_ge(h_ready, b + 1)
                nc.scalar.activation(h02[s][:, :], ps_h[s % 2][:, :], ACT.Copy, scale=0.2).then_inc(h02_ready, 1)

            skewed(act, [(4, fifth), (2, sqrt(0)), (3, sqrt(1)), (2, normalise(0)), (3, normalise(1)), (3, copy_x1_t), (1, copy_msg_t)])

        @block.tensor
        def _(pe):
            pe.wait_ge(weights_in, 12 * 16)

            def turn_x1(b, s):
                pe.wait_ge(normed[1], b + 1)
                if not early(b, 1):
                    pe.wait_ge(x1_t_ready, b)
                for c in range(2):
                    last = nc.tensor.transpose(ps_t[1][:, c, :], x1[s][:, c * P:(c + 1) * P], ident[:, :])
                last.then_inc(x1_turned, 1)

            def turn_msg(b, s):
                pe.wait_ge(msg_ready, b + 1)
                if not early(b, 1):
                    pe.wait_ge(msg_t_ready, b)
                for c in range(2):
                    last = nc.tensor.transpose(ps_t[0][:, c, :], msg[s][:, c * P:(c + 1) * P], ident[:, :])
                last.then_inc(msg_turned, 1)

            def project_x1(b, s):
                pe.wait_ge(x1_t_ready, b + 1)
                if not early(b):
                    pe.wait_ge(xj_ready, b - 1)
                for c in range(2):
                    nc.tensor.matmul(ps_h[s % 2][:, :], x1_t[s][:, c, :], w_12[:, c, :], start=(c == 0), stop=False)
                nc.tensor.matmul(ps_h[s % 2][:, :], ones[0:1, :], b_row[:, D:3 * D], start=False, stop=True).then_inc(h_ready, 1)

            def project_msg(b, s):
                pe.wait_ge(msg_t_ready, b + 1)
                if not early(b):
                    pe.wait_ge(var_ready[0], b - 1)
                for c in range(2):
                    nc.tensor.matmul(ps_o[s % 2][:, :], msg_t[s][:, c, :], w_o[:, c, :], start=(c == 0), stop=False)
                nc.tensor.matmul(ps_o[s % 2][:, :], ones[0:1, :], b_row[:, 0:D], start=False, stop=True).then_inc(o_ready, 1)

            skewed(pe, [(3, turn_x1), (1, turn_msg), (3, project_x1), (1, project_msg)])

        @block.vector
        def _(dve):
            step = Serial(dve, dve_step, 4 * 16)
            dve.wait_ge(weights_in, 12 * 16)
            dve.wait_ge(pads_set, 4)

            def stats(k):
                def f(b, s):
                    v, m = (y, z)[k][s], small[s]
                    if k == 0:
                        dve.wait_ge(o_ready, b + 1)
                        step(dve.tensor_tensor(v[:, :], ps_o[s % 2][:, :], x_in[s][:, :], ALU.add))
                    else:
                        dve.wait_ge(z_ready, b + 1)
                    step(dve.bn_stats(m[:, 24:30], v[:, :]))
                    dve.sem_inc(dve_turn, 1)
                    step(dve.bn_aggr(m[:, 8 + 2 * k:10 + 2 * k], m[:, 24:30]))
                    dve.tensor_scalar(m[:, 9 + 2 * k:10 + 2 * k], m[:, 9 + 2 * k:10 + 2 * k], EPS, None, ALU.add).then_inc(var_ready[k], 1)
                return f

            def scale(k):
                def f(b, s):
                    m = small[s]
                    dve.wait_ge(std_ready[k], b + 1)
                    step(dve.reciprocal(m[:, 20 + 2 * k:21 + 2 * k], m[:, 16 + k:17 + k]))
                    dve.scalar_tensor_tensor(m[:, 21 + 2 * k:22 + 2 * k], m[:, 8 + 2 * k:9 + 2 * k], -1.0, m[:, 20 + 2 * k:21 + 2 * k],
                                             ALU.mult, ALU.mult).then_inc(scale_ready[k], 1)
                return f

            def message(b, s):
                m, acc = small[s], tab[:, bass.ds(b * AW, D)]
                den = tab[:, bass.ds(b * AW + D, H)]
                dve.wait_ge(loaded[s], (b - s) * 8 + 32 if not isinstance(b, int) else 32 * (b // 4 + 1))
                step(dve.tensor_scalar(m[:, 0:H], den, 0.0, None, ALU.is_equal))
                step(dve.tensor_tensor(m[:, H:2 * H], den, m[:, 0:H], ALU.add))
                step(dve.reciprocal(m[:, H:2 * H], m[:, H:2 * H]))
                step(dve.tensor_tensor(msg[s][:, :].rearrange("p (h d) -> p h d", h=H), acc.rearrange("p (h d) -> p h d", h=H),
                                       m[:, H:2 * H].unsqueeze(2).broadcast_to([P, H, DH]), ALU.mult))
                dve.scalar_tensor_tensor(msg[s][:, :], v_in[s][:, :], m[:, 0:1], msg[s][:, :], ALU.mult, ALU.add).then_inc(msg_ready, 1)

            def scores(b, s):
                dve.wait_ge(h02_ready, b + 1)
                if not early(b, 4):
                    dve.wait_ge(xj_stored[s], (b - s) * 4 if not isinstance(b, int) else 16 * (b // 4))
                step(dve.tensor_tensor(h02[s][:, 0:D], ps_h[s % 2][:, 0:D], h02[s][:, 0:D], ALU.max))
                step(dve.tensor_tensor(xj[s][:, 0:D], ps_h[s % 2][:, D:2 * D], h02[s][:, D:2 * D], ALU.max))
                step(dve.tensor_tensor_reduce(junk[:, :], h02[s][:, 0:D], wide["wa1"][:, :], 1.0, 0.0, ALU.mult, ALU.add, small[s][:, 32:33]))
                step(dve.tensor_tensor_reduce(junk[:, :], xj[s][:, 0:D], wide["wa2"][:, :], 1.0, 0.0, ALU.mult, ALU.add, small[s][:, 33:34]))
                step(dve.tensor_tensor(t["a1_tab"][:, bass.ds(b, 1)], small[s][:, 32:33], ba[:, 0:1], ALU.add))
                dve.tensor_tensor(xj[s][:, D:D + 1], small[s][:, 33:34], ba[:, 1:2], ALU.add).then_inc(xj_ready, 1)

            skewed(dve, [(2, stats(0)), (3, stats(1)), (2, scale(0)), (3, scale(1)), (1, message), (4, scores)], step)
            dve.wait_ge(xj_ready, NB)


def attend(nc, t):
    with ExitStack() as ctx:
        def sb(name, shape, dt=fp32):
            return ctx.enter_context(nc.sbuf_tensor(name, shape, dt))

        def sem(name):
            return ctx.enter_context(nc.semaphore(name))

        tab = t["node_tab"]
        index = [sb(f"t_index{u}", [P, U], i32) for u in range(V)]
        rows = [sb(f"t_rows{u}", [P, U, XW]) for u in range(V)]
        hot = [sb(f"t_hot{u}", [P, U, P]) for u in range(4)]
        node_hot = [sb(f"t_node_hot{u}", [P, U, P]) for u in range(2)]
        hot_att = [sb(f"t_hot_att{u}", [P, U, P]) for u in range(2)]
        logit = [sb(f"t_logit{u}", [P, U]) for u in range(2)]
        att = [sb(f"t_att{u}", [P, U]) for u in range(2)]
        ps_hot = ctx.enter_context(nc.psum_tensor("ps_hot", [P, U, P], fp32))
        ps_a1 = [ctx.enter_context(nc.psum_tensor(f"ps_a1{u}", [P, U], fp32)) for u in range(2)]
        ps_sum = [ctx.enter_context(nc.psum_tensor(f"ps_xsum{u}", [P, U, D], fp32)) for u in range(2)]
        index_ready, rows_in = sem("t_index_ready"), [sem(f"t_rows_in{u}") for u in range(V)]
        hot_ready, turned, turned_copied, a1_ready = sem("t_hot_ready"), sem("t_turned"), sem("t_turned_copied"), sem("t_a1_ready")
        logit_ready, att_ready, hot_att_ready, summed, added = sem("logit_ready"), sem("att_ready"), sem("hot_att_ready"), sem("t_summed"), sem("t_added")
        pool_turn, cleared = sem("t_pool_turn"), sem("t_cleared")
        block = ctx.enter_context(nc.Block())

        @block.gpsimd
        def _(pool):
            def turn(i):
                for u in range(V):
                    g = V * i + u
                    pool.wait_ge(index_ready, g + 1)
                    if not early(i, 1):
                        pool.wait_ge(summed, g - V + 1)
                    pool.sem_inc(pool_turn, 1)
                    for k in range(U):
                        pool.indirect_dma_start(out=rows[u][:, k, :], out_offset=None, in_=t["xj_rows"],
                                                in_offset=bass.IndirectOffsetOnAxis(ap=index[u][:, k:k + 1], axis=0))\
                            .then_inc(rows_in[u], 16)

            group_turns(pool, turn)

        @block.scalar
        def _(act):
            def turn(i):
                for u in range(V):
                    g = V * i + u
                    if not early(i, 1):
                        act.wait_ge(rows_in[u], 16 * U * i)
                    nc.scalar.copy(index[u][:, :], t["other1"][:, bass.ds(g * U, U)]).then_inc(index_ready, 1)
                    act.wait_ge(turned, g + 1)
                    if not early(g):
                        act.wait_ge(a1_ready, g - 1)
                    nc.scalar.copy(node_hot[u % 2][:, :, :], ps_hot[:, :, :]).then_inc(turned_copied, 1)
                    if not early(g, 1):
                        weigh(g - 1, u - 1)

            def weigh(g, u):
                act.wait_ge(logit_ready, g + 1)
                nc.scalar.activation(att[u % 2][:, :], logit[u % 2][:, :], ACT.Sigmoid).then_inc(att_ready, 1)
                act.wait_ge(att_ready, g + 1)
                if not early(g):
                    act.wait_ge(summed, g - 1)
                for k in range(U):
                    last = nc.scalar.activation(hot_att[u % 2][:, k, :], hot[u % 4][:, k, :], ACT.Copy, scale=att[u % 2][:, k:k + 1])
                last.then_inc(hot_att_ready, 1)

            group_turns(act, turn)
            weigh(G - 1, V - 1)

        @block.vector
        def _(dve):
            def encode(g, u):
                if not early(g, 4):
                    dve.wait_ge(hot_att_ready, g - 3)
                local = t["local1"][:, bass.ds(g * U, U)].unsqueeze(2).broadcast_to([P, U, P])
                dve.tensor_tensor(hot[u % 4][:, :, :], t["iota"][:, :].unsqueeze(1).broadcast_to([P, U, P]), local, ALU.is_equal)\
                    .then_inc(hot_ready, 1)

            def add_logits(g, u, i):
                dve.wait_ge(rows_in[u], 16 * U * (i + 1))
                dve.wait_ge(a1_ready, g + 1)
                dve.tensor_tensor(logit[u % 2][:, :], ps_a1[u % 2][:, :], rows[u][:, :, D], ALU.add).then_inc(logit_ready, 1)

            def add(g, u, blocks):
                dve.wait_ge(summed, g + 1)
                for k in range(U):
                    acc = tab[:, bass.ds(blocks[k] * D, D)]
                    if not (isinstance(g, int) and g == 0 and k == 0):
                        dve.wait_ge(added, g * U + k)
                    dve.tensor_tensor(acc, acc, ps_sum[u % 2][:, k, :], ALU.add).then_inc(added, 1)

            def turn(i):
                blocks = blocks_of(dve, t["packed_late1"], i)
                for u in range(V):
                    g = V * i + u
                    if not (isinstance(g, int) and g + 2 >= G):
                        encode(g + 2, u + 2)
                    add_logits(g, u, i)
                    if not early(g, LAG):
                        add(g - LAG, u - LAG, blocks[u * U:])

            encode(0, 0)
            encode(1, 1)
            dve.memset(tab[:, 0:NB * D], 0.0).then_inc(cleared, 1)
            dve.wait_ge(cleared, 1)
            group_turns(dve, turn)
            blocks = blocks_of(dve, t["packed_late1"], G // V)
            for k in range(LAG):
                add(G - LAG + k, k, blocks[k * U:])
            dve.wait_ge(added, G * U)

        @block.tensor
        def _(pe):
            def turn_hot(g, u):
                pe.wait_ge(hot_ready, g + 1)
                if not early(g, 1):
                    pe.wait_ge(turned_copied, g)
                for k in range(U):
                    last = nc.tensor.transpose(ps_hot[:, k, :], hot[u % 4][:, k, :], t["ident"][:, :])
                last.then_inc(turned, 1)

            def sum_up(g, u):
                pe.wait_ge(hot_att_ready, g + 1)
                if not early(g):
                    pe.wait_ge(added, (g - 1) * U)
                for k in range(U):
                    last = nc.tensor.matmul(ps_sum[u % 2][:, k, :], hot_att[u % 2][:, k, :], rows[u % V][:, k, 0:D], start=True, stop=True)
                last.then_inc(summed, 1)

            def turn(i):
                blocks = blocks_of(pe, t["packed1"], i)
                for u in range(V):
                    g = V * i + u
                    if not (isinstance(g, int) and g == G - 1):
                        turn_hot(g + 1, u + 1)
                    pe.wait_ge(turned_copied, g + 1)
                    if not early(g):
                        pe.wait_ge(logit_ready, g - 1)
                    for k in range(U):
                        last = nc.tensor.matmul(ps_a1[u % 2][:, k:k + 1], node_hot[u % 2][:, k, :],
                                                t["a1_tab"][:, bass.ds(blocks[u * U + k], 1)], start=True, stop=True)
                    last.then_inc(a1_ready, 1)
                    if not early(g, 1):
                        sum_up(g - 1, u - 1)

            turn_hot(0, 0)
            group_turns(pe, turn)
            sum_up(G - 1, V - 1)


def finish(nc, t):
    with ExitStack() as ctx:
        def ring(name, shape):
            return [ctx.enter_context(nc.sbuf_tensor(f"{name}{u}", shape, fp32)) for u in range(4)]

        def sem(name):
            return ctx.enter_context(nc.semaphore(name))

        tab = t["node_tab"]
        x1, y, small = ring("f_x1", [P, D]), ring("f_y", [P, D]), ring("f_small", [P, 16])
        loaded, stored = [sem(f"f_loaded{u}") for u in range(4)], [sem(f"f_stored{u}") for u in range(4)]
        var_ready, std_ready, scale_ready, normed, dve_step = sem("f_var"), sem("f_std"), sem("f_scale"), sem("f_normed"), sem("f_dve_step")
        dve_turn = sem("f_turn")
        block = ctx.enter_context(nc.Block())

        @block.sync
        def _(sp):
            def load(b, s):
                if not early(b, 4):
                    sp.wait_ge(var_ready, b - 3)
                r = rows_of(b)
                sp.dma_start(x1[s][0:r, :], t["x1_rows"][bass.ds(b * P, r), :]).then_inc(loaded[s], 16)

            def store(b, s):
                r = rows_of(b)
                sp.wait_ge(normed, b + 1)
                sp.dma_start(t["out"][bass.ds(b * P, r), :], y[s][0:r, :]).then_inc(stored[s], 16)

            skewed(sp, [(0, load), (3, store)])
            for s in range(4):
                sp.wait_ge(stored[s], 16 * len(range(s, NB, 4)))

        @block.scalar
        def _(act):
            def sqrt(b, s):
                act.wait_ge(var_ready, b + 1)
                nc.scalar.activation(small[s][:, 8:9], small[s][:, 7:8], ACT.Sqrt).then_inc(std_ready, 1)

            def normalise(b, s):
                act.wait_ge(scale_ready, b + 1)
                nc.scalar.activation(y[s][:, :], y[s][:, :], ACT.Identity, scale=small[s][:, 9:10], bias=small[s][:, 10:11]).then_inc(normed, 1)

            skewed(act, [(2, normalise), (1, sqrt)])

        @block.vector
        def _(dve):
            step = Serial(dve, dve_step, 4 * 4)

            def stats(b, s):
                m = small[s]
                dve.wait_ge(loaded[s], (b - s) * 4 + 16 if not isinstance(b, int) else 16 * (b // 4 + 1))
                if not early(b, 4):
                    dve.wait_ge(stored[s], (b - s) * 4 if not isinstance(b, int) else 16 * (b // 4))
                step(dve.scalar_tensor_tensor(y[s][:, :], x1[s][:, :], 2.0, tab[:, bass.ds(b * D, D)], ALU.mult, ALU.add))
                step(dve.bn_stats(m[:, 0:6], y[s][:, :]))
                dve.sem_inc(dve_turn, 1)
                step(dve.bn_aggr(m[:, 6:8], m[:, 0:6]))
                dve.tensor_scalar(m[:, 7:8], m[:, 7:8], EPS, None, ALU.add).then_inc(var_ready, 1)

            def scale(b, s):
                m = small[s]
                dve.wait_ge(std_ready, b + 1)
                step(dve.reciprocal(m[:, 9:10], m[:, 8:9]))
                dve.scalar_tensor_tensor(m[:, 10:11], m[:, 6:7], -1.0, m[:, 9:10], ALU.mult, ALU.mult).then_inc(scale_ready, 1)

            skewed(dve, [(1, stats), (2, scale)], step)


_INS = ["x", "src", "dst", "edge_type_64", "L0_gnn_query_emb", "L0_gnn_Wq", "L0_gnn_bq", "L0_gnn_Wk", "L0_gnn_bk",
        "L0_gnn_Wv", "L0_gnn_bv", "L0_gnn_rel_w", "L0_gnn_Wo", "L0_gnn_bo", "L0_gnn_gamma", "L0_gnn_beta",
        "L1_gnn_W1", "L1_gnn_b1", "L1_gnn_W2", "L1_gnn_b2", "L1_gnn_wa1", "L1_gnn_ba1", "L1_gnn_wa2", "L1_gnn_ba2"]


def kernel(**inputs):
    import numpy as _np
    import concourse.bacc as _bacc
    from concourse.bass_utils import run_bass_kernel_spmd as _run

    nc = _bacc.Bacc("TRN2", target_bir_lowering=False, num_devices=1)
    arrays, args = {}, []
    for name in _INS:
        a = _np.ascontiguousarray(inputs[name])
        arrays[f"in_{name}"] = a
        args.append(nc.dram_tensor(f"in_{name}", a.shape, mybir.dt.from_np(a.dtype), kind="ExternalInput").ap())
    out = nc.dram_tensor("out", (N, D), fp32, kind="ExternalOutput").ap()
    gnn_kernel(nc, *args, out)
    r = _run(nc, [arrays], core_ids=[0])
    return r.results[0]["out"]
```

```python
import concourse.bass as bass
from concourse import mybir
from contextlib import ExitStack

fp32 = mybir.dt.float32
bf16 = mybir.dt.bfloat16
i32 = mybir.dt.int32
ALU = mybir.AluOpType
ACT = mybir.ActivationFunctionType
AX = mybir.AxisListType

P = 128
N = 12500
E = 200000
D = 256
H = 4
DH = D // H
R = 64
NB = -(-N // P)
LAST_ROWS = N - (NB - 1) * P
T = -(-E // P)
U = 4
V = 4
TURN = U * V
LAG = 2
AHEAD = 2
G = -(-(T + NB - 1) // TURN) * V
S = G * U
C = S // P
AW = D + H
XW = D + 4
LOGN = 18
F = (1 << LOGN) // P
NODE_BITS = 14
NODE_MASK = (1 << NODE_BITS) - 1
KEY_BIAS = 1 << 30
PAD_NODE = NB * P - 1
EPS = 1e-5
LOWEST = -1.0e30
assert S % P == 0 and C * P >= T and PAD_NODE >= N and PAD_NODE < (1 << NODE_BITS) and NB <= P


class Serial:

    def __init__(self, eng, sem, per_loop=0):
        self.eng, self.sem, self.per_loop, self.n, self.turn = eng, sem, per_loop, 0, 0

    def __call__(self, ins):
        self.n += 1
        ins.then_inc(self.sem, 1)
        self.eng.wait_ge(self.sem, self.turn + self.n)

    def enter(self, i, per_turn):
        self.turn, self.start, self.per = i * per_turn, self.n, per_turn

    def leave(self, turns):
        assert self.n - self.start == self.per, (self.n, self.start, self.per)
        self.n, self.turn = self.start + self.per * turns, 0


def block_pairs(eng, body):
    body(0, 0)
    body(1, 1)
    with eng.Fori(1, NB // 2 - 1) as i:
        body(2 * i, 0)
        body(2 * i + 1, 1)
    body(NB - 2, 0)
    body(NB - 1, 1)


def pairs_and_flips(eng, body, flip):
    rounds = LOGN - 11
    few = 3
    first = NB // 2 - few * rounds
    body(0, 0)
    body(1, 1)
    start = 1
    for r in range(rounds + 1):
        end = first + few * r
        with eng.Fori(start, end - (r == rounds)) as i:
            body(2 * i, 0)
            body(2 * i + 1, 1)
        if r < rounds:
            flip(2 * r)
            flip(2 * r + 1)
        start = end
    body(NB - 2, 0)
    body(NB - 1, 1)


def split_exactly(pool, step, numbers, parts, rest):
    step(pool.tensor_copy(parts[0], numbers))
    step(pool.tensor_tensor(rest, numbers, parts[0], ALU.subtract))
    step(pool.tensor_copy(parts[1], rest))
    step(pool.tensor_tensor(rest, rest, parts[1], ALU.subtract))
    step(pool.tensor_copy(parts[2], rest))


def early(b, n=2):
    return isinstance(b, int) and b < n


def skewed(eng, stages, step=None):
    deepest = max(lag for lag, _ in stages)
    first = -(-(deepest + 4) // 4) * 4
    last = first + (NB - 1 - first) // 4 * 4

    def turn(i, w):
        for lag, stage in stages:
            if not isinstance(i, int) or 0 <= i - lag < NB:
                stage(i - lag, (w - lag) % 4)

    for i in range(first):
        turn(i, i % 4)
    with eng.Fori(first // 4, last // 4) as i:
        if step:
            step.enter(i - first // 4, step.per_loop)
        for w in range(4):
            turn(4 * i + w, w)
        if step:
            step.leave(last // 4 - first // 4)
    for i in range(last, NB + deepest):
        turn(i, i % 4)


def rows_of(b):
    return LAST_ROWS if isinstance(b, int) and b == NB - 1 else P


def group_turns(eng, turn):
    turn(0)
    with eng.Fori(1, G // V - 1) as i:
        turn(i)
    turn(G // V - 1)


def places_of(eng, packed, i, row):
    v = eng.value_load(packed[0:1, bass.ds(i, 1)], min_val=0, max_val=(P << (TURN - 1)) - 1)
    places = [eng.snap(((v & (P - 1)) * row).with_bounds(min_val=0, max_val=(NB - 1) * row))]
    for k in range(1, TURN):
        places.append(eng.snap((places[-1] + ((v >> (6 + k)) & 1) * row).with_bounds(min_val=0, max_val=(NB - 1) * row)))
    return places


def gnn_kernel(nc, x, src, dst, edge_type, query, wq, bq, wk, bk, wv, bv, rel_w, wo, bo, gamma, beta,
               w1, b1, w2, b2, wa1, ba1, wa2, ba2, out):
    with ExitStack() as ctx:
        def sb(name, shape, dt=fp32):
            return ctx.enter_context(nc.sbuf_tensor(name, shape, dt))

        def dram(name, shape, dt=fp32):
            return nc.dram_tensor(name, shape, dt, kind="Internal").ap()

        t = {}
        t["k_rows"] = dram("k_rows", (N, D))
        t["v_rows"] = dram("v_rows", (N, D))
        t["x1_rows"] = dram("x1_rows", (N, D))
        t["xj_rows"] = dram("xj_rows", (N, XW))
        t["sorted_keys"] = dram("sorted_keys", (1 << LOGN,), i32)

        t["node_tab"] = sb("node_tab", [P, NB * AW])
        t["ident"] = sb("ident", [P, P])
        t["ident_h"] = sb("ident_h", [P, P], bf16)
        t["iota"] = sb("iota", [P, P])
        t["ones"] = sb("ones", [P, P])
        t["ones_h"] = sb("ones_h", [P, P], bf16)
        for layer in range(2):
            t[f"other{layer}"] = sb(f"other{layer}", [P, S], i32)
            t[f"local{layer}"] = sb(f"local{layer}", [P, S])
            t[f"packed_late{layer}"] = sb(f"packed_late{layer}", [1, S // TURN + 1], i32)
            t[f"packed{layer}"] = sb(f"packed{layer}", [1, S // TURN], i32)
        t["rel"] = sb("rel", [P, S])
        t["score"] = sb("score", [P, S * H])
        t["a1_tab"] = sb("a1_tab", [P, NB])

        t["x"], t["src"], t["dst"], t["edge_type"], t["out"] = x, src, dst, edge_type, out
        project_and_sort(nc, t, query, wq, bq, wk, bk, wv, bv)
        build_steps(nc, t)
        edge_scores(nc, t, rel_w)
        softmax_numerators(nc, t)
        aggregate(nc, t)
        update_nodes(nc, t, wo, bo, gamma, beta, w1, b1, w2, b2, wa1, ba1, wa2, ba2)
        attend(nc, t)
        finish(nc, t)


def project_and_sort(nc, t, query, wq, bq, wk, bk, wv, bv):
    x, tab, ident, ones = t["x"], t["node_tab"], t["ident"], t["ones"]
    with ExitStack() as ctx:
        def sb(name, shape, dt=fp32):
            return ctx.enter_context(nc.sbuf_tensor(name, shape, dt))

        def sem(name):
            return ctx.enter_context(nc.semaphore(name))

        x_in = [sb(f"x_in{u}", [P, D]) for u in range(2)]
        enh = [sb(f"enh{u}", [P, 2, P]) for u in range(2)]
        kv_out = [sb(f"kv_out{u}", [P, 2 * D]) for u in range(2)]
        w_qkv = sb("w_qkv", [P, 2, 3 * D])
        b_qkv, b_rest = sb("b_qkv", [3 * D // P, P]), sb("b_rest", [3 * D // P, P])
        b_part = [sb(f"b_part{k}", [3 * D // P, P], bf16) for k in range(3)]
        b_parts = sb("b_parts", [3, 3 * D], bf16)
        q_col = sb("q_col", [P, 2])
        q01 = sb("q01", [P, 2])
        keys = [sb(f"keys{u}", [P, F], i32) for u in range(2)]
        sign = sb("sign", [P, 8])
        pbit = sb("pbit", [P, 8], i32)
        pid = sb("pid", [P, 1], i32)
        ps_xt = ctx.enter_context(nc.psum_tensor("ps_xt", [P, 2, P], fp32))
        ps_q = ctx.enter_context(nc.psum_tensor("ps_q", [P, D], fp32))
        ps_kv = [ctx.enter_context(nc.psum_tensor(f"ps_kv{u}", [P, 2 * D], fp32)) for u in range(2)]
        ps_flip = ctx.enter_context(nc.psum_tensor("ps_flip", [P, 4, 512], fp32))

        consts_set, weights_in, x_loaded = sem("consts_set"), sem("weights_in"), [sem("x_loaded0"), sem("x_loaded1")]
        xt_ready, enh_ready, mm_done = sem("xt_ready"), sem("enh_ready"), sem("mm_done")
        evacuated = sem("evacuated")
        kv_stored, q01_ready = [sem("kv_stored0"), sem("kv_stored1")], sem("q01_ready")
        pool_step, dve_step = sem("pool_step"), sem("dve_step")
        keys_in, pads_set = sem("keys_in"), sem("pads_set")
        to_flip, flipped, flip_copied, keys_out = sem("to_flip"), sem("flipped"), sem("flip_copied"), sem("keys_out")
        sorted_ready, b_parts_in, q_left = sem("sorted_ready"), sem("b_parts_in"), sem("q_left")
        full_p = E // F
        rest = E - full_p * F
        block = ctx.enter_context(nc.Block())

        @block.sync
        def _(sp):
            sp.wait_ge(pads_set, 1)
            for n, a in enumerate((t["src"], t["dst"])):
                sp.dma_start(keys[n][0:full_p, :], a[0:full_p * F].rearrange("(p f) -> p f", f=F)).then_inc(keys_in, 16)
                sp.dma_start(keys[n][full_p:full_p + 1, 0:rest],
                             a[full_p * F:E].rearrange("(p f) -> p f", p=1)).then_inc(keys_in, 16)
            for n, (w, b) in enumerate(((wq, bq), (wk, bk), (wv, bv))):
                sp.dma_start(w_qkv[:, :, n * D:(n + 1) * D], w.rearrange("(c p) n -> p c n", p=P)).then_inc(weights_in, 16)
                sp.dma_start(b_qkv[2 * n:2 * n + 2, :], b.rearrange("(a n) -> a n", n=P)).then_inc(weights_in, 16)
            with nc.allow_non_contiguous_dma(reason="256 numbers, once"):
                sp.dma_start(q_col[:, :], query.rearrange("(c p) -> p c", p=P)).then_inc(weights_in, 16)

            def load(b, u):
                r = rows_of(b)
                sp.dma_start(x_in[u][0:r, :], x[bass.ds(b * P, r), :]).then_inc(x_loaded[u], 16)

            load(0, 0)
            load(1, 1)

            def body(b, u):
                sp.wait_ge(xt_ready, b + 1)
                if not (isinstance(b, int) and b + 2 >= NB):
                    load(b + 2, u)

            with sp.Fori(0, NB // 2 - 2) as i:
                body(2 * i, 0)
                body(2 * i + 1, 1)
            body(NB - 4, 0)
            body(NB - 3, 1)
            sp.wait_ge(sorted_ready, 1)
            sp.dma_start(t["sorted_keys"].rearrange("(p f) -> p f", f=F), keys[0][:, :]).then_inc(keys_out, 16)
            sp.wait_ge(keys_out, 16)

        @block.gpsimd
        def _(pool):
            step = Serial(pool, pool_step)
            step(nc.gpsimd.memset(keys[0][96:P, :], PAD_NODE))
            nc.gpsimd.memset(keys[1][96:P, :], 0).then_inc(pads_set, 1)
            pool.wait_ge(pads_set, 1)
            for m, base in ((t["ident"], 0.0), (t["ident_h"], 0.0), (ones, 1.0)):
                step(nc.gpsimd.memset(m[:, :], base))
            for m in (t["ident"], t["ident_h"]):
                step(nc.gpsimd.affine_select(out=m[:, :], in_=m[:, :], compare_op=ALU.not_equal, fill=1.0,
                                             base=0, pattern=[[-1, P]], channel_multiplier=1))
            step(nc.gpsimd.iota(t["iota"][:, :], [[1, P]], base=0, channel_multiplier=0,
                                allow_small_or_imprecise_dtypes=True))
            step(nc.gpsimd.iota(pid[:, :], [[1, 1]], base=0, channel_multiplier=1))
            step(nc.gpsimd.memset(t["a1_tab"][:, :], 0.0))
            step(nc.gpsimd.memset(t["ones_h"][:, :], 1.0))
            pool.sem_inc(consts_set, 1)
            pool.wait_ge(weights_in, 7 * 16)
            split_exactly(nc.gpsimd, step, b_qkv[:, :], [p[:, :] for p in b_part], b_rest[:, :])
            for k in range(3):
                pool.dma_start(b_parts[k:k + 1, :], b_part[k][:, :]).then_inc(b_parts_in, 16)

            def body(b, u):
                r = rows_of(b)
                pool.wait_ge(evacuated, b + 1)
                for k, rows in enumerate((t["k_rows"], t["v_rows"])):
                    pool.dma_start(rows[bass.ds(b * P, r), :], kv_out[u][0:r, k * D:(k + 1) * D])\
                        .then_inc(kv_stored[u], 16)

            block_pairs(pool, body)
            for u in range(2):
                pool.wait_ge(kv_stored[u], NB // 2 * 32)

        @block.scalar
        def _(act):
            act.wait_ge(weights_in, 7 * 16)
            nc.scalar.mul(q01[:, :], q_col[:, :], 0.1).then_inc(q01_ready, 1)
            act.wait_ge(q01_ready, 1)

            def enhance(b, u):
                act.wait_ge(xt_ready, b + 1)
                for c in range(2):
                    last = nc.scalar.activation(enh[u][:, c, :], ps_xt[:, c, :], ACT.Identity, bias=q01[:, c:c + 1])
                last.then_inc(enh_ready, 1)

            def evacuate(b, u):
                act.wait_ge(mm_done, b + 1)
                if not early(b):
                    act.wait_ge(kv_stored[u], (b - u) * 16)
                nc.scalar.activation(tab[:, bass.ds(b * AW, D)], ps_q[:, :], ACT.Copy, scale=float(DH) ** -0.5)\
                    .then_inc(q_left, 1)
                nc.scalar.activation(kv_out[u][:, :], ps_kv[u][:, :], ACT.Copy).then_inc(evacuated, 1)

            enhance(0, 0)

            def body(b, u):
                if not (isinstance(b, int) and b == NB - 1):
                    enhance(b + 1, 1 - u)
                evacuate(b, u)

            def copy_flipped(r):
                for bank in range(4):
                    act.wait_ge(flipped, 4 * r + bank + 1)
                    last = nc.scalar.activation(keys[0][:, bank * 512:(bank + 1) * 512].bitcast(fp32),
                                                ps_flip[:, bank, :], ACT.Copy)
                last.then_inc(flip_copied, 1)

            pairs_and_flips(act, body, copy_flipped)

        @block.tensor
        def _(pe):
            pe.wait_ge(consts_set, 1)
            pe.wait_ge(weights_in, 7 * 16)
            pe.wait_ge(b_parts_in, 3 * 16)

            def transpose(b, u):
                pe.wait_ge(x_loaded[u], (b - u) * 8 + 16)
                for c in range(2):
                    last = nc.tensor.transpose(ps_xt[:, c, :], x_in[u][:, c * P:(c + 1) * P], ident[:, :])
                last.then_inc(xt_ready, 1)

            def body(b, u):
                pe.wait_ge(enh_ready, b + 1)
                if not (isinstance(b, int) and b == NB - 1):
                    transpose(b + 1, 1 - u)
                if not early(b):
                    pe.wait_ge(evacuated, b - 1)
                for o, (lo, hi) in ((ps_kv[u][:, :], (D, 3 * D)), (ps_q[:, :], (0, D))):
                    if lo == 0 and not early(b, 1):
                        pe.wait_ge(q_left, b)
                    for c in range(2):
                        nc.tensor.matmul(o, enh[u][:, c, :], w_qkv[:, c, lo:hi], start=(c == 0), stop=False)
                    last = nc.tensor.matmul(o, t["ones_h"][0:3, :], b_parts[:, lo:hi], start=False, stop=True)
                last.then_inc(mm_done, 1)

            transpose(0, 0)

            def flip(r):
                pe.wait_ge(to_flip, r + 1)
                for bank in range(4):
                    for c in range(4):
                        col = bank * 4 + c
                        last = nc.tensor.transpose(ps_flip[:, bank, c * P:(c + 1) * P],
                                                   keys[0][:, col * P:(col + 1) * P].bitcast(fp32), ident[:, :])
                    last.then_inc(flipped, 1)

            pairs_and_flips(pe, body, flip)

        @block.vector
        def _(dve):
            step = Serial(dve, dve_step)
            pair = [keys[0][:, :].bitcast(fp32), keys[1][:, :].bitcast(fp32)]
            dve.wait_ge(keys_in, 64)
            dve.wait_ge(consts_set, 1)
            step(dve.tensor_scalar(keys[0][:, :], keys[0][:, :], NODE_BITS, KEY_BIAS,
                                   ALU.logical_shift_left, ALU.bitwise_or))
            step(dve.tensor_tensor(keys[0][:, :], keys[0][:, :], keys[1][:, :], ALU.bitwise_or))
            for m in range(7):
                step(dve.tensor_scalar(pbit[:, m:m + 1], pid[:, :], m, 1, ALU.logical_shift_right, ALU.bitwise_and))
            step(dve.tensor_scalar(sign[:, 0:7], pbit[:, 0:7], -2.0, 1.0, ALU.mult, ALU.add))
            step(dve.memset(sign[:, 7:8], 1.0))
            now = 0

            def exchange(distance, now):
                a, b = (z.rearrange("p (n two d) -> p n two d", two=2, d=distance) for z in (pair[now], pair[1 - now]))
                dve.tensor_tensor(b[:, :, 0, :], a[:, :, 0, :], a[:, :, 1, :], ALU.min)
                step(dve.tensor_tensor(b[:, :, 1, :], a[:, :, 0, :], a[:, :, 1, :], ALU.max))
                return 1 - now

            rounds = 0
            for k in range(1, LOGN + 1):
                z = pair[now]
                if k == 1:
                    v = z.rearrange("p (n s w) -> p n s w", s=2, w=2)[:, :, 1, :]
                    step(dve.tensor_scalar(v, v, -1.0, None, ALU.mult))
                elif k < 11:
                    v = z.rearrange("p (n s w) -> p n s w", s=4, w=1 << (k - 1))[:, :, 1:3, :]
                    step(dve.tensor_scalar(v, v, -1.0, None, ALU.mult))
                else:
                    if k == 11:
                        v = z[:, F // 2:F]
                        step(dve.tensor_scalar(v, v, -1.0, None, ALU.mult))
                    else:
                        step(dve.tensor_scalar(z, z, sign[:, k - 12:k - 11], None, ALU.mult))
                    if k < LOGN:
                        step(dve.tensor_scalar(z, z, sign[:, k - 11:k - 10], None, ALU.mult))
                if k > 11:
                    for back in range(2):
                        if now == 1:
                            step(dve.tensor_copy(pair[0], pair[1]))
                            now = 0
                        dve.sem_inc(to_flip, 1)
                        rounds += 1
                        dve.wait_ge(flip_copied, rounds)
                        if back == 0:
                            for j in range(k - 12, -1, -1):
                                now = exchange(1 << j, now)
                for j in range(min(k, 11) - 1, -1, -1):
                    now = exchange(1 << j, now)
            if now == 1:
                step(dve.tensor_copy(keys[0][:, :], keys[1][:, :]))
            dve.sem_inc(sorted_ready, 1)


def build_steps(nc, t):
    with ExitStack() as ctx:
        def sb(name, shape, dt=fp32):
            return ctx.enter_context(nc.sbuf_tensor(name, shape, dt))

        def sem(name):
            return ctx.enter_context(nc.semaphore(name))

        names = (("dst", "src", "edge_type"), ("key",))
        raw = {n: t["score"][:, k * S:(k + 1) * S].bitcast(i32).rearrange("q (c e) -> q c e", e=P)
               for k, n in enumerate(names[0] + names[1])}
        node = [raw["dst"], sb("sorted_src", [P, C, P], i32)]
        far = [raw["src"], raw["key"]]
        arrays = [[node[0], far[0], raw["edge_type"]], [node[1], far[1]]]
        last_block = sb("last_block", [P, C], i32)
        tile_end = sb("tile_end", [P, C])
        tile_id = sb("tile_id", [P, C])
        step_id = sb("step_id", [P, S])
        tile_row = sb("tile_row", [P, S])
        block_row = sb("block_row", [P, S])
        before = sb("before", [P, 2, P])
        hit = sb("hit", [P, 2, P])
        coef = sb("coef", [1, TURN])
        late = sb("late", [1, S + TURN])
        mixed = sb("mixed", [1, S + TURN])
        packed = block_row[0:1, 0:S // TURN + 1]
        ps_tile = ctx.enter_context(nc.psum_tensor("ps_tile", [P, P], fp32))
        ps_val = ctx.enter_context(nc.psum_tensor("ps_val", [P, 3, 512], fp32))
        pads_set, edges_in, pool_step, dve_step = sem("tile_pads"), sem("edges_in"), sem("pool_step2"), sem("dve_step2")
        ids_set, before_ready, tile_ready = sem("ids_set"), sem("before_ready"), sem("tile_ready")
        hit_ready, val_ready = sem("hit_ready"), sem("val_ready")
        full_c = T // P
        full_q = E // P - full_c * P
        rest = E - (full_c * P + full_q) * P
        block = ctx.enter_context(nc.Block())

        @block.sync
        def _(sp):
            sp.wait_ge(pads_set, 1)
            for n in names[0]:
                a = t[n]
                sp.dma_start(raw[n][:, 0:full_c, :], a[0:full_c * P * P].rearrange("(c q e) -> q c e", q=P, e=P)).then_inc(edges_in, 16)
                sp.dma_start(raw[n][0:full_q, full_c, :],
                             a[full_c * P * P:(full_c * P + full_q) * P].rearrange("(q e) -> q e", e=P)).then_inc(edges_in, 16)
                sp.dma_start(raw[n][full_q:full_q + 1, full_c, 0:rest],
                             a[E - rest:E].rearrange("(q e) -> q e", q=1)).then_inc(edges_in, 16)
            sp.dma_start(raw["key"][:, :, :], t["sorted_keys"][0:C * P * P].rearrange("(c q e) -> q c e", q=P, e=P))\
                .then_inc(edges_in, 16)

        @block.gpsimd
        def _(pool):
            step = Serial(pool, pool_step)
            for n, pad in zip(names[0], (PAD_NODE, 0, 0)):
                step(nc.gpsimd.memset(raw[n][:, full_c:C, :], pad))
            pool.sem_inc(pads_set, 1)
            step(nc.gpsimd.iota(step_id[:, :], [[1, S]], base=0, channel_multiplier=0,
                                allow_small_or_imprecise_dtypes=True))
            step(nc.gpsimd.iota(tile_id[:, :], [[P, C]], base=0, channel_multiplier=1,
                                allow_small_or_imprecise_dtypes=True))
            for k in range(TURN):
                step(nc.gpsimd.memset(coef[:, k:k + 1], float(P << (k - 1)) if k else 1.0))
            pool.sem_inc(ids_set, 1)

        @block.vector
        def _(dve):
            step = Serial(dve, dve_step)
            dve.wait_ge(ids_set, 1)
            dve.wait_ge(edges_in, (3 * 3 + 1) * 16)
            step(dve.tensor_scalar(node[1][:, :, :], raw["key"][:, :, :], NODE_BITS, NODE_MASK,
                                   ALU.logical_shift_right, ALU.bitwise_and))
            step(dve.tensor_scalar(raw["key"][:, :, :], raw["key"][:, :, :], NODE_MASK, None, ALU.bitwise_and))
            seen = 0
            for layer in range(2):
                step(dve.tensor_scalar(last_block[:, :], node[layer][:, :, P - 1], 7, None, ALU.logical_shift_right))
                step(dve.tensor_tensor(tile_end[:, :], last_block[:, :], tile_id[:, :], ALU.add))
                for a in arrays[layer]:
                    step(dve.tensor_copy(a[:, :, :].bitcast(fp32), a[:, :, :]))
                for c in range(C):
                    cols = slice(c * P, (c + 1) * P)
                    near = [c - 1, c] if c else [c]
                    for k, a in enumerate(near):
                        step(dve.tensor_scalar(before[:, k, :], step_id[:, cols], tile_end[:, a:a + 1], None, ALU.is_gt))
                    dve.sem_inc(before_ready, 1)
                    dve.wait_ge(tile_ready, layer * C + c + 1)
                    step(dve.tensor_scalar(tile_row[:, cols], ps_tile[:, :], float(near[0] * P), None, ALU.add))
                    for k, a in enumerate(near):
                        step(dve.tensor_scalar(hit[:, k, :], tile_row[:, cols], tile_id[:, a:a + 1], None, ALU.is_equal))
                    dve.sem_inc(hit_ready, 1)
                    step(dve.tensor_tensor(block_row[:, cols], step_id[:, cols], tile_row[:, cols], ALU.subtract))
                    dve.wait_ge(val_ready, layer * C + c + 1)
                    step(dve.scalar_tensor_tensor(t[f"local{layer}"][:, cols], block_row[:, cols], -float(P),
                                                  ps_val[:, 0, 0:P], ALU.mult, ALU.add))
                    step(dve.tensor_copy(t[f"other{layer}"][:, cols], ps_val[:, 1, 0:P]))
                    if layer == 0:
                        step(dve.tensor_copy(t["rel"][:, cols], ps_val[:, 2, 0:P]))
                step(dve.memset(late[:, 0:LAG * U], 0.0))
                step(dve.tensor_copy(late[:, LAG * U:LAG * U + S], block_row[0:1, :]))
                step(dve.tensor_scalar(late[:, LAG * U + S:S + TURN], late[:, 0:TURN - LAG * U], 0.0, float(NB - 1), ALU.mult, ALU.add))
                for blocks, into, turns in ((block_row, "packed", S // TURN), (late, "packed_late", S // TURN + 1)):
                    by_turn, m = (z[0:1, 0:turns * TURN].rearrange("p (g k) -> p g k", k=TURN) for z in (blocks, mixed))
                    step(dve.tensor_tensor(m[:, :, 1:TURN], by_turn[:, :, 1:TURN], by_turn[:, :, 0:TURN - 1], ALU.subtract))
                    step(dve.tensor_copy(m[:, :, 0], by_turn[:, :, 0]))
                    step(dve.tensor_tensor(m, m, coef[:, :].unsqueeze(1).broadcast_to([1, turns, TURN]), ALU.mult))
                    step(dve.tensor_reduce(packed[:, 0:turns], m, AX.X, ALU.add))
                    step(dve.tensor_copy(t[f"{into}{layer}"][:, 0:turns], packed[:, 0:turns]))

        @block.tensor
        def _(pe):
            for layer in range(2):
                for c in range(C):
                    near = [c - 1, c] if c else [c]
                    pe.wait_ge(before_ready, layer * C + c + 1)
                    for k in range(len(near)):
                        last = nc.tensor.matmul(ps_tile[:, :], t["ones"][:, :], before[:, k, :],
                                                start=(k == 0), stop=(k == len(near) - 1))
                    last.then_inc(tile_ready, 1)
                    pe.wait_ge(hit_ready, layer * C + c + 1)
                    for v, vals in enumerate(arrays[layer]):
                        for k, a in enumerate(near):
                            last = nc.tensor.matmul(ps_val[:, v, 0:P], vals[:, a, :].bitcast(fp32), hit[:, k, :],
                                                    start=(k == 0), stop=(k == len(near) - 1))
                    last.then_inc(val_ready, 1)


def edge_scores(nc, t, rel_w):
    with ExitStack() as ctx:
        def sb(name, shape, dt=fp32):
            return ctx.enter_context(nc.sbuf_tensor(name, shape, dt))

        def pb(name, shape, dt=fp32):
            return ctx.enter_context(nc.psum_tensor(name, shape, dt))

        def sem(name):
            return ctx.enter_context(nc.semaphore(name))

        rel_in = sb("rel_in", [R, DH])
        rel_02 = sb("rel_02", [R, DH])
        index = [sb(f"s_index{u}", [P, U], i32) for u in range(V)]
        rows = [sb(f"s_rows{u}", [P, U, D]) for u in range(V)]
        prod = sb("prod", [P, U, D])
        what = sb("what", [P, 2, S], bf16)
        minus_p = sb("minus_p", [P, 1])
        apart = [sb(f"apart{u}", [P, 2, U, P], bf16) for u in range(2)]
        hot = [sb(f"hot{u}", [P, 2, U, P]) for u in range(2)]
        ps_what = [pb(f"ps_what{u}", [P, 2, U, P], bf16) for u in range(2)]
        ps_q = [pb(f"ps_q{u}", [P, U, D]) for u in range(2)]
        ps_rel = [pb(f"ps_rel{u}", [P, U, DH]) for u in range(2)]
        weights_in, rel_ready = sem("rel_in_sem"), sem("rel_ready")
        index_ready, rows_in, rows_used = sem("s_index_ready"), [sem(f"s_rows_in{u}") for u in range(V)], sem("s_rows_used")
        what_ready, minus_ready, turned, apart_ready, hot_ready = (sem(f"s_{n}") for n in ("what_ready", "minus_ready", "turned", "apart_ready", "hot_ready"))
        picked, picked_used, scored = sem("s_picked"), sem("s_picked_used"), sem("s_scored")
        pool_turn = sem("s_pool_turn")
        block = ctx.enter_context(nc.Block())

        @block.sync
        def _(sp):
            sp.dma_start(rel_in[:, :], rel_w).then_inc(weights_in, 16)

        @block.gpsimd
        def _(pool):
            nc.gpsimd.iota(minus_p[:, :], [[1, 1]], base=0, channel_multiplier=-1,
                           allow_small_or_imprecise_dtypes=True).then_inc(minus_ready, 1)

            def turn(i):
                for u in range(V):
                    g = V * i + u
                    pool.wait_ge(index_ready, g + 1)
                    if not early(i, 1):
                        pool.wait_ge(rows_used, g - V + 1)
                    pool.sem_inc(pool_turn, 1)
                    for k in range(U):
                        pool.indirect_dma_start(out=rows[u][:, k, :], out_offset=None, in_=t["k_rows"],
                                                in_offset=bass.IndirectOffsetOnAxis(ap=index[u][:, k:k + 1], axis=0))\
                            .then_inc(rows_in[u], 16)

            group_turns(pool, turn)

        @block.scalar
        def _(act):
            def set_index(g, u, i):
                if not early(i, 1):
                    act.wait_ge(rows_in[u], 16 * U * i)
                nc.scalar.copy(index[u][:, :], t["other0"][:, bass.ds(g * U, U)]).then_inc(index_ready, 1)

            for g in range(AHEAD):
                set_index(g, g, 0)

            act.wait_ge(weights_in, 16)
            nc.scalar.mul(rel_02[:, :], rel_in[:, :], 0.2).then_inc(rel_ready, 1)

            def turn(i):
                for u in range(V):
                    g = V * i + u
                    if not (isinstance(g, int) and g + AHEAD >= G):
                        set_index(g + AHEAD, (u + AHEAD) % V, i + (u + AHEAD) // V)
                    act.wait_ge(turned, g + 1)
                    nc.scalar.activation(apart[u % 2][:, :, :, :], ps_what[u % 2][:, :, :, :], ACT.Abs,
                                         bias=minus_p[:, 0:1]).then_inc(apart_ready, 1)
                    act.wait_ge(apart_ready, g + 1)
                    if not early(g):
                        act.wait_ge(picked, g - 1)
                    nc.scalar.activation(hot[u % 2][:, :, :, :], apart[u % 2][:, :, :, :], ACT.Relu,
                                         scale=-1.0, bias=t["ones"][:, 0:1]).then_inc(hot_ready, 1)

            act.wait_ge(minus_ready, 1)
            group_turns(act, turn)

        @block.vector
        def _(dve):
            def work(g, u, i):
                by_head = rows[u][:, :, :].rearrange("p k (h d) -> p k h d", h=H)
                dve.wait_ge(picked, g + 1)
                dve.wait_ge(rows_in[u], 16 * U * (i + 1))
                if not (isinstance(g, int) and g == 0):
                    dve.wait_ge(scored, g)
                dve.tensor_tensor(prod[:, :, :].rearrange("p k (h d) -> p k h d", h=H), by_head,
                                  ps_rel[u % 2][:, :, :].unsqueeze(2).broadcast_to([P, U, H, DH]), ALU.add).then_inc(rows_used, 1)
                dve.wait_ge(rows_used, g + 1)
                dve.tensor_tensor(prod[:, :, :], prod[:, :, :], ps_q[u % 2][:, :, :], ALU.mult).then_inc(picked_used, 1)
                dve.wait_ge(picked_used, g + 1)
                dve.tensor_reduce(t["score"][:, bass.ds(g * U * H, U * H)],
                                  prod[:, :, :].rearrange("p k (h d) -> p (k h) d", h=H), AX.X, ALU.add).then_inc(scored, 1)

            def turn(i):
                for u in range(V):
                    g = V * i + u
                    work(g, u, i)

            dve.tensor_scalar(what[:, 0, :], t["local0"][:, :], -1.0, float(P), ALU.max, ALU.min)
            dve.tensor_copy(what[:, 1, :], t["rel"][:, :]).then_inc(what_ready, 1)
            group_turns(dve, turn)
            dve.wait_ge(scored, G)

        @block.tensor
        def _(pe):
            def spread(g, u):
                if not early(g):
                    pe.wait_ge(apart_ready, g - 1)
                for n in range(2):
                    for k in range(U):
                        number = what[:, n, bass.ds(g * U + k, 1)].broadcast_to([P, P])
                        last = nc.tensor.transpose(ps_what[u % 2][:, n, k, :], number, t["ident_h"][:, :])
                last.then_inc(turned, 1)

            def turn(i):
                places = places_of(pe, t["packed0"], i, AW)
                for u in range(V):
                    g = V * i + u
                    if not (isinstance(g, int) and g == G - 1):
                        spread(g + 1, u + 1)
                    pe.wait_ge(hot_ready, g + 1)
                    if not early(g):
                        pe.wait_ge(picked_used, g - 1)
                    for k in range(U):
                        nc.tensor.matmul(ps_rel[u % 2][:, k, :], hot[u % 2][0:R, 1, k, :], rel_02[:, :], start=True, stop=True)
                    for k in range(U):
                        last = nc.tensor.matmul(ps_q[u % 2][:, k, :], hot[u % 2][:, 0, k, :],
                                                t["node_tab"][:, bass.ds(places[u * U + k], D)], start=True, stop=True)
                    last.then_inc(picked, 1)

            pe.wait_ge(rel_ready, 1)
            pe.wait_ge(what_ready, 1)
            spread(0, 0)
            group_turns(pe, turn)


def softmax_numerators(nc, t):
    with ExitStack() as ctx:
        def sb(name, shape, dt=fp32):
            return ctx.enter_context(nc.sbuf_tensor(name, shape, dt))

        def sem(name):
            return ctx.enter_context(nc.semaphore(name))

        W = S * H
        tab = t["node_tab"]
        y, fwd, bwd = tab[:, 0:W], tab[:, W:2 * W], tab[:, 2 * W:3 * W]
        loc, valid, pen = (tab[:, 3 * W + k * S:3 * W + (k + 1) * S] for k in range(3))
        score = t["score"]

        def by_edge(v):
            return v.rearrange("q (c e) -> q c e", e=P)

        def by_head(v):
            return v.rearrange("q (c h e) -> q c h e", h=H, e=P)

        def all_heads(v):
            return by_edge(v).unsqueeze(2).broadcast_to([P, C, H, P])

        restart = sb("restart", [P, W + 1])
        ends = sb("ends", [P, 4, C, H])
        rows = [score[0:H, k * S:(k + 1) * S] for k in range(4)]
        cont = sb("cont", [H, S + 1])
        reach = t["rel"][0:H, :]
        carry = [restart[0:H, k * S:(k + 1) * S] for k in range(2)]
        carry_in = sb("carry_in", [P, 2, C, H])
        ps_y = [ctx.enter_context(nc.psum_tensor(f"ps_y{u}", [P, H, P], fp32)) for u in range(2)]
        ps_rows = ctx.enter_context(nc.psum_tensor("ps_rows", [P, 4 * 512], fp32))
        ps_carry = ctx.enter_context(nc.psum_tensor("ps_carry", [P, 2, C, H], fp32))
        y_turned, y_copied, loc_turned, loc_copied = sem("y_turned"), sem("y_copied"), sem("loc_turned"), sem("loc_copied")
        ends_ready, ends_turned, ends_copied = sem("ends_ready"), sem("ends_turned"), sem("ends_copied")
        carry_ready, carry_turned = sem("carry_ready"), sem("carry_turned")
        less_max, exp_done, w_turned, w_copied = sem("less_max"), sem("exp_done"), sem("w_turned"), sem("w_copied")
        dve_step = sem("dve_step4")
        block = ctx.enter_context(nc.Block())

        @block.tensor
        def _(pe):
            ident = t["ident"]
            for c in range(C):
                last = nc.tensor.transpose(ps_rows[:, c * P:(c + 1) * P], t["local0"][:, c * P:(c + 1) * P], ident[:, :])
            last.then_inc(loc_turned, 1)
            for c in range(C):
                if c >= 2:
                    pe.wait_ge(y_copied, c - 1)
                s = score[:, c * P * H:(c + 1) * P * H].rearrange("p (s h) -> p h s", h=H)
                for h in range(H):
                    last = nc.tensor.transpose(ps_y[c % 2][:, h, :], s[:, h, :], ident[:, :])
                last.then_inc(y_turned, 1)
            pe.wait_ge(ends_ready, 1)
            pe.wait_ge(loc_copied, 1)
            for k in range(4):
                if k:
                    pe.wait_ge(ends_copied, k)
                for c in range(C):
                    last = nc.tensor.transpose(ps_rows[0:H, c * P:(c + 1) * P], ends[:, k, c, :], ident[:, :])
                last.then_inc(ends_turned, 1)
            pe.wait_ge(carry_ready, 1)
            for k in range(2):
                for c in range(C):
                    last = nc.tensor.transpose(ps_carry[:, k, c, :], carry[k][:, c * P:(c + 1) * P], ident[0:H, 0:H])
            last.then_inc(carry_turned, 1)
            pe.wait_ge(exp_done, 1)
            for c in range(C):
                if c >= 2:
                    pe.wait_ge(w_copied, c - 1)
                for h in range(H):
                    last = nc.tensor.transpose(ps_y[c % 2][:, h, :], by_head(y)[:, c, h, :], ident[:, :])
                last.then_inc(w_turned, 1)

        @block.scalar
        def _(act):
            act.wait_ge(loc_turned, 1)
            nc.scalar.copy(loc, ps_rows[:, 0:S]).then_inc(loc_copied, 1)
            for c in range(C):
                act.wait_ge(y_turned, c + 1)
                nc.scalar.copy(by_head(y)[:, c, :, :], ps_y[c % 2][:, :, :]).then_inc(y_copied, 1)
            for k in range(4):
                act.wait_ge(ends_turned, k + 1)
                nc.scalar.copy(rows[k], ps_rows[0:H, 0:S]).then_inc(ends_copied, 1)
            act.wait_ge(less_max, 1)
            nc.scalar.activation(y, y, ACT.Exp).then_inc(exp_done, 1)
            for c in range(C):
                act.wait_ge(w_turned, c + 1)
                nc.scalar.copy(score[:, c * P * H:(c + 1) * P * H].rearrange("p (s h) -> p h s", h=H), ps_y[c % 2][:, :, :])\
                    .then_inc(w_copied, 1)
            act.wait_ge(w_copied, C)

        @block.vector
        def _(dve):
            step = Serial(dve, dve_step)
            dve.wait_ge(loc_copied, 1)
            step(dve.tensor_scalar(valid, loc, 0.0, None, ALU.is_ge))
            step(dve.scalar_tensor_tensor(valid, loc, float(P - 1), valid, ALU.is_le, ALU.mult))
            step(dve.tensor_scalar(pen, valid, 1.0, -LOWEST, ALU.subtract, ALU.mult))
            dve.wait_ge(y_copied, C)
            step(dve.tensor_tensor(by_head(y), by_head(y), all_heads(pen), ALU.add))
            step(dve.memset(restart[:, :], LOWEST))
            other = by_edge(loc)
            step(dve.tensor_tensor(by_edge(pen)[:, :, 1:P], other[:, :, 1:P], other[:, :, 0:P - 1], ALU.not_equal))
            step(dve.tensor_scalar(by_head(restart[:, 0:W])[:, :, :, 1:P],
                                   by_edge(pen)[:, :, 1:P].unsqueeze(2).broadcast_to([P, C, H, P - 1]), LOWEST, None, ALU.mult))
            step(dve.tensor_tensor_scan(fwd, restart[:, 0:W], y, LOWEST, ALU.add, ALU.max))
            step(dve.tensor_tensor_scan(bwd[:, ::-1], restart[:, W:0:-1], y[:, ::-1], LOWEST, ALU.add, ALU.max))
            step(dve.tensor_copy(ends[:, 0, :, :], by_head(fwd)[:, :, :, P - 1]))
            step(dve.tensor_copy(ends[:, 1, :, :], by_head(bwd)[:, :, :, 0]))
            for k, edge, none in ((2, P - 1, 2.0), (3, 0, 1.0)):
                shape = [P, C, H]
                at = by_edge(loc)[:, :, edge:edge + 1].broadcast_to(shape)
                step(dve.tensor_scalar(ends[:, k, :, :], at, none, None, ALU.add))
                step(dve.tensor_tensor(ends[:, k, :, :], ends[:, k, :, :], by_edge(valid)[:, :, edge:edge + 1].broadcast_to(shape), ALU.mult))
                step(dve.tensor_scalar(ends[:, k, :, :], ends[:, k, :, :], none, None, ALU.subtract))
            dve.sem_inc(ends_ready, 1)
            dve.wait_ge(ends_copied, 4)
            leave_end, leave_start, last_node, first_node = rows
            step(dve.memset(cont[:, :], 0.0))
            step(dve.tensor_tensor(cont[:, 1:S], first_node[:, 1:S], last_node[:, 0:S - 1], ALU.is_equal))
            step(dve.tensor_tensor(first_node[:, :], first_node[:, :], last_node[:, :], ALU.is_equal))
            for k, shift in ((0, 0), (1, 1)):
                step(dve.tensor_tensor(reach[:, :], first_node[:, :], cont[:, shift:shift + S], ALU.mult))
                step(dve.tensor_scalar(reach[:, :], reach[:, :], 1.0, -LOWEST, ALU.subtract, ALU.mult))
                if k == 0:
                    step(dve.tensor_tensor_scan(leave_end[:, :], reach[:, :], leave_end[:, :], LOWEST, ALU.add, ALU.max))
                else:
                    step(dve.tensor_tensor_scan(leave_start[:, ::-1], reach[:, ::-1], leave_start[:, ::-1], LOWEST, ALU.add, ALU.max))
            step(dve.tensor_scalar(cont[:, :], cont[:, :], 1.0, -LOWEST, ALU.subtract, ALU.mult))
            step(dve.memset(carry[0][:, 0:1], LOWEST))
            step(dve.memset(carry[1][:, S - 1:S], LOWEST))
            step(dve.tensor_tensor(carry[0][:, 1:S], leave_end[:, 0:S - 1], cont[:, 1:S], ALU.add))
            step(dve.tensor_tensor(carry[1][:, 0:S - 1], leave_start[:, 1:S], cont[:, 1:S], ALU.add))
            dve.sem_inc(carry_ready, 1)
            step(dve.tensor_tensor(fwd, fwd, bwd, ALU.max))
            dve.wait_ge(carry_turned, 1)
            step(dve.tensor_copy(carry_in[:, :, :, :], ps_carry[:, :, :, :]))
            for k, edge in ((0, 0), (1, P - 1)):
                step(dve.tensor_tensor(by_edge(pen), by_edge(loc), by_edge(loc)[:, :, edge:edge + 1].broadcast_to([P, C, P]), ALU.is_equal))
                step(dve.tensor_scalar(pen, pen, 1.0, -LOWEST, ALU.subtract, ALU.mult))
                step(dve.tensor_tensor(by_head(bwd), all_heads(pen), carry_in[:, k, :, :].unsqueeze(3).broadcast_to([P, C, H, P]), ALU.add))
                step(dve.tensor_tensor(fwd, fwd, bwd, ALU.max))
            step(dve.tensor_tensor(y, y, fwd, ALU.subtract))
            dve.sem_inc(less_max, 1)


def aggregate(nc, t):
    with ExitStack() as ctx:
        def sb(name, shape, dt=fp32):
            return ctx.enter_context(nc.sbuf_tensor(name, shape, dt))

        def sem(name):
            return ctx.enter_context(nc.semaphore(name))

        tab = t["node_tab"]
        index = [sb(f"a_index{u}", [P, U], i32) for u in range(V)]
        rows = [sb(f"a_rows{u}", [P, U, D]) for u in range(V)]
        hot = [sb(f"a_hot{u}", [P, U, P]) for u in range(2)]
        terms = [sb(f"a_terms{u}", [P, U, AW]) for u in range(2)]
        ps_sum = [ctx.enter_context(nc.psum_tensor(f"ps_sum{u}", [P, U, 512], fp32)) for u in range(2)]
        index_ready, rows_in, rows_used = sem("a_index_ready"), [sem(f"a_rows_in{u}") for u in range(V)], sem("a_rows_used")
        hot_ready, weights_ready, summed, added = sem("a_hot_ready"), sem("a_weights_ready"), sem("a_summed"), sem("a_added")
        pool_turn, cleared = sem("a_pool_turn"), sem("a_cleared")
        block = ctx.enter_context(nc.Block())

        @block.gpsimd
        def _(pool):
            def turn(i):
                for u in range(V):
                    g = V * i + u
                    pool.wait_ge(index_ready, g + 1)
                    if not early(i, 1):
                        pool.wait_ge(rows_used, g - V + 1)
                    pool.sem_inc(pool_turn, 1)
                    for k in range(U):
                        pool.indirect_dma_start(out=rows[u][:, k, :], out_offset=None, in_=t["v_rows"],
                                                in_offset=bass.IndirectOffsetOnAxis(ap=index[u][:, k:k + 1], axis=0))\
                            .then_inc(rows_in[u], 16)

            group_turns(pool, turn)

        @block.scalar
        def _(act):
            def set_index(g, u, i):
                if not early(i, 1):
                    act.wait_ge(rows_in[u], 16 * U * i)
                nc.scalar.copy(index[u][:, :], t["other0"][:, bass.ds(g * U, U)]).then_inc(index_ready, 1)

            for g in range(AHEAD):
                set_index(g, g, 0)

            def turn(i):
                for u in range(V):
                    g = V * i + u
                    if not (isinstance(g, int) and g + AHEAD >= G):
                        set_index(g + AHEAD, (u + AHEAD) % V, i + (u + AHEAD) // V)
                    if not early(g):
                        act.wait_ge(summed, g - 1)
                    nc.scalar.copy(terms[u % 2][:, :, D:AW],
                                   t["score"][:, bass.ds(g * U * H, U * H)].rearrange("p (k h) -> p k h", h=H))\
                        .then_inc(weights_ready, 1)

            group_turns(act, turn)

        @block.vector
        def _(dve):
            def weigh(g, u, i):
                if not early(g):
                    dve.wait_ge(summed, g - 1)
                local = t["local0"][:, bass.ds(g * U, U)].unsqueeze(2).broadcast_to([P, U, P])
                dve.tensor_tensor(hot[u % 2][:, :, :], t["iota"][:, :].unsqueeze(1).broadcast_to([P, U, P]), local, ALU.is_equal)\
                    .then_inc(hot_ready, 1)
                dve.wait_ge(rows_in[u], 16 * U * (i + 1))
                weight = t["score"][:, bass.ds(g * U * H, U * H)].rearrange("p (k h) -> p k h", h=H)
                dve.tensor_tensor(terms[u % 2][:, :, 0:D].rearrange("p k (h d) -> p k h d", h=H),
                                  rows[u][:, :, :].rearrange("p k (h d) -> p k h d", h=H),
                                  weight.unsqueeze(3).broadcast_to([P, U, H, DH]), ALU.mult).then_inc(rows_used, 1)

            def add(g, u, places):
                for k in range(U):
                    dve.compute_val(places[k])
                dve.wait_ge(summed, g + 1)
                for k in range(U):
                    acc = tab[:, bass.ds(places[k], AW)]
                    if not (isinstance(g, int) and g == 0 and k == 0):
                        dve.wait_ge(added, g * U + k)
                    dve.tensor_tensor(acc, acc, ps_sum[u % 2][:, k, 0:AW], ALU.add).then_inc(added, 1)

            def turn(i):
                places = places_of(dve, t["packed_late0"], i, AW)
                for u in range(V):
                    g = V * i + u
                    if not early(g, LAG):
                        add(g - LAG, u - LAG, places[u * U:])
                    weigh(g, u, i)

            dve.memset(tab[:, :], 0.0).then_inc(cleared, 1)
            dve.wait_ge(cleared, 1)
            group_turns(dve, turn)
            places = places_of(dve, t["packed_late0"], G // V, AW)
            for k in range(LAG):
                add(G - LAG + k, k, places[k * U:])
            dve.wait_ge(added, G * U)

        @block.tensor
        def _(pe):
            def turn(i):
                for u in range(V):
                    g = V * i + u
                    pe.wait_ge(hot_ready, g + 1)
                    pe.wait_ge(weights_ready, g + 1)
                    pe.wait_ge(rows_used, g + 1)
                    if not early(g):
                        pe.wait_ge(added, (g - 1) * U)
                    for k in range(U):
                        last = nc.tensor.matmul(ps_sum[u % 2][:, k, 0:AW], hot[u % 2][:, k, :], terms[u % 2][:, k, :],
                                                start=True, stop=True)
                    last.then_inc(summed, 1)

            group_turns(pe, turn)


def update_nodes(nc, t, wo, bo, gamma, beta, w1, b1, w2, b2, wa1, ba1, wa2, ba2):
    with ExitStack() as ctx:
        def sb(name, shape, dt=fp32):
            return ctx.enter_context(nc.sbuf_tensor(name, shape, dt))

        def ring(name, shape):
            return [sb(f"{name}{u}", shape) for u in range(4)]

        def pb(name, shape):
            return ctx.enter_context(nc.psum_tensor(name, shape, fp32))

        def sem(name):
            return ctx.enter_context(nc.semaphore(name))

        tab, ident, ones_h = t["node_tab"], t["ident"], t["ones_h"]
        w_o, w_12 = sb("w_o", [P, 2, D]), sb("w_12", [P, 2, 2 * D])
        wide = {n: sb(f"wide_{n}", [P, D]) for n in ("gamma", "beta", "wa1", "wa2")}
        ba = sb("ba", [P, 2])
        b_row, b_rest = (t["rel"][0:3 * D // P, P * k:P * (k + 1)] for k in range(2))
        b_part = [t["local0"][0:3 * D // P, :].bitcast(bf16)[:, P * k:P * (k + 1)] for k in range(3)]
        b_parts = sb("b_parts6", [3, 3 * D], bf16)
        x_in, v_in, xj = ring("n_x", [P, D]), ring("n_v", [P, D]), ring("n_xj", [P, XW])
        msg, y, z, x1 = ([t["score"][:, (4 * k + u) * D:(4 * k + u + 1) * D] for u in range(4)] for k in range(4))
        msg_t, x1_t = ring("n_msg_t", [P, 2, P]), ring("n_x1_t", [P, 2, P])
        h02, small = ring("n_h02", [P, 2 * D]), ring("n_small", [P, 48])
        junk, eps = sb("junk", [P, D]), sb("n_eps", [P, 1])
        ps_t = [pb(f"ps_t{k}", [P, 2, P]) for k in range(2)]
        ps_o = [pb(f"ps_o{k}", [P, D]) for k in range(2)]
        ps_h = [pb(f"ps_h{k}", [P, 2 * D]) for k in range(2)]
        weights_in, v_loaded, x_loaded = sem("n_weights_in"), [sem(f"n_v_loaded{u}") for u in range(4)], [sem(f"n_x_loaded{u}") for u in range(4)]
        msg_ready, msg_turned, msg_t_ready, o_ready = sem("msg_ready"), sem("msg_turned"), sem("msg_t_ready"), sem("o_ready")
        var_ready, std_ready, scale_ready, normed = ([sem(f"{n}{k}") for k in range(2)] for n in ("var_ready", "std_ready", "scale_ready", "normed"))
        z_ready, x1_turned, x1_t_ready, h_ready = sem("z_ready"), sem("x1_turned"), sem("x1_t_ready"), sem("h_ready")
        h02_ready, xj_ready, pads_set = sem("h02_ready"), sem("xj_ready"), sem("xj_pads_set")
        x1_stored, xj_stored = [sem(f"x1_stored{u}") for u in range(4)], [sem(f"xj_stored{u}") for u in range(4)]
        dve_step, pool_step = sem("dve_step6"), sem("pool_step6")
        dve_turn, b_parts_in = sem("n_turn"), sem("n_b_parts_in")
        block = ctx.enter_context(nc.Block())

        @block.sync
        def _(sp):
            sp.dma_start(w_o[:, :, :], wo.rearrange("(c p) n -> p c n", p=P)).then_inc(weights_in, 16)
            for k, (w, b) in enumerate(((w1, b1), (w2, b2))):
                sp.dma_start(w_12[:, :, k * D:(k + 1) * D], w.rearrange("(c p) n -> p c n", p=P)).then_inc(weights_in, 16)
                sp.dma_start(b_row[2 * k + 2:2 * k + 4, :], b.rearrange("(a n) -> a n", n=P)).then_inc(weights_in, 16)
            sp.dma_start(b_row[0:2, :], bo.rearrange("(a n) -> a n", n=P)).then_inc(weights_in, 16)
            for n, a in (("gamma", gamma), ("beta", beta), ("wa1", wa1), ("wa2", wa2)):
                sp.dma_start(wide[n][:, :], a.partition_broadcast(P)).then_inc(weights_in, 16)
            for k, a in enumerate((ba1, ba2)):
                sp.dma_start(ba[:, k:k + 1], a.partition_broadcast(P)).then_inc(weights_in, 16)

            def load_v(b, s):
                if not early(b, 4):
                    sp.wait_ge(msg_ready, b - 3)
                r = rows_of(b)
                sp.dma_start(v_in[s][0:r, :], t["v_rows"][bass.ds(b * P, r), :]).then_inc(v_loaded[s], 16)

            def load_x(b, s):
                if not early(b, 4):
                    sp.wait_ge(z_ready, b - 3)
                r = rows_of(b)
                sp.dma_start(x_in[s][0:r, :], t["x"][bass.ds(b * P, r), :]).then_inc(x_loaded[s], 16)

            def store_x1(b, s):
                r = rows_of(b)
                sp.wait_ge(normed[1], b + 1)
                sp.dma_start(t["x1_rows"][bass.ds(b * P, r), :], x1[s][0:r, :]).then_inc(x1_stored[s], 16)

            def store_xj(b, s):
                r = rows_of(b)
                sp.wait_ge(xj_ready, b + 1)
                sp.dma_start(t["xj_rows"][bass.ds(b * P, r), :], xj[s][0:r, :]).then_inc(xj_stored[s], 16)

            skewed(sp, [(0, load_v), (1, load_x), (6, store_x1), (9, store_xj)])
            for s in range(4):
                uses = len(range(s, NB, 4))
                sp.wait_ge(x1_stored[s], 16 * uses)
                sp.wait_ge(xj_stored[s], 16 * uses)

        @block.gpsimd
        def _(pool):
            step = Serial(pool, pool_step, 4 * 2)
            for s in range(4):
                nc.gpsimd.memset(xj[s][:, D:XW], 0.0).then_inc(pads_set, 1)
            nc.gpsimd.memset(eps[:, :], EPS).then_inc(pads_set, 1)
            pool.wait_ge(weights_in, 12 * 16)
            split_exactly(nc.gpsimd, step, b_row, b_part, b_rest)
            for k in range(3):
                pool.dma_start(b_parts[k:k + 1, :], b_part[k]).then_inc(b_parts_in, 16)

            def affine(b, s):
                pool.wait_ge(normed[0], b + 1)
                step(nc.gpsimd.tensor_tensor(z[s][:, :], y[s][:, :], wide["gamma"][:, :], ALU.mult))
                step(nc.gpsimd.tensor_tensor(z[s][:, :], z[s][:, :], wide["beta"][:, :], ALU.add))
                nc.gpsimd.tensor_tensor(z[s][:, :], z[s][:, :], x_in[s][:, :], ALU.add).then_inc(z_ready, 1)

            skewed(pool, [(4, affine)], step)

        @block.scalar
        def _(act):
            act.wait_ge(pads_set, 5)

            def sqrt(k):
                def f(b, s):
                    act.wait_ge(var_ready[k], b + 1)
                    nc.scalar.activation(small[s][:, 16 + k:17 + k], small[s][:, 9 + 2 * k:10 + 2 * k], ACT.Sqrt, bias=eps[:, 0:1]).then_inc(std_ready[k], 1)
                return f

            def normalise(k):
                def f(b, s):
                    act.wait_ge(scale_ready[k], b + 1)
                    src, dst = ((y, y), (z, x1))[k]
                    if k and not early(b, 4):
                        act.wait_ge(x1_stored[s], (b - s) * 4)
                    if k and not early(b, 4):
                        act.wait_ge(x1_turned, b - 3)
                    nc.scalar.activation(dst[s][:, :], src[s][:, :], ACT.Identity, scale=small[s][:, 20 + 2 * k:21 + 2 * k],
                                         bias=small[s][:, 21 + 2 * k:22 + 2 * k]).then_inc(normed[k], 1)
                return f

            def copy_x1_t(b, s):
                act.wait_ge(x1_turned, b + 1)
                nc.scalar.copy(x1_t[s][:, :, :], ps_t[1][:, :, :]).then_inc(x1_t_ready, 1)

            def copy_msg_t(b, s):
                act.wait_ge(msg_turned, b + 1)
                nc.scalar.copy(msg_t[s][:, :, :], ps_t[0][:, :, :]).then_inc(msg_t_ready, 1)

            def fifth(b, s):
                act.wait_ge(h_ready, b + 1)
                nc.scalar.activation(h02[s][:, :], ps_h[s % 2][:, :], ACT.Copy, scale=0.2).then_inc(h02_ready, 1)

            skewed(act, [(2, copy_msg_t), (4, sqrt(0)), (8, fifth), (4, normalise(0)), (6, copy_x1_t), (5, sqrt(1)), (5, normalise(1))])

        @block.tensor
        def _(pe):
            pe.wait_ge(weights_in, 12 * 16)
            pe.wait_ge(b_parts_in, 3 * 16)

            def turn_x1(b, s):
                pe.wait_ge(normed[1], b + 1)
                if not early(b, 1):
                    pe.wait_ge(x1_t_ready, b)
                for c in range(2):
                    last = nc.tensor.transpose(ps_t[1][:, c, :], x1[s][:, c * P:(c + 1) * P], ident[:, :])
                last.then_inc(x1_turned, 1)

            def turn_msg(b, s):
                pe.wait_ge(msg_ready, b + 1)
                if not early(b, 1):
                    pe.wait_ge(msg_t_ready, b)
                for c in range(2):
                    last = nc.tensor.transpose(ps_t[0][:, c, :], msg[s][:, c * P:(c + 1) * P], ident[:, :])
                last.then_inc(msg_turned, 1)

            def project_x1(b, s):
                pe.wait_ge(x1_t_ready, b + 1)
                if not early(b):
                    pe.wait_ge(xj_ready, b - 1)
                for c in range(2):
                    nc.tensor.matmul(ps_h[s % 2][:, :], x1_t[s][:, c, :], w_12[:, c, :], start=(c == 0), stop=False)
                nc.tensor.matmul(ps_h[s % 2][:, :], ones_h[0:3, :], b_parts[:, D:3 * D], start=False, stop=True).then_inc(h_ready, 1)

            def project_msg(b, s):
                pe.wait_ge(msg_t_ready, b + 1)
                if not early(b):
                    pe.wait_ge(var_ready[0], b - 1)
                for c in range(2):
                    nc.tensor.matmul(ps_o[s % 2][:, :], msg_t[s][:, c, :], w_o[:, c, :], start=(c == 0), stop=False)
                nc.tensor.matmul(ps_o[s % 2][:, :], ones_h[0:3, :], b_parts[:, 0:D], start=False, stop=True).then_inc(o_ready, 1)

            skewed(pe, [(2, turn_msg), (3, project_msg), (6, turn_x1), (7, project_x1)])

        @block.vector
        def _(dve):
            step = Serial(dve, dve_step, 4 * 10)
            dve.wait_ge(weights_in, 12 * 16)
            dve.wait_ge(pads_set, 5)

            def stats(k):
                def f(b, s):
                    v, m = (y, z)[k][s], small[s]
                    if k == 0:
                        dve.wait_ge(o_ready, b + 1)
                        dve.wait_ge(x_loaded[s], (b - s) * 4 + 16 if not isinstance(b, int) else 16 * (b // 4 + 1))
                        step(dve.tensor_tensor(v[:, :], ps_o[s % 2][:, :], x_in[s][:, :], ALU.add))
                    else:
                        dve.wait_ge(z_ready, b + 1)
                    step(dve.bn_stats(m[:, 24:30], v[:, :]))
                    dve.sem_inc(dve_turn, 1)
                    dve.bn_aggr(m[:, 8 + 2 * k:10 + 2 * k], m[:, 24:30]).then_inc(var_ready[k], 1)
                return f

            def scale(k):
                def f(b, s):
                    m = small[s]
                    dve.wait_ge(std_ready[k], b + 1)
                    step(dve.reciprocal(m[:, 20 + 2 * k:21 + 2 * k], m[:, 16 + k:17 + k]))
                    dve.scalar_tensor_tensor(m[:, 21 + 2 * k:22 + 2 * k], m[:, 8 + 2 * k:9 + 2 * k], -1.0, m[:, 20 + 2 * k:21 + 2 * k],
                                             ALU.mult, ALU.mult).then_inc(scale_ready[k], 1)
                return f

            def message(b, s):
                m, acc = small[s], tab[:, bass.ds(b * AW, D)]
                den = tab[:, bass.ds(b * AW + D, H)]
                dve.wait_ge(v_loaded[s], (b - s) * 4 + 16 if not isinstance(b, int) else 16 * (b // 4 + 1))
                dve.tensor_scalar(m[:, 0:H], den, 0.0, None, ALU.is_equal)
                step(dve.tensor_scalar(m[:, H:2 * H], den, 0.5, None, ALU.max))
                step(dve.reciprocal(m[:, H:2 * H], m[:, H:2 * H]))
                step(dve.tensor_tensor(msg[s][:, :].rearrange("p (h d) -> p h d", h=H), acc.rearrange("p (h d) -> p h d", h=H),
                                       m[:, H:2 * H].unsqueeze(2).broadcast_to([P, H, DH]), ALU.mult))
                dve.scalar_tensor_tensor(msg[s][:, :], v_in[s][:, :], m[:, 0:1], msg[s][:, :], ALU.mult, ALU.add).then_inc(msg_ready, 1)

            def scores(b, s):
                dve.wait_ge(h02_ready, b + 1)
                if not early(b, 4):
                    dve.wait_ge(xj_stored[s], (b - s) * 4 if not isinstance(b, int) else 16 * (b // 4))
                dve.tensor_tensor(h02[s][:, 0:D], ps_h[s % 2][:, 0:D], h02[s][:, 0:D], ALU.max)
                step(dve.tensor_tensor(xj[s][:, 0:D], ps_h[s % 2][:, D:2 * D], h02[s][:, D:2 * D], ALU.max))
                dve.tensor_tensor_reduce(junk[:, :], h02[s][:, 0:D], wide["wa1"][:, :], 1.0, 0.0, ALU.mult, ALU.add, small[s][:, 32:33])
                step(dve.tensor_tensor_reduce(h02[s][:, D:2 * D], xj[s][:, 0:D], wide["wa2"][:, :], 1.0, 0.0, ALU.mult, ALU.add, small[s][:, 33:34]))
                dve.tensor_tensor(t["a1_tab"][:, bass.ds(b, 1)], small[s][:, 32:33], ba[:, 0:1], ALU.add)
                dve.tensor_tensor(xj[s][:, D:D + 1], small[s][:, 33:34], ba[:, 1:2], ALU.add).then_inc(xj_ready, 1)

            skewed(dve, [(4, stats(0)), (1, message), (4, scale(0)), (5, stats(1)), (8, scores), (5, scale(1))], step)
            dve.wait_ge(xj_ready, NB)


def attend(nc, t):
    with ExitStack() as ctx:
        def sb(name, shape, dt=fp32):
            return ctx.enter_context(nc.sbuf_tensor(name, shape, dt))

        def sem(name):
            return ctx.enter_context(nc.semaphore(name))

        tab = t["node_tab"]
        index = [sb(f"t_index{u}", [P, U], i32) for u in range(V)]
        rows = [sb(f"t_rows{u}", [P, U, XW]) for u in range(V)]
        hot = [sb(f"t_hot{u}", [P, U, P]) for u in range(4)]
        node_hot = [sb(f"t_node_hot{u}", [P, U, P]) for u in range(2)]
        hot_att = [sb(f"t_hot_att{u}", [P, U, P]) for u in range(2)]
        logit = [sb(f"t_logit{u}", [P, U]) for u in range(2)]
        att = [sb(f"t_att{u}", [P, U]) for u in range(2)]
        ps_hot = ctx.enter_context(nc.psum_tensor("ps_hot", [P, U, P], fp32))
        ps_a1 = [ctx.enter_context(nc.psum_tensor(f"ps_a1{u}", [P, U], fp32)) for u in range(2)]
        ps_sum = [ctx.enter_context(nc.psum_tensor(f"ps_xsum{u}", [P, U, D], fp32)) for u in range(2)]
        index_ready, rows_in = sem("t_index_ready"), [sem(f"t_rows_in{u}") for u in range(V)]
        hot_ready, turned, turned_copied, a1_ready = sem("t_hot_ready"), sem("t_turned"), sem("t_turned_copied"), sem("t_a1_ready")
        logit_ready, att_ready, hot_att_ready, summed, added = sem("logit_ready"), sem("att_ready"), sem("hot_att_ready"), sem("t_summed"), sem("t_added")
        pool_turn, cleared = sem("t_pool_turn"), sem("t_cleared")
        block = ctx.enter_context(nc.Block())

        @block.gpsimd
        def _(pool):
            def turn(i):
                for u in range(V):
                    g = V * i + u
                    pool.wait_ge(index_ready, g + 1)
                    if not early(i, 1):
                        pool.wait_ge(summed, g - V + 1)
                    pool.sem_inc(pool_turn, 1)
                    for k in range(U):
                        pool.indirect_dma_start(out=rows[u][:, k, :], out_offset=None, in_=t["xj_rows"],
                                                in_offset=bass.IndirectOffsetOnAxis(ap=index[u][:, k:k + 1], axis=0))\
                            .then_inc(rows_in[u], 16)

            group_turns(pool, turn)

        @block.scalar
        def _(act):
            def set_index(g, u, i):
                if not early(i, 1):
                    act.wait_ge(rows_in[u], 16 * U * i)
                nc.scalar.copy(index[u][:, :], t["other1"][:, bass.ds(g * U, U)]).then_inc(index_ready, 1)

            for g in range(AHEAD):
                set_index(g, g, 0)

            def turn(i):
                for u in range(V):
                    g = V * i + u
                    if not (isinstance(g, int) and g + AHEAD >= G):
                        set_index(g + AHEAD, (u + AHEAD) % V, i + (u + AHEAD) // V)
                    act.wait_ge(turned, g + 1)
                    if not early(g):
                        act.wait_ge(a1_ready, g - 1)
                    nc.scalar.copy(node_hot[u % 2][:, :, :], ps_hot[:, :, :]).then_inc(turned_copied, 1)
                    if not early(g, 1):
                        weigh(g - 1, u - 1)

            def weigh(g, u):
                act.wait_ge(logit_ready, g + 1)
                nc.scalar.activation(att[u % 2][:, :], logit[u % 2][:, :], ACT.Sigmoid).then_inc(att_ready, 1)
                act.wait_ge(att_ready, g + 1)
                if not early(g):
                    act.wait_ge(summed, g - 1)
                for k in range(U):
                    last = nc.scalar.activation(hot_att[u % 2][:, k, :], hot[u % 4][:, k, :], ACT.Copy, scale=att[u % 2][:, k:k + 1])
                last.then_inc(hot_att_ready, 1)

            group_turns(act, turn)
            weigh(G - 1, V - 1)

        @block.vector
        def _(dve):
            def encode(g, u):
                if not early(g, 4):
                    dve.wait_ge(hot_att_ready, g - 3)
                local = t["local1"][:, bass.ds(g * U, U)].unsqueeze(2).broadcast_to([P, U, P])
                dve.tensor_tensor(hot[u % 4][:, :, :], t["iota"][:, :].unsqueeze(1).broadcast_to([P, U, P]), local, ALU.is_equal)\
                    .then_inc(hot_ready, 1)

            def add_logits(g, u, i):
                dve.wait_ge(rows_in[u], 16 * U * (i + 1))
                dve.wait_ge(a1_ready, g + 1)
                dve.tensor_tensor(logit[u % 2][:, :], ps_a1[u % 2][:, :], rows[u][:, :, D], ALU.add).then_inc(logit_ready, 1)

            def add(g, u, places):
                for k in range(U):
                    dve.compute_val(places[k])
                dve.wait_ge(summed, g + 1)
                for k in range(U):
                    acc = tab[:, bass.ds(places[k], D)]
                    if not (isinstance(g, int) and g == 0 and k == 0):
                        dve.wait_ge(added, g * U + k)
                    dve.tensor_tensor(acc, acc, ps_sum[u % 2][:, k, :], ALU.add).then_inc(added, 1)

            def turn(i):
                places = places_of(dve, t["packed_late1"], i, D)
                for u in range(V):
                    g = V * i + u
                    if not (isinstance(g, int) and g + 2 >= G):
                        encode(g + 2, u + 2)
                    add_logits(g, u, i)
                    if not early(g, LAG):
                        add(g - LAG, u - LAG, places[u * U:])

            encode(0, 0)
            encode(1, 1)
            dve.memset(tab[:, 0:NB * D], 0.0).then_inc(cleared, 1)
            dve.wait_ge(cleared, 1)
            group_turns(dve, turn)
            places = places_of(dve, t["packed_late1"], G // V, D)
            for k in range(LAG):
                add(G - LAG + k, k, places[k * U:])
            dve.wait_ge(added, G * U)

        @block.tensor
        def _(pe):
            def turn_hot(g, u):
                pe.wait_ge(hot_ready, g + 1)
                if not early(g, 1):
                    pe.wait_ge(turned_copied, g)
                for k in range(U):
                    last = nc.tensor.transpose(ps_hot[:, k, :], hot[u % 4][:, k, :], t["ident"][:, :])
                last.then_inc(turned, 1)

            def sum_up(g, u):
                pe.wait_ge(hot_att_ready, g + 1)
                if not early(g):
                    pe.wait_ge(added, (g - 1) * U)
                for k in range(U):
                    last = nc.tensor.matmul(ps_sum[u % 2][:, k, :], hot_att[u % 2][:, k, :], rows[u % V][:, k, 0:D], start=True, stop=True)
                last.then_inc(summed, 1)

            def turn(i):
                places = places_of(pe, t["packed1"], i, 1)
                for u in range(V):
                    g = V * i + u
                    if not (isinstance(g, int) and g == G - 1):
                        turn_hot(g + 1, u + 1)
                    pe.wait_ge(turned_copied, g + 1)
                    if not early(g):
                        pe.wait_ge(logit_ready, g - 1)
                    for k in range(U):
                        last = nc.tensor.matmul(ps_a1[u % 2][:, k:k + 1], node_hot[u % 2][:, k, :],
                                                t["a1_tab"][:, bass.ds(places[u * U + k], 1)], start=True, stop=True)
                    last.then_inc(a1_ready, 1)
                    if not early(g, 1):
                        sum_up(g - 1, u - 1)

            turn_hot(0, 0)
            group_turns(pe, turn)
            sum_up(G - 1, V - 1)


def finish(nc, t):
    with ExitStack() as ctx:
        def ring(name, shape):
            return [ctx.enter_context(nc.sbuf_tensor(f"{name}{u}", shape, fp32)) for u in range(4)]

        def sem(name):
            return ctx.enter_context(nc.semaphore(name))

        tab = t["node_tab"]
        x1, y, small = ring("f_x1", [P, D]), ring("f_y", [P, D]), ring("f_small", [P, 16])
        eps, eps_set = ctx.enter_context(nc.sbuf_tensor("f_eps", [P, 1], fp32)), sem("f_eps_set")
        loaded, stored = [sem(f"f_loaded{u}") for u in range(4)], [sem(f"f_stored{u}") for u in range(4)]
        var_ready, std_ready, scale_ready, normed, dve_step = sem("f_var"), sem("f_std"), sem("f_scale"), sem("f_normed"), sem("f_dve_step")
        dve_turn = sem("f_turn")
        block = ctx.enter_context(nc.Block())

        @block.sync
        def _(sp):
            def load(b, s):
                if not early(b, 4):
                    sp.wait_ge(var_ready, b - 3)
                r = rows_of(b)
                sp.dma_start(x1[s][0:r, :], t["x1_rows"][bass.ds(b * P, r), :]).then_inc(loaded[s], 16)

            def store(b, s):
                r = rows_of(b)
                sp.wait_ge(normed, b + 1)
                sp.dma_start(t["out"][bass.ds(b * P, r), :], y[s][0:r, :]).then_inc(stored[s], 16)

            skewed(sp, [(0, load), (4, store)])
            for s in range(4):
                sp.wait_ge(stored[s], 16 * len(range(s, NB, 4)))

        @block.scalar
        def _(act):
            act.wait_ge(eps_set, 1)

            def sqrt(b, s):
                act.wait_ge(var_ready, b + 1)
                nc.scalar.activation(small[s][:, 8:9], small[s][:, 7:8], ACT.Sqrt, bias=eps[:, 0:1]).then_inc(std_ready, 1)

            def normalise(b, s):
                act.wait_ge(scale_ready, b + 1)
                nc.scalar.activation(y[s][:, :], y[s][:, :], ACT.Identity, scale=small[s][:, 9:10], bias=small[s][:, 10:11]).then_inc(normed, 1)

            skewed(act, [(3, normalise), (2, sqrt)])

        @block.vector
        def _(dve):
            dve.memset(eps[:, :], EPS).then_inc(eps_set, 1)
            step = Serial(dve, dve_step, 4 * 3)

            def stats(b, s):
                m = small[s]
                dve.wait_ge(loaded[s], (b - s) * 4 + 16 if not isinstance(b, int) else 16 * (b // 4 + 1))
                if not early(b, 4):
                    dve.wait_ge(stored[s], (b - s) * 4 if not isinstance(b, int) else 16 * (b // 4))
                step(dve.scalar_tensor_tensor(y[s][:, :], x1[s][:, :], 2.0, tab[:, bass.ds(b * D, D)], ALU.mult, ALU.add))
                step(dve.bn_stats(m[:, 0:6], y[s][:, :]))
                dve.sem_inc(dve_turn, 1)
                dve.bn_aggr(m[:, 6:8], m[:, 0:6]).then_inc(var_ready, 1)

            def scale(b, s):
                m = small[s]
                dve.wait_ge(std_ready, b + 1)
                step(dve.reciprocal(m[:, 9:10], m[:, 8:9]))
                dve.scalar_tensor_tensor(m[:, 10:11], m[:, 6:7], -1.0, m[:, 9:10], ALU.mult, ALU.mult).then_inc(scale_ready, 1)

            skewed(dve, [(2, stats), (3, scale)], step)


_INS = ["x", "src", "dst", "edge_type_64", "L0_gnn_query_emb", "L0_gnn_Wq", "L0_gnn_bq", "L0_gnn_Wk", "L0_gnn_bk",
        "L0_gnn_Wv", "L0_gnn_bv", "L0_gnn_rel_w", "L0_gnn_Wo", "L0_gnn_bo", "L0_gnn_gamma", "L0_gnn_beta",
        "L1_gnn_W1", "L1_gnn_b1", "L1_gnn_W2", "L1_gnn_b2", "L1_gnn_wa1", "L1_gnn_ba1", "L1_gnn_wa2", "L1_gnn_ba2"]


def kernel(**inputs):
    import numpy as _np
    import concourse.bacc as _bacc
    from concourse.bass_utils import run_bass_kernel_spmd as _run

    nc = _bacc.Bacc("TRN2", target_bir_lowering=False, num_devices=1)
    arrays, args = {}, []
    for name in _INS:
        a = _np.ascontiguousarray(inputs[name])
        arrays[f"in_{name}"] = a
        args.append(nc.dram_tensor(f"in_{name}", a.shape, mybir.dt.from_np(a.dtype), kind="ExternalInput").ap())
    out = nc.dram_tensor("out", (N, D), fp32, kind="ExternalOutput").ap()
    gnn_kernel(nc, *args, out)
    r = _run(nc, [arrays], core_ids=[0])
    return r.results[0]["out"]
```

```python
import concourse.bass as bass
from concourse import mybir
from contextlib import ExitStack

fp32 = mybir.dt.float32
bf16 = mybir.dt.bfloat16
i32 = mybir.dt.int32
ALU = mybir.AluOpType
ACT = mybir.ActivationFunctionType
AX = mybir.AxisListType

P = 128
N = 12500
E = 200000
D = 256
H = 4
DH = D // H
R = 64
NB = -(-N // P)
LAST_ROWS = N - (NB - 1) * P
T = -(-E // P)
U = 4
V = 4
TURN = U * V
LAG = 2
AHEAD = 2
G = -(-(T + NB - 1) // TURN) * V
S = G * U
BANKS = -(-S // 512)
C = S // P
AW = D + H
XW = D + 4
LOGN = 18
F = (1 << LOGN) // P
NODE_BITS = 14
NODE_MASK = (1 << NODE_BITS) - 1
KEY_BIAS = 1 << 30
PAD_NODE = NB * P - 1
EPS = 1e-5
LOWEST = -1.0e30
assert S % P == 0 and C * P >= T and PAD_NODE >= N and PAD_NODE < (1 << NODE_BITS) and NB <= P


class Serial:

    def __init__(self, eng, sem, per_loop=0):
        self.eng, self.sem, self.per_loop, self.n, self.turn = eng, sem, per_loop, 0, 0

    def __call__(self, ins):
        self.n += 1
        ins.then_inc(self.sem, 1)
        self.eng.wait_ge(self.sem, self.turn + self.n)

    def enter(self, i, per_turn):
        self.turn, self.start, self.per = i * per_turn, self.n, per_turn

    def leave(self, turns):
        assert self.n - self.start == self.per, (self.n, self.start, self.per)
        self.n, self.turn = self.start + self.per * turns, 0


def block_pairs(eng, body):
    body(0, 0)
    body(1, 1)
    with eng.Fori(1, NB // 2 - 1) as i:
        body(2 * i, 0)
        body(2 * i + 1, 1)
    body(NB - 2, 0)
    body(NB - 1, 1)


def pairs_and_flips(eng, body, flip):
    rounds = LOGN - 11
    few = 4
    first = NB // 2 - few * rounds
    body(0, 0)
    body(1, 1)
    start = 1
    for r in range(rounds + 1):
        end = first + few * r
        with eng.Fori(start, end - (r == rounds)) as i:
            body(2 * i, 0)
            body(2 * i + 1, 1)
        if r < rounds:
            flip(2 * r)
            flip(2 * r + 1)
        start = end
    body(NB - 2, 0)
    body(NB - 1, 1)


def split_exactly(pool, step, numbers, parts, rest):
    step(pool.tensor_copy(parts[0], numbers))
    step(pool.tensor_tensor(rest, numbers, parts[0], ALU.subtract))
    step(pool.tensor_copy(parts[1], rest))
    step(pool.tensor_tensor(rest, rest, parts[1], ALU.subtract))
    step(pool.tensor_copy(parts[2], rest))


def early(b, n=2):
    return isinstance(b, int) and b < n


def skewed(eng, stages, step=None):
    deepest = max(lag for lag, _ in stages)
    first = -(-(deepest + 4) // 4) * 4
    last = first + (NB - 1 - first) // 4 * 4

    def turn(i, w):
        for lag, stage in stages:
            if not isinstance(i, int) or 0 <= i - lag < NB:
                stage(i - lag, (w - lag) % 4)

    for i in range(first):
        turn(i, i % 4)
    with eng.Fori(first // 4, last // 4) as i:
        if step:
            step.enter(i - first // 4, step.per_loop)
        for w in range(4):
            turn(4 * i + w, w)
        if step:
            step.leave(last // 4 - first // 4)
    for i in range(last, NB + deepest):
        turn(i, i % 4)


def rows_of(b):
    return LAST_ROWS if isinstance(b, int) and b == NB - 1 else P


def group_turns(eng, turn):
    turn(0)
    with eng.Fori(1, G // V - 1) as i:
        turn(i)
    turn(G // V - 1)


def places_of(eng, packed, i, row):
    v = eng.value_load(packed[0:1, bass.ds(i, 1)], min_val=0, max_val=(P << (TURN - 1)) - 1)
    places = [eng.snap(((v & (P - 1)) * row).with_bounds(min_val=0, max_val=(NB - 1) * row))]
    for k in range(1, TURN):
        places.append(eng.snap((places[-1] + ((v >> (6 + k)) & 1) * row).with_bounds(min_val=0, max_val=(NB - 1) * row)))
    return places


def gnn_kernel(nc, x, src, dst, edge_type, query, wq, bq, wk, bk, wv, bv, rel_w, wo, bo, gamma, beta,
               w1, b1, w2, b2, wa1, ba1, wa2, ba2, out):
    with ExitStack() as ctx:
        def sb(name, shape, dt=fp32):
            return ctx.enter_context(nc.sbuf_tensor(name, shape, dt))

        def dram(name, shape, dt=fp32):
            return nc.dram_tensor(name, shape, dt, kind="Internal").ap()

        t = {}
        t["k_rows"] = dram("k_rows", (N, D))
        t["v_rows"] = dram("v_rows", (N, D))
        t["x1_rows"] = dram("x1_rows", (N, D))
        t["xj_rows"] = dram("xj_rows", (N, XW))
        t["sorted_keys"] = dram("sorted_keys", (1 << LOGN,), i32)

        t["node_tab"] = sb("node_tab", [P, NB * AW])
        t["ident"] = sb("ident", [P, P])
        t["ident_h"] = sb("ident_h", [P, P], bf16)
        t["iota"] = sb("iota", [P, P])
        t["ones"] = sb("ones", [P, P])
        t["ones_h"] = sb("ones_h", [P, P], bf16)
        for layer in range(2):
            t[f"other{layer}"] = sb(f"other{layer}", [P, S], i32)
            t[f"local{layer}"] = sb(f"local{layer}", [P, S])
            t[f"packed_late{layer}"] = sb(f"packed_late{layer}", [1, S // TURN + 1], i32)
            t[f"packed{layer}"] = sb(f"packed{layer}", [1, S // TURN], i32)
        t["rel"] = sb("rel", [P, S])
        t["score"] = sb("score", [P, S * H])
        t["a1_tab"] = sb("a1_tab", [P, NB])

        t["x"], t["src"], t["dst"], t["edge_type"], t["out"] = x, src, dst, edge_type, out
        project_and_sort(nc, t, query, wq, bq, wk, bk, wv, bv)
        build_steps(nc, t)
        edge_scores(nc, t, rel_w)
        softmax_numerators(nc, t)
        aggregate(nc, t)
        update_nodes(nc, t, wo, bo, gamma, beta, w1, b1, w2, b2, wa1, ba1, wa2, ba2)
        attend(nc, t)
        finish(nc, t)


def project_and_sort(nc, t, query, wq, bq, wk, bk, wv, bv):
    x, tab, ident, ones = t["x"], t["node_tab"], t["ident"], t["ones"]
    with ExitStack() as ctx:
        def sb(name, shape, dt=fp32):
            return ctx.enter_context(nc.sbuf_tensor(name, shape, dt))

        def sem(name):
            return ctx.enter_context(nc.semaphore(name))

        x_in = [sb(f"x_in{u}", [P, D]) for u in range(2)]
        enh = [sb(f"enh{u}", [P, 2, P]) for u in range(2)]
        kv_out = [sb(f"kv_out{u}", [P, 2 * D]) for u in range(2)]
        w_qkv = sb("w_qkv", [P, 2, 3 * D])
        b_qkv, b_rest = sb("b_qkv", [3 * D // P, P]), sb("b_rest", [3 * D // P, P])
        b_part = [sb(f"b_part{k}", [3 * D // P, P], bf16) for k in range(3)]
        b_parts = sb("b_parts", [3, 3 * D], bf16)
        q_col = sb("q_col", [P, 2])
        q01 = sb("q01", [P, 2])
        keys = [sb(f"keys{u}", [P, F], i32) for u in range(2)]
        sign = sb("sign", [P, 8])
        two_signs = sb("two_signs", [P, 8])
        pbit = sb("pbit", [P, 8], i32)
        pid = sb("pid", [P, 1], i32)
        ps_xt = ctx.enter_context(nc.psum_tensor("ps_xt", [P, 2, P], fp32))
        ps_q = ctx.enter_context(nc.psum_tensor("ps_q", [P, D], fp32))
        ps_kv = [ctx.enter_context(nc.psum_tensor(f"ps_kv{u}", [P, 2 * D], fp32)) for u in range(2)]
        ps_flip = ctx.enter_context(nc.psum_tensor("ps_flip", [P, 4, 512], fp32))

        consts_set, weights_in, x_loaded = sem("consts_set"), sem("weights_in"), [sem("x_loaded0"), sem("x_loaded1")]
        xt_ready, enh_ready, mm_done = sem("xt_ready"), sem("enh_ready"), sem("mm_done")
        evacuated = sem("evacuated")
        kv_stored, q01_ready = [sem("kv_stored0"), sem("kv_stored1")], sem("q01_ready")
        pool_step, dve_step = sem("pool_step"), sem("dve_step")
        keys_in, pads_set = sem("keys_in"), sem("pads_set")
        to_flip, flipped, flip_copied, keys_out = sem("to_flip"), sem("flipped"), sem("flip_copied"), sem("keys_out")
        sorted_ready, b_parts_in, q_left = sem("sorted_ready"), sem("b_parts_in"), sem("q_left")
        flip_from, now = [], 0
        for k in range(1, LOGN + 1):
            if k > 11:
                flip_from += [now, (k - 11) % 2]
                now = 0
            now = (now + min(k, 11)) % 2
        flip_from.append(now)
        full_p = E // F
        rest = E - full_p * F
        block = ctx.enter_context(nc.Block())

        @block.sync
        def _(sp):
            sp.wait_ge(pads_set, 1)
            for n, a in enumerate((t["src"], t["dst"])):
                sp.dma_start(keys[n][0:full_p, :], a[0:full_p * F].rearrange("(p f) -> p f", f=F)).then_inc(keys_in, 16)
                sp.dma_start(keys[n][full_p:full_p + 1, 0:rest],
                             a[full_p * F:E].rearrange("(p f) -> p f", p=1)).then_inc(keys_in, 16)
            for n, (w, b) in enumerate(((wq, bq), (wk, bk), (wv, bv))):
                sp.dma_start(w_qkv[:, :, n * D:(n + 1) * D], w.rearrange("(c p) n -> p c n", p=P)).then_inc(weights_in, 16)
                sp.dma_start(b_qkv[2 * n:2 * n + 2, :], b.rearrange("(a n) -> a n", n=P)).then_inc(weights_in, 16)
            with nc.allow_non_contiguous_dma(reason="256 numbers, once"):
                sp.dma_start(q_col[:, :], query.rearrange("(c p) -> p c", p=P)).then_inc(weights_in, 16)

            def load(b, u):
                r = rows_of(b)
                sp.dma_start(x_in[u][0:r, :], x[bass.ds(b * P, r), :]).then_inc(x_loaded[u], 16)

            load(0, 0)
            load(1, 1)

            def body(b, u):
                sp.wait_ge(xt_ready, b + 1)
                if not (isinstance(b, int) and b + 2 >= NB):
                    load(b + 2, u)

            with sp.Fori(0, NB // 2 - 2) as i:
                body(2 * i, 0)
                body(2 * i + 1, 1)
            body(NB - 4, 0)
            body(NB - 3, 1)
            sp.wait_ge(sorted_ready, 1)
            sp.dma_start(t["sorted_keys"].rearrange("(p f) -> p f", f=F), keys[flip_from[-1]][:, :]).then_inc(keys_out, 16)
            sp.wait_ge(keys_out, 16)

        @block.gpsimd
        def _(pool):
            step = Serial(pool, pool_step)
            step(nc.gpsimd.memset(keys[0][96:P, :], PAD_NODE))
            nc.gpsimd.memset(keys[1][96:P, :], 0).then_inc(pads_set, 1)
            pool.wait_ge(pads_set, 1)
            for m, base in ((t["ident"], 0.0), (t["ident_h"], 0.0), (ones, 1.0)):
                step(nc.gpsimd.memset(m[:, :], base))
            for m in (t["ident"], t["ident_h"]):
                step(nc.gpsimd.affine_select(out=m[:, :], in_=m[:, :], compare_op=ALU.not_equal, fill=1.0,
                                             base=0, pattern=[[-1, P]], channel_multiplier=1))
            step(nc.gpsimd.iota(t["iota"][:, :], [[1, P]], base=0, channel_multiplier=0,
                                allow_small_or_imprecise_dtypes=True))
            step(nc.gpsimd.iota(pid[:, :], [[1, 1]], base=0, channel_multiplier=1))
            step(nc.gpsimd.memset(t["a1_tab"][:, :], 0.0))
            step(nc.gpsimd.memset(t["ones_h"][:, :], 1.0))
            pool.sem_inc(consts_set, 1)
            pool.wait_ge(weights_in, 7 * 16)
            split_exactly(nc.gpsimd, step, b_qkv[:, :], [p[:, :] for p in b_part], b_rest[:, :])
            for k in range(3):
                pool.dma_start(b_parts[k:k + 1, :], b_part[k][:, :]).then_inc(b_parts_in, 16)

            def body(b, u):
                r = rows_of(b)
                pool.wait_ge(evacuated, b + 1)
                for k, rows in enumerate((t["k_rows"], t["v_rows"])):
                    pool.dma_start(rows[bass.ds(b * P, r), :], kv_out[u][0:r, k * D:(k + 1) * D])\
                        .then_inc(kv_stored[u], 16)

            block_pairs(pool, body)
            for u in range(2):
                pool.wait_ge(kv_stored[u], NB // 2 * 32)

        @block.scalar
        def _(act):
            act.wait_ge(weights_in, 7 * 16)
            nc.scalar.mul(q01[:, :], q_col[:, :], 0.1).then_inc(q01_ready, 1)
            act.wait_ge(q01_ready, 1)

            def enhance(b, u):
                act.wait_ge(xt_ready, b + 1)
                for c in range(2):
                    last = nc.scalar.activation(enh[u][:, c, :], ps_xt[:, c, :], ACT.Identity, bias=q01[:, c:c + 1])
                last.then_inc(enh_ready, 1)

            def evacuate(b, u):
                act.wait_ge(mm_done, b + 1)
                if not early(b):
                    act.wait_ge(kv_stored[u], (b - u) * 16)
                nc.scalar.activation(tab[:, bass.ds(b * AW, D)], ps_q[:, :], ACT.Copy, scale=float(DH) ** -0.5)\
                    .then_inc(q_left, 1)
                nc.scalar.activation(kv_out[u][:, :], ps_kv[u][:, :], ACT.Copy).then_inc(evacuated, 1)

            enhance(0, 0)

            def body(b, u):
                if not (isinstance(b, int) and b == NB - 1):
                    enhance(b + 1, 1 - u)
                evacuate(b, u)

            def copy_flipped(r):
                for bank in range(4):
                    act.wait_ge(flipped, 4 * r + bank + 1)
                    nc.scalar.activation(keys[0][:, bank * 512:(bank + 1) * 512].bitcast(fp32),
                                         ps_flip[:, bank, :], ACT.Copy).then_inc(flip_copied, 1)

            pairs_and_flips(act, body, copy_flipped)

        @block.tensor
        def _(pe):
            pe.wait_ge(consts_set, 1)
            pe.wait_ge(weights_in, 7 * 16)
            pe.wait_ge(b_parts_in, 3 * 16)

            def transpose(b, u):
                pe.wait_ge(x_loaded[u], (b - u) * 8 + 16)
                for c in range(2):
                    last = nc.tensor.transpose(ps_xt[:, c, :], x_in[u][:, c * P:(c + 1) * P], ident[:, :])
                last.then_inc(xt_ready, 1)

            def body(b, u):
                pe.wait_ge(enh_ready, b + 1)
                if not (isinstance(b, int) and b == NB - 1):
                    transpose(b + 1, 1 - u)
                if not early(b):
                    pe.wait_ge(evacuated, b - 1)
                for o, (lo, hi) in ((ps_kv[u][:, :], (D, 3 * D)), (ps_q[:, :], (0, D))):
                    if lo == 0 and not early(b, 1):
                        pe.wait_ge(q_left, b)
                    for c in range(2):
                        nc.tensor.matmul(o, enh[u][:, c, :], w_qkv[:, c, lo:hi], start=(c == 0), stop=False)
                    last = nc.tensor.matmul(o, t["ones_h"][0:3, :], b_parts[:, lo:hi], start=False, stop=True)
                last.then_inc(mm_done, 1)

            transpose(0, 0)

            def flip(r):
                for bank in range(4):
                    pe.wait_ge(to_flip, 4 * r + bank + 1)
                    for c in range(4):
                        col = bank * 4 + c
                        last = nc.tensor.transpose(ps_flip[:, bank, c * P:(c + 1) * P],
                                                   keys[flip_from[r]][:, col * P:(col + 1) * P].bitcast(fp32), ident[:, :])
                    last.then_inc(flipped, 1)

            pairs_and_flips(pe, body, flip)

        @block.vector
        def _(dve):
            step = Serial(dve, dve_step)
            pair = [keys[0][:, :].bitcast(fp32), keys[1][:, :].bitcast(fp32)]
            dve.wait_ge(keys_in, 64)
            dve.wait_ge(consts_set, 1)
            step(dve.tensor_scalar(keys[0][:, :], keys[0][:, :], NODE_BITS, KEY_BIAS,
                                   ALU.logical_shift_left, ALU.bitwise_or))
            step(dve.tensor_tensor(keys[0][:, :], keys[0][:, :], keys[1][:, :], ALU.bitwise_or))
            for m in range(7):
                step(dve.tensor_scalar(pbit[:, m:m + 1], pid[:, :], m, 1, ALU.logical_shift_right, ALU.bitwise_and))
            step(dve.tensor_scalar(sign[:, 0:7], pbit[:, 0:7], -2.0, 1.0, ALU.mult, ALU.add))
            step(dve.memset(sign[:, 7:8], 1.0))
            step(dve.tensor_tensor(two_signs[:, 0:7], sign[:, 0:7], sign[:, 1:8], ALU.mult))
            now = 0

            def exchange(distance, now, copied=None, to=None):
                parts = 1 if copied is None and to is None else 4
                for q in range(parts):
                    if copied is not None:
                        dve.wait_ge(flip_copied, copied + q + 1)
                    a, b = (z[:, q * F // parts:(q + 1) * F // parts].rearrange("p (n two d) -> p n two d", two=2, d=distance)
                            for z in (pair[now], pair[1 - now]))
                    dve.tensor_tensor(b[:, :, 0, :], a[:, :, 0, :], a[:, :, 1, :], ALU.min)
                    last = dve.tensor_tensor(b[:, :, 1, :], a[:, :, 0, :], a[:, :, 1, :], ALU.max)
                    if to is not None:
                        last.then_inc(to, 1)
                if to is None:
                    step(last)
                return 1 - now

            rounds = 0
            for k in range(1, LOGN + 1):
                z = pair[now]
                if k == 1:
                    v = z.rearrange("p (n s w) -> p n s w", s=2, w=2)[:, :, 1, :]
                    step(dve.tensor_scalar(v, v, -1.0, None, ALU.mult))
                elif k < 11:
                    v = z.rearrange("p (n s w) -> p n s w", s=4, w=1 << (k - 1))[:, :, 1:3, :]
                    step(dve.tensor_scalar(v, v, -1.0, None, ALU.mult))
                else:
                    if k == 11:
                        v = z[:, F // 2:F]
                        step(dve.tensor_scalar(v, v, -1.0, None, ALU.mult))
                        step(dve.tensor_scalar(z, z, sign[:, 0:1], None, ALU.mult))
                    else:
                        for q in range(4):
                            v = z[:, q * F // 4:(q + 1) * F // 4]
                            dve.tensor_scalar(v, v, two_signs[:, k - 12:k - 11], None, ALU.mult).then_inc(to_flip, 1)
                if k > 11:
                    assert now == flip_from[rounds]
                    now = 0
                    for j in range(k - 12, -1, -1):
                        now = exchange(1 << j, now, copied=4 * rounds if j == k - 12 else None, to=to_flip if j == 0 else None)
                    rounds += 1
                    assert now == flip_from[rounds]
                    rounds += 1
                    dve.wait_ge(flip_copied, 4 * rounds)
                    now = 0
                for j in range(min(k, 11) - 1, -1, -1):
                    now = exchange(1 << j, now)
            assert now == flip_from[rounds]
            dve.sem_inc(sorted_ready, 1)


def build_steps(nc, t):
    with ExitStack() as ctx:
        def sb(name, shape, dt=fp32):
            return ctx.enter_context(nc.sbuf_tensor(name, shape, dt))

        def sem(name):
            return ctx.enter_context(nc.semaphore(name))

        names = (("dst", "src", "edge_type"), ("key",))
        raw = {n: t["score"][:, k * S:(k + 1) * S].bitcast(i32).rearrange("q (c e) -> q c e", e=P)
               for k, n in enumerate(names[0] + names[1])}
        node = [raw["dst"], sb("sorted_src", [P, C, P], i32)]
        far = [raw["src"], raw["key"]]
        arrays = [[node[0], far[0], raw["edge_type"]], [node[1], far[1]]]
        last_block = sb("last_block", [P, C], i32)
        partition = sb("partition", [P, 2])
        iota_p = sb("iota_p", [P, P])
        tile_end = sb("tile_end", [P, C, 2])
        block_row = sb("block_row", [P, C, P])
        before = t["local1"][:, :].bitcast(bf16).rearrange("q (c k s) -> q c k s", k=2, s=P)
        hit = sb("hit", [P, C, 2, P])
        coef = sb("coef", [1, TURN])
        late = sb("late", [1, S + TURN])
        mixed = sb("mixed", [1, S + TURN])
        packed = sb("packed", [1, S // TURN + 1])
        ps_tile = ctx.enter_context(nc.psum_tensor("ps_tile", [P, BANKS * 4, P], fp32))
        ps_val = [ctx.enter_context(nc.psum_tensor(f"ps_val{k}", [P, 4, P], fp32)) for k in range(BANKS)]
        pads_set, edges_in, pool_step, dve_step = sem("tile_pads"), sem("edges_in"), sem("pool_step2"), sem("dve_step2")
        ids_set, before_ready, tile_ready, far_ready = sem("ids_set"), sem("before_ready"), sem("tile_ready"), sem("far_ready")
        tile_left = sem("tile_left")
        hit_ready, val_ready = sem("hit_ready"), sem("val_ready")
        val_left = [sem(f"val_left{k}") for k in range(BANKS)]
        fills = [(layer, v, range(j * 4, min(C, j * 4 + 4)))
                 for layer in range(2) for j in range(BANKS) for v in range(len(arrays[layer]))]
        full_c = T // P
        full_q = E // P - full_c * P
        rest = E - (full_c * P + full_q) * P
        block = ctx.enter_context(nc.Block())

        @block.sync
        def _(sp):
            sp.wait_ge(pads_set, 1)
            for n in names[0]:
                a = t[n]
                sp.dma_start(raw[n][:, 0:full_c, :], a[0:full_c * P * P].rearrange("(c q e) -> q c e", q=P, e=P)).then_inc(edges_in, 16)
                sp.dma_start(raw[n][0:full_q, full_c, :],
                             a[full_c * P * P:(full_c * P + full_q) * P].rearrange("(q e) -> q e", e=P)).then_inc(edges_in, 16)
                sp.dma_start(raw[n][full_q:full_q + 1, full_c, 0:rest],
                             a[E - rest:E].rearrange("(q e) -> q e", q=1)).then_inc(edges_in, 16)
            sp.dma_start(raw["key"][:, :, :], t["sorted_keys"][0:C * P * P].rearrange("(c q e) -> q c e", q=P, e=P))\
                .then_inc(edges_in, 16)

        @block.gpsimd
        def _(pool):
            step = Serial(pool, pool_step)
            for n, pad in zip(names[0], (PAD_NODE, 0, 0)):
                step(nc.gpsimd.memset(raw[n][:, full_c:C, :], pad))
            pool.sem_inc(pads_set, 1)
            step(nc.gpsimd.iota(iota_p[:, :], [[1, P]], base=P, channel_multiplier=0,
                                allow_small_or_imprecise_dtypes=True))
            step(nc.gpsimd.iota(partition[:, :], [[P, 2]], base=0, channel_multiplier=1,
                                allow_small_or_imprecise_dtypes=True))
            step(nc.gpsimd.memset(tile_end[:, 0, 0:1], -1.0))
            for k in range(TURN):
                step(nc.gpsimd.memset(coef[:, k:k + 1], float(P << (k - 1)) if k else 1.0))
            pool.sem_inc(ids_set, 1)

        @block.scalar
        def _(act):
            act.wait_ge(edges_in, (3 * 3 + 1) * 16)
            for a in arrays[0][1:]:
                nc.scalar.copy(a[:, :, :].bitcast(fp32), a[:, :, :]).then_inc(far_ready, 1)
            for n, (layer, v, chunks) in enumerate(fills):
                if v > 0:
                    into = t["rel"] if v == 2 else t[f"other{layer}"]
                    act.wait_ge(val_ready, n + 1)
                    nc.scalar.copy(into[:, chunks[0] * P:(chunks[-1] + 1) * P].rearrange("p (c s) -> p c s", s=P),
                                   ps_val[n % BANKS][:, 0:len(chunks), :]).then_inc(val_left[n % BANKS], 1)

        @block.vector
        def _(dve):
            step = Serial(dve, dve_step)
            dve.wait_ge(ids_set, 1)
            dve.wait_ge(edges_in, (3 * 3 + 1) * 16)

            def find_ends(layer):
                step(dve.tensor_scalar(last_block[:, :], node[layer][:, :, P - 1], 7, None, ALU.logical_shift_right))
                step(dve.tensor_scalar(tile_end[:, :, 1], last_block[:, :], partition[:, 0:1], None, ALU.add))
                step(dve.tensor_scalar(tile_end[:, 1:C, 0], tile_end[:, 0:C - 1, 1], -float(P), None, ALU.add))
                dve.tensor_tensor(before.rearrange("q c k s -> q (c k) s"), t["iota"][:, :].unsqueeze(1).broadcast_to([P, 2 * C, P]),
                                  tile_end[:, :, :].rearrange("q c k -> q (c k)").unsqueeze(2).broadcast_to([P, 2 * C, P]), ALU.is_gt)\
                    .then_inc(before_ready, 1)
                step(dve.tensor_copy(node[layer][:, :, :].bitcast(fp32), node[layer][:, :, :]))

            def find_hits(layer):
                dve.wait_ge(tile_ready, layer + 1)
                if layer:
                    dve.wait_ge(val_ready, len([f for f in fills if f[0] == 0]))
                for k in range(2):
                    step(dve.tensor_scalar(hit[:, :, k, :], ps_tile[:, 0:C, :], partition[:, k:k + 1], None, ALU.is_equal))
                dve.sem_inc(hit_ready, 1)
                step(dve.tensor_tensor(block_row[:, :, :], iota_p[:, :].unsqueeze(1).broadcast_to([P, C, P]), ps_tile[:, 0:C, :],
                                       ALU.subtract))
                dve.sem_inc(tile_left, 1)

            def find_places(layer):
                for n, (l, v, chunks) in enumerate(fills):
                    if l == layer and v == 0:
                        dve.wait_ge(val_ready, n + 1)
                        dve.scalar_tensor_tensor(t[f"local{layer}"][:, chunks[0] * P:(chunks[-1] + 1) * P].rearrange("p (c s) -> p c s", s=P),
                                                 block_row[:, chunks[0]:chunks[-1] + 1, :], -float(P),
                                                 ps_val[n % BANKS][:, 0:len(chunks), :], ALU.mult, ALU.add).then_inc(val_left[n % BANKS], 1)

            def pack(layer):
                row = block_row[0:1, :, :].rearrange("p c s -> p (c s)")
                step(dve.memset(late[:, 0:LAG * U], 0.0))
                step(dve.tensor_copy(late[:, LAG * U:LAG * U + S], row))
                step(dve.tensor_scalar(late[:, LAG * U + S:S + TURN], late[:, 0:TURN - LAG * U], 0.0, float(NB - 1), ALU.mult, ALU.add))
                for blocks, into, turns in ((row, "packed", S // TURN), (late, "packed_late", S // TURN + 1)):
                    by_turn, m = (z[0:1, 0:turns * TURN].rearrange("p (g k) -> p g k", k=TURN) for z in (blocks, mixed))
                    step(dve.tensor_tensor(m[:, :, 1:TURN], by_turn[:, :, 1:TURN], by_turn[:, :, 0:TURN - 1], ALU.subtract))
                    step(dve.tensor_copy(m[:, :, 0], by_turn[:, :, 0]))
                    step(dve.tensor_tensor(m, m, coef[:, :].unsqueeze(1).broadcast_to([1, turns, TURN]), ALU.mult))
                    step(dve.tensor_reduce(packed[:, 0:turns], m, AX.X, ALU.add))
                    step(dve.tensor_copy(t[f"{into}{layer}"][:, 0:turns], packed[:, 0:turns]))

            find_ends(0)
            step(dve.tensor_scalar(node[1][:, :, :], raw["key"][:, :, :], NODE_BITS, NODE_MASK,
                                   ALU.logical_shift_right, ALU.bitwise_and))
            find_hits(0)
            step(dve.tensor_scalar(raw["key"][:, :, :], raw["key"][:, :, :], NODE_MASK, None, ALU.bitwise_and))
            step(dve.tensor_copy(raw["key"][:, :, :].bitcast(fp32), raw["key"][:, :, :]))
            find_ends(1)
            find_places(0)
            pack(0)
            find_hits(1)
            pack(1)
            find_places(1)

        @block.tensor
        def _(pe):
            for layer in range(2):
                pe.wait_ge(before_ready, layer + 1)
                if layer:
                    pe.wait_ge(tile_left, 1)
                for j in range(BANKS):
                    chunks = range(j * 4, min(C, j * 4 + 4))
                    for k in range(2):
                        last = nc.tensor.matmul(ps_tile[:, chunks[0]:chunks[-1] + 1, :], t["ones_h"][:, :],
                                                before[:, chunks[0]:chunks[-1] + 1, k, :], start=(k == 0), stop=(k == 1))
                last.then_inc(tile_ready, 1)
                pe.wait_ge(hit_ready, layer + 1)
                if layer == 0:
                    pe.wait_ge(far_ready, 2)
                for n, (l, v, chunks) in enumerate(fills):
                    if l == layer:
                        if n >= BANKS:
                            pe.wait_ge(val_left[n % BANKS], n // BANKS)
                        for c in chunks:
                            near = [c - 1, c] if c else [c]
                            for a in near:
                                last = nc.tensor.matmul(ps_val[n % BANKS][:, c - chunks[0], :], arrays[layer][v][:, a, :].bitcast(fp32),
                                                        hit[:, c, a - c + 1, :], start=(a == near[0]), stop=(a == c))
                        last.then_inc(val_ready, 1)


def edge_scores(nc, t, rel_w):
    with ExitStack() as ctx:
        def sb(name, shape, dt=fp32):
            return ctx.enter_context(nc.sbuf_tensor(name, shape, dt))

        def pb(name, shape, dt=fp32):
            return ctx.enter_context(nc.psum_tensor(name, shape, dt))

        def sem(name):
            return ctx.enter_context(nc.semaphore(name))

        rel_in = sb("rel_in", [R, DH])
        rel_02 = sb("rel_02", [R, DH])
        index = [sb(f"s_index{u}", [P, U], i32) for u in range(V)]
        rows = [sb(f"s_rows{u}", [P, U, D]) for u in range(V)]
        prod = sb("prod", [P, U, D])
        what = sb("what", [P, 2, S], bf16)
        minus_p = sb("minus_p", [P, 1])
        apart = [sb(f"apart{u}", [P, 2, U, P], bf16) for u in range(2)]
        hot = [sb(f"hot{u}", [P, 2, U, P]) for u in range(2)]
        ps_what = [pb(f"ps_what{u}", [P, 2, U, P], bf16) for u in range(2)]
        ps_q = [pb(f"ps_q{u}", [P, U, D]) for u in range(2)]
        ps_rel = [pb(f"ps_rel{u}", [P, U, DH]) for u in range(2)]
        weights_in, rel_ready = sem("rel_in_sem"), sem("rel_ready")
        index_ready, rows_in, rows_used = sem("s_index_ready"), [sem(f"s_rows_in{u}") for u in range(V)], sem("s_rows_used")
        what_ready, minus_ready, turned, apart_ready, hot_ready = (sem(f"s_{n}") for n in ("what_ready", "minus_ready", "turned", "apart_ready", "hot_ready"))
        picked, picked_used, scored = sem("s_picked"), sem("s_picked_used"), sem("s_scored")
        pool_turn = sem("s_pool_turn")
        block = ctx.enter_context(nc.Block())

        @block.sync
        def _(sp):
            sp.dma_start(rel_in[:, :], rel_w).then_inc(weights_in, 16)

        @block.gpsimd
        def _(pool):
            nc.gpsimd.iota(minus_p[:, :], [[1, 1]], base=0, channel_multiplier=-1,
                           allow_small_or_imprecise_dtypes=True).then_inc(minus_ready, 1)

            def turn(i):
                for u in range(V):
                    g = V * i + u
                    pool.wait_ge(index_ready, g + 1)
                    if not early(i, 1):
                        pool.wait_ge(rows_used, g - V + 1)
                    pool.sem_inc(pool_turn, 1)
                    for k in range(U):
                        pool.indirect_dma_start(out=rows[u][:, k, :], out_offset=None, in_=t["k_rows"],
                                                in_offset=bass.IndirectOffsetOnAxis(ap=index[u][:, k:k + 1], axis=0))\
                            .then_inc(rows_in[u], 16)

            group_turns(pool, turn)

        @block.scalar
        def _(act):
            def set_index(g, u, i):
                if not early(i, 1):
                    act.wait_ge(rows_in[u], 16 * U * i)
                nc.scalar.copy(index[u][:, :], t["other0"][:, bass.ds(g * U, U)]).then_inc(index_ready, 1)

            for g in range(AHEAD):
                set_index(g, g, 0)

            act.wait_ge(weights_in, 16)
            nc.scalar.mul(rel_02[:, :], rel_in[:, :], 0.2).then_inc(rel_ready, 1)

            def turn(i):
                for u in range(V):
                    g = V * i + u
                    if not (isinstance(g, int) and g + AHEAD >= G):
                        set_index(g + AHEAD, (u + AHEAD) % V, i + (u + AHEAD) // V)
                    act.wait_ge(turned, g + 1)
                    nc.scalar.activation(apart[u % 2][:, :, :, :], ps_what[u % 2][:, :, :, :], ACT.Abs,
                                         bias=minus_p[:, 0:1]).then_inc(apart_ready, 1)
                    act.wait_ge(apart_ready, g + 1)
                    if not early(g):
                        act.wait_ge(picked, g - 1)
                    nc.scalar.activation(hot[u % 2][:, :, :, :], apart[u % 2][:, :, :, :], ACT.Relu,
                                         scale=-1.0, bias=t["ones"][:, 0:1]).then_inc(hot_ready, 1)

            act.wait_ge(minus_ready, 1)
            group_turns(act, turn)

        @block.vector
        def _(dve):
            def work(g, u, i):
                by_head = rows[u][:, :, :].rearrange("p k (h d) -> p k h d", h=H)
                dve.wait_ge(picked, g + 1)
                dve.wait_ge(rows_in[u], 16 * U * (i + 1))
                if not (isinstance(g, int) and g == 0):
                    dve.wait_ge(scored, g)
                dve.tensor_tensor(prod[:, :, :].rearrange("p k (h d) -> p k h d", h=H), by_head,
                                  ps_rel[u % 2][:, :, :].unsqueeze(2).broadcast_to([P, U, H, DH]), ALU.add).then_inc(rows_used, 1)
                dve.wait_ge(rows_used, g + 1)
                dve.tensor_tensor(prod[:, :, :], prod[:, :, :], ps_q[u % 2][:, :, :], ALU.mult).then_inc(picked_used, 1)
                dve.wait_ge(picked_used, g + 1)
                dve.tensor_reduce(t["score"][:, bass.ds(g * U * H, U * H)],
                                  prod[:, :, :].rearrange("p k (h d) -> p (k h) d", h=H), AX.X, ALU.add).then_inc(scored, 1)

            def turn(i):
                for u in range(V):
                    g = V * i + u
                    work(g, u, i)

            dve.tensor_scalar(what[:, 0, :], t["local0"][:, :], -1.0, float(P), ALU.max, ALU.min)
            dve.tensor_copy(what[:, 1, :], t["rel"][:, :]).then_inc(what_ready, 1)
            group_turns(dve, turn)
            dve.wait_ge(scored, G)

        @block.tensor
        def _(pe):
            def spread(g, u):
                if not early(g):
                    pe.wait_ge(apart_ready, g - 1)
                for n in range(2):
                    for k in range(U):
                        number = what[:, n, bass.ds(g * U + k, 1)].broadcast_to([P, P])
                        last = nc.tensor.transpose(ps_what[u % 2][:, n, k, :], number, t["ident_h"][:, :])
                last.then_inc(turned, 1)

            def turn(i):
                places = places_of(pe, t["packed0"], i, AW)
                for u in range(V):
                    g = V * i + u
                    if not (isinstance(g, int) and g == G - 1):
                        spread(g + 1, u + 1)
                    pe.wait_ge(hot_ready, g + 1)
                    if not early(g):
                        pe.wait_ge(picked_used, g - 1)
                    for k in range(U):
                        nc.tensor.matmul(ps_rel[u % 2][:, k, :], hot[u % 2][0:R, 1, k, :], rel_02[:, :], start=True, stop=True)
                    for k in range(U):
                        last = nc.tensor.matmul(ps_q[u % 2][:, k, :], hot[u % 2][:, 0, k, :],
                                                t["node_tab"][:, bass.ds(places[u * U + k], D)], start=True, stop=True)
                    last.then_inc(picked, 1)

            pe.wait_ge(rel_ready, 1)
            pe.wait_ge(what_ready, 1)
            spread(0, 0)
            group_turns(pe, turn)


def softmax_numerators(nc, t):
    with ExitStack() as ctx:
        def sb(name, shape, dt=fp32):
            return ctx.enter_context(nc.sbuf_tensor(name, shape, dt))

        def sem(name):
            return ctx.enter_context(nc.semaphore(name))

        W = S * H
        tab = t["node_tab"]
        y, fwd, bwd = tab[:, 0:W], tab[:, W:2 * W], tab[:, 2 * W:3 * W]
        loc, valid, pen = (tab[:, 3 * W + k * S:3 * W + (k + 1) * S] for k in range(3))
        score = t["score"]

        def by_edge(v):
            return v.rearrange("q (c e) -> q c e", e=P)

        def by_head(v):
            return v.rearrange("q (c h e) -> q c h e", h=H, e=P)

        def all_heads(v):
            return by_edge(v).unsqueeze(2).broadcast_to([P, C, H, P])

        restart = sb("restart", [P, W + 1])
        differs = by_edge(fwd[:, 0:S])
        ends = sb("ends", [P, 4, C, H])
        rows = [score[0:H, k * S:(k + 1) * S] for k in range(4)]
        cont = sb("cont", [H, S + 1])
        reach = t["rel"][0:H, :]
        carry = [v[0:H, :] for v in (valid, pen)]
        ps_y = [ctx.enter_context(nc.psum_tensor(f"ps_y{u}", [P, H, P], fp32)) for u in range(2)]
        ps_rows = ctx.enter_context(nc.psum_tensor("ps_rows", [P, 4 * 512], fp32))
        ps_carry = ctx.enter_context(nc.psum_tensor("ps_carry", [P, 2, C, H], fp32))
        y_turned, y_copied, loc_turned, loc_copied = sem("y_turned"), sem("y_copied"), sem("loc_turned"), sem("loc_copied")
        ends_ready, ends_turned, ends_copied = sem("ends_ready"), sem("ends_turned"), sem("ends_copied")
        carry_ready, carry_turned = sem("carry_ready"), sem("carry_turned")
        less_max, w_turned, w_copied = sem("less_max"), sem("w_turned"), sem("w_copied")
        dve_step, differs_ready, restart_ready = sem("dve_step4"), sem("differs_ready"), sem("restart_ready")
        block = ctx.enter_context(nc.Block())

        @block.tensor
        def _(pe):
            ident = t["ident"]
            for c in range(C):
                last = nc.tensor.transpose(ps_rows[:, c * P:(c + 1) * P], t["local0"][:, c * P:(c + 1) * P], ident[:, :])
            last.then_inc(loc_turned, 1)
            for c in range(C):
                if c >= 2:
                    pe.wait_ge(y_copied, c - 1)
                s = score[:, c * P * H:(c + 1) * P * H].rearrange("p (s h) -> p h s", h=H)
                for h in range(H):
                    last = nc.tensor.transpose(ps_y[c % 2][:, h, :], s[:, h, :], ident[:, :])
                last.then_inc(y_turned, 1)
            pe.wait_ge(ends_ready, 1)
            pe.wait_ge(loc_copied, 1)
            for k in range(4):
                if k:
                    pe.wait_ge(ends_copied, k)
                for c in range(C):
                    last = nc.tensor.transpose(ps_rows[0:H, c * P:(c + 1) * P], ends[:, k, c, :], ident[:, :])
                last.then_inc(ends_turned, 1)
            pe.wait_ge(carry_ready, 1)
            for k in range(2):
                for c in range(C):
                    last = nc.tensor.transpose(ps_carry[:, k, c, :], carry[k][:, c * P:(c + 1) * P], ident[0:H, 0:H])
            last.then_inc(carry_turned, 1)
            for c in range(C):
                pe.wait_ge(less_max, c + 1)
                if c >= 2:
                    pe.wait_ge(w_copied, c - 1)
                for h in range(H):
                    last = nc.tensor.transpose(ps_y[c % 2][:, h, :], by_head(y)[:, c, h, :], ident[:, :])
                last.then_inc(w_turned, 1)

        @block.gpsimd
        def _(pool):
            pool.wait_ge(less_max, 1)
            nc.gpsimd.memset(tab[:, 2 * W:], 0.0)

        @block.scalar
        def _(act):
            act.wait_ge(loc_turned, 1)
            nc.scalar.copy(loc, ps_rows[:, 0:S]).then_inc(loc_copied, 1)
            for c in range(C):
                act.wait_ge(y_turned, c + 1)
                nc.scalar.copy(by_head(y)[:, c, :, :], ps_y[c % 2][:, :, :]).then_inc(y_copied, 1)
            act.wait_ge(differs_ready, 1)
            nc.scalar.activation(by_head(restart[:, 0:W])[:, :, :, 1:P], differs[:, :, 1:P].unsqueeze(2).broadcast_to([P, C, H, P - 1]),
                                 ACT.Copy, scale=LOWEST).then_inc(restart_ready, 1)
            for k in range(4):
                act.wait_ge(ends_turned, k + 1)
                nc.scalar.copy(rows[k], ps_rows[0:H, 0:S]).then_inc(ends_copied, 1)
            for c in range(C):
                act.wait_ge(w_turned, c + 1)
                nc.scalar.activation(score[:, c * P * H:(c + 1) * P * H].rearrange("p (s h) -> p h s", h=H), ps_y[c % 2][:, :, :],
                                     ACT.Exp).then_inc(w_copied, 1)
            act.wait_ge(w_copied, C)

        @block.vector
        def _(dve):
            step = Serial(dve, dve_step)
            dve.wait_ge(loc_copied, 1)
            step(dve.tensor_scalar(valid, loc, 0.0, None, ALU.is_ge))
            step(dve.scalar_tensor_tensor(valid, loc, float(P - 1), valid, ALU.is_le, ALU.mult))
            step(dve.tensor_scalar(pen, valid, 1.0, -LOWEST, ALU.subtract, ALU.mult))
            step(dve.memset(by_head(restart[:, 0:W])[:, :, :, 0], LOWEST))
            step(dve.memset(restart[:, W:W + 1], LOWEST))
            other = by_edge(loc)
            dve.tensor_tensor(differs[:, :, 1:P], other[:, :, 1:P], other[:, :, 0:P - 1], ALU.not_equal).then_inc(differs_ready, 1)
            dve.wait_ge(y_copied, C)
            step(dve.tensor_tensor(by_head(y), by_head(y), all_heads(pen), ALU.add))
            dve.wait_ge(restart_ready, 1)
            step(dve.tensor_tensor_scan(fwd, restart[:, 0:W], y, LOWEST, ALU.add, ALU.max))
            step(dve.tensor_tensor_scan(bwd[:, ::-1], restart[:, W:0:-1], y[:, ::-1], LOWEST, ALU.add, ALU.max))
            step(dve.tensor_copy(ends[:, 0, :, :], by_head(fwd)[:, :, :, P - 1]))
            step(dve.tensor_copy(ends[:, 1, :, :], by_head(bwd)[:, :, :, 0]))
            for k, edge, none in ((2, P - 1, 2.0), (3, 0, 1.0)):
                shape = [P, C, H]
                at = by_edge(loc)[:, :, edge:edge + 1].broadcast_to(shape)
                step(dve.tensor_scalar(ends[:, k, :, :], at, none, None, ALU.add))
                step(dve.tensor_tensor(ends[:, k, :, :], ends[:, k, :, :], by_edge(valid)[:, :, edge:edge + 1].broadcast_to(shape), ALU.mult))
                step(dve.tensor_scalar(ends[:, k, :, :], ends[:, k, :, :], none, None, ALU.subtract))
            dve.sem_inc(ends_ready, 1)
            dve.wait_ge(ends_copied, 4)
            leave_end, leave_start, last_node, first_node = rows
            step(dve.memset(cont[:, :], 0.0))
            step(dve.tensor_tensor(cont[:, 1:S], first_node[:, 1:S], last_node[:, 0:S - 1], ALU.is_equal))
            step(dve.tensor_tensor(first_node[:, :], first_node[:, :], last_node[:, :], ALU.is_equal))
            for k, shift in ((0, 0), (1, 1)):
                step(dve.tensor_tensor(reach[:, :], first_node[:, :], cont[:, shift:shift + S], ALU.mult))
                step(dve.tensor_scalar(reach[:, :], reach[:, :], 1.0, -LOWEST, ALU.subtract, ALU.mult))
                if k == 0:
                    step(dve.tensor_tensor_scan(leave_end[:, :], reach[:, :], leave_end[:, :], LOWEST, ALU.add, ALU.max))
                else:
                    step(dve.tensor_tensor_scan(leave_start[:, ::-1], reach[:, ::-1], leave_start[:, ::-1], LOWEST, ALU.add, ALU.max))
            step(dve.tensor_scalar(cont[:, :], cont[:, :], 1.0, -LOWEST, ALU.subtract, ALU.mult))
            step(dve.memset(carry[0][:, 0:1], LOWEST))
            step(dve.memset(carry[1][:, S - 1:S], LOWEST))
            step(dve.tensor_tensor(carry[0][:, 1:S], leave_end[:, 0:S - 1], cont[:, 1:S], ALU.add))
            step(dve.tensor_tensor(carry[1][:, 0:S - 1], leave_start[:, 1:S], cont[:, 1:S], ALU.add))
            dve.sem_inc(carry_ready, 1)
            dve.wait_ge(carry_turned, 1)
            for k, edge in ((0, 0), (1, P - 1)):
                step(dve.tensor_copy(ends[:, k, :, :], by_head(y)[:, :, :, edge]))
                step(dve.tensor_tensor(by_head(y)[:, :, :, edge], by_head(y)[:, :, :, edge], ps_carry[:, k, :, :], ALU.max))
            step(dve.tensor_tensor_scan(fwd, restart[:, 0:W], y, LOWEST, ALU.add, ALU.max))
            step(dve.tensor_tensor_scan(bwd[:, ::-1], restart[:, W:0:-1], y[:, ::-1], LOWEST, ALU.add, ALU.max))
            for k, edge in ((0, 0), (1, P - 1)):
                step(dve.tensor_copy(by_head(y)[:, :, :, edge], ends[:, k, :, :]))
            step(dve.tensor_tensor(fwd, fwd, bwd, ALU.max))
            for c in range(C):
                cols = slice(c * P * H, (c + 1) * P * H)
                dve.tensor_tensor(y[:, cols], y[:, cols], fwd[:, cols], ALU.subtract).then_inc(less_max, 1)
            dve.wait_ge(less_max, C)
            dve.memset(fwd, 0.0)


def aggregate(nc, t):
    with ExitStack() as ctx:
        def sb(name, shape, dt=fp32):
            return ctx.enter_context(nc.sbuf_tensor(name, shape, dt))

        def sem(name):
            return ctx.enter_context(nc.semaphore(name))

        tab = t["node_tab"]
        index = [sb(f"a_index{u}", [P, U], i32) for u in range(V)]
        rows = [sb(f"a_rows{u}", [P, U, D]) for u in range(V)]
        hot = [sb(f"a_hot{u}", [P, U, P]) for u in range(2)]
        terms = [sb(f"a_terms{u}", [P, U, AW]) for u in range(2)]
        ps_sum = [ctx.enter_context(nc.psum_tensor(f"ps_sum{u}", [P, U, 512], fp32)) for u in range(2)]
        index_ready, rows_in, rows_used = sem("a_index_ready"), [sem(f"a_rows_in{u}") for u in range(V)], sem("a_rows_used")
        hot_ready, weights_ready, summed, added = sem("a_hot_ready"), sem("a_weights_ready"), sem("a_summed"), sem("a_added")
        pool_turn, cleared = sem("a_pool_turn"), sem("a_cleared")
        block = ctx.enter_context(nc.Block())

        @block.gpsimd
        def _(pool):
            def turn(i):
                for u in range(V):
                    g = V * i + u
                    pool.wait_ge(index_ready, g + 1)
                    if not early(i, 1):
                        pool.wait_ge(rows_used, g - V + 1)
                    pool.sem_inc(pool_turn, 1)
                    for k in range(U):
                        pool.indirect_dma_start(out=rows[u][:, k, :], out_offset=None, in_=t["v_rows"],
                                                in_offset=bass.IndirectOffsetOnAxis(ap=index[u][:, k:k + 1], axis=0))\
                            .then_inc(rows_in[u], 16)

            group_turns(pool, turn)

        @block.scalar
        def _(act):
            def set_index(g, u, i):
                if not early(i, 1):
                    act.wait_ge(rows_in[u], 16 * U * i)
                nc.scalar.copy(index[u][:, :], t["other0"][:, bass.ds(g * U, U)]).then_inc(index_ready, 1)

            for g in range(AHEAD):
                set_index(g, g, 0)

            def turn(i):
                for u in range(V):
                    g = V * i + u
                    if not (isinstance(g, int) and g + AHEAD >= G):
                        set_index(g + AHEAD, (u + AHEAD) % V, i + (u + AHEAD) // V)
                    if not early(g):
                        act.wait_ge(summed, g - 1)
                    nc.scalar.copy(terms[u % 2][:, :, D:AW],
                                   t["score"][:, bass.ds(g * U * H, U * H)].rearrange("p (k h) -> p k h", h=H))\
                        .then_inc(weights_ready, 1)

            group_turns(act, turn)

        @block.vector
        def _(dve):
            def weigh(g, u, i):
                if not early(g):
                    dve.wait_ge(summed, g - 1)
                local = t["local0"][:, bass.ds(g * U, U)].unsqueeze(2).broadcast_to([P, U, P])
                dve.tensor_tensor(hot[u % 2][:, :, :], t["iota"][:, :].unsqueeze(1).broadcast_to([P, U, P]), local, ALU.is_equal)\
                    .then_inc(hot_ready, 1)
                dve.wait_ge(rows_in[u], 16 * U * (i + 1))
                weight = t["score"][:, bass.ds(g * U * H, U * H)].rearrange("p (k h) -> p k h", h=H)
                dve.tensor_tensor(terms[u % 2][:, :, 0:D].rearrange("p k (h d) -> p k h d", h=H),
                                  rows[u][:, :, :].rearrange("p k (h d) -> p k h d", h=H),
                                  weight.unsqueeze(3).broadcast_to([P, U, H, DH]), ALU.mult).then_inc(rows_used, 1)

            def add(g, u, places):
                for k in range(U):
                    dve.compute_val(places[k])
                dve.wait_ge(summed, g + 1)
                for k in range(U):
                    acc = tab[:, bass.ds(places[k], AW)]
                    if not (isinstance(g, int) and g == 0 and k == 0):
                        dve.wait_ge(added, g * U + k)
                    dve.tensor_tensor(acc, acc, ps_sum[u % 2][:, k, 0:AW], ALU.add).then_inc(added, 1)

            def turn(i):
                places = places_of(dve, t["packed_late0"], i, AW)
                for u in range(V):
                    g = V * i + u
                    if not early(g, LAG):
                        add(g - LAG, u - LAG, places[u * U:])
                    weigh(g, u, i)

            dve.memset(tab[:, 0:S * H], 0.0).then_inc(cleared, 1)
            dve.wait_ge(cleared, 1)
            group_turns(dve, turn)
            places = places_of(dve, t["packed_late0"], G // V, AW)
            for k in range(LAG):
                add(G - LAG + k, k, places[k * U:])
            dve.wait_ge(added, G * U)

        @block.tensor
        def _(pe):
            def turn(i):
                for u in range(V):
                    g = V * i + u
                    pe.wait_ge(hot_ready, g + 1)
                    pe.wait_ge(weights_ready, g + 1)
                    pe.wait_ge(rows_used, g + 1)
                    if not early(g):
                        pe.wait_ge(added, (g - 1) * U)
                    for k in range(U):
                        last = nc.tensor.matmul(ps_sum[u % 2][:, k, 0:AW], hot[u % 2][:, k, :], terms[u % 2][:, k, :],
                                                start=True, stop=True)
                    last.then_inc(summed, 1)

            group_turns(pe, turn)


def update_nodes(nc, t, wo, bo, gamma, beta, w1, b1, w2, b2, wa1, ba1, wa2, ba2):
    with ExitStack() as ctx:
        def sb(name, shape, dt=fp32):
            return ctx.enter_context(nc.sbuf_tensor(name, shape, dt))

        def ring(name, shape):
            return [sb(f"{name}{u}", shape) for u in range(4)]

        def pb(name, shape):
            return ctx.enter_context(nc.psum_tensor(name, shape, fp32))

        def sem(name):
            return ctx.enter_context(nc.semaphore(name))

        tab, ident, ones_h = t["node_tab"], t["ident"], t["ones_h"]
        w_o, w_12 = sb("w_o", [P, 2, D]), sb("w_12", [P, 2, 2 * D])
        wide = {n: sb(f"wide_{n}", [P, D]) for n in ("gamma", "beta", "wa1", "wa2")}
        ba = sb("ba", [P, 2])
        b_row, b_rest = (t["rel"][0:3 * D // P, P * k:P * (k + 1)] for k in range(2))
        b_part = [t["local0"][0:3 * D // P, :].bitcast(bf16)[:, P * k:P * (k + 1)] for k in range(3)]
        b_parts = sb("b_parts6", [3, 3 * D], bf16)
        x_in, v_in, xj = ring("n_x", [P, D]), ring("n_v", [P, D]), ring("n_xj", [P, XW])
        msg, y, z, x1 = ([t["score"][:, (4 * k + u) * D:(4 * k + u + 1) * D] for u in range(4)] for k in range(4))
        msg_t, x1_t = ring("n_msg_t", [P, 2, P]), ring("n_x1_t", [P, 2, P])
        h02, small = ring("n_h02", [P, 2 * D]), ring("n_small", [P, 48])
        junk, eps, zero = sb("junk", [P, D]), sb("n_eps", [P, 1]), sb("n_zero", [P, 1])
        ps_t = [pb(f"ps_t{k}", [P, 2, P]) for k in range(2)]
        ps_o = [pb(f"ps_o{k}", [P, D]) for k in range(2)]
        ps_h = [pb(f"ps_h{k}", [P, 2 * D]) for k in range(2)]
        weights_in, v_loaded, x_loaded = sem("n_weights_in"), [sem(f"n_v_loaded{u}") for u in range(4)], [sem(f"n_x_loaded{u}") for u in range(4)]
        msg_ready, msg_turned, msg_t_ready, o_ready = sem("msg_ready"), sem("msg_turned"), sem("msg_t_ready"), sem("o_ready")
        var_ready, std_ready, scale_ready, normed = ([sem(f"{n}{k}") for k in range(2)] for n in ("var_ready", "std_ready", "scale_ready", "normed"))
        z_ready, x1_turned, x1_t_ready, h_ready = sem("z_ready"), sem("x1_turned"), sem("x1_t_ready"), sem("h_ready")
        h02_ready, xj_ready, pads_set = sem("h02_ready"), sem("xj_ready"), sem("xj_pads_set")
        x1_stored, xj_stored = [sem(f"x1_stored{u}") for u in range(4)], [sem(f"xj_stored{u}") for u in range(4)]
        dve_step, pool_step = sem("dve_step6"), sem("pool_step6")
        dve_turn, b_parts_in = sem("n_turn"), sem("n_b_parts_in")
        block = ctx.enter_context(nc.Block())

        @block.sync
        def _(sp):
            sp.dma_start(w_o[:, :, :], wo.rearrange("(c p) n -> p c n", p=P)).then_inc(weights_in, 16)
            for k, (w, b) in enumerate(((w1, b1), (w2, b2))):
                sp.dma_start(w_12[:, :, k * D:(k + 1) * D], w.rearrange("(c p) n -> p c n", p=P)).then_inc(weights_in, 16)
                sp.dma_start(b_row[2 * k + 2:2 * k + 4, :], b.rearrange("(a n) -> a n", n=P)).then_inc(weights_in, 16)
            sp.dma_start(b_row[0:2, :], bo.rearrange("(a n) -> a n", n=P)).then_inc(weights_in, 16)
            for n, a in (("gamma", gamma), ("beta", beta), ("wa1", wa1), ("wa2", wa2)):
                sp.dma_start(wide[n][:, :], a.partition_broadcast(P)).then_inc(weights_in, 16)
            for k, a in enumerate((ba1, ba2)):
                sp.dma_start(ba[:, k:k + 1], a.partition_broadcast(P)).then_inc(weights_in, 16)

            def load_v(b, s):
                if not early(b, 4):
                    sp.wait_ge(msg_ready, b - 3)
                r = rows_of(b)
                sp.dma_start(v_in[s][0:r, :], t["v_rows"][bass.ds(b * P, r), :]).then_inc(v_loaded[s], 16)

            def load_x(b, s):
                if not early(b, 4):
                    sp.wait_ge(z_ready, b - 3)
                r = rows_of(b)
                sp.dma_start(x_in[s][0:r, :], t["x"][bass.ds(b * P, r), :]).then_inc(x_loaded[s], 16)

            def store_x1(b, s):
                r = rows_of(b)
                sp.wait_ge(normed[1], b + 1)
                sp.dma_start(t["x1_rows"][bass.ds(b * P, r), :], x1[s][0:r, :]).then_inc(x1_stored[s], 16)

            def store_xj(b, s):
                r = rows_of(b)
                sp.wait_ge(xj_ready, b + 1)
                sp.dma_start(t["xj_rows"][bass.ds(b * P, r), :], xj[s][0:r, :]).then_inc(xj_stored[s], 16)

            skewed(sp, [(0, load_v), (1, load_x), (6, store_x1), (9, store_xj)])
            for s in range(4):
                uses = len(range(s, NB, 4))
                sp.wait_ge(x1_stored[s], 16 * uses)
                sp.wait_ge(xj_stored[s], 16 * uses)

        @block.gpsimd
        def _(pool):
            step = Serial(pool, pool_step, 4 * 2)
            for s in range(4):
                nc.gpsimd.memset(xj[s][:, D:XW], 0.0).then_inc(pads_set, 1)
            nc.gpsimd.memset(eps[:, :], EPS).then_inc(pads_set, 1)
            nc.gpsimd.memset(zero[:, :], 0.0).then_inc(pads_set, 1)
            pool.wait_ge(weights_in, 12 * 16)
            split_exactly(nc.gpsimd, step, b_row, b_part, b_rest)
            for k in range(3):
                pool.dma_start(b_parts[k:k + 1, :], b_part[k]).then_inc(b_parts_in, 16)

            def affine(b, s):
                pool.wait_ge(normed[0], b + 1)
                step(nc.gpsimd.tensor_tensor(z[s][:, :], y[s][:, :], wide["gamma"][:, :], ALU.mult))
                step(nc.gpsimd.tensor_tensor(z[s][:, :], z[s][:, :], wide["beta"][:, :], ALU.add))
                nc.gpsimd.tensor_tensor(z[s][:, :], z[s][:, :], x_in[s][:, :], ALU.add).then_inc(z_ready, 1)

            skewed(pool, [(4, affine)], step)

        @block.scalar
        def _(act):
            act.wait_ge(pads_set, 6)

            def sqrt(k):
                def f(b, s):
                    act.wait_ge(var_ready[k], b + 1)
                    nc.scalar.activation(small[s][:, 16 + k:17 + k], small[s][:, 9 + 2 * k:10 + 2 * k], ACT.Sqrt, bias=eps[:, 0:1]).then_inc(std_ready[k], 1)
                return f

            def normalise(k):
                def f(b, s):
                    act.wait_ge(scale_ready[k], b + 1)
                    src, dst = ((y, y), (z, x1))[k]
                    if k and not early(b, 4):
                        act.wait_ge(x1_stored[s], (b - s) * 4)
                    if k and not early(b, 4):
                        act.wait_ge(x1_turned, b - 3)
                    nc.scalar.activation(dst[s][:, :], src[s][:, :], ACT.Identity, scale=small[s][:, 20 + 2 * k:21 + 2 * k],
                                         bias=small[s][:, 21 + 2 * k:22 + 2 * k]).then_inc(normed[k], 1)
                return f

            def copy_x1_t(b, s):
                act.wait_ge(x1_turned, b + 1)
                nc.scalar.copy(x1_t[s][:, :, :], ps_t[1][:, :, :]).then_inc(x1_t_ready, 1)

            def copy_msg_t(b, s):
                act.wait_ge(msg_turned, b + 1)
                nc.scalar.copy(msg_t[s][:, :, :], ps_t[0][:, :, :]).then_inc(msg_t_ready, 1)

            def fifth(b, s):
                act.wait_ge(h_ready, b + 1)
                nc.scalar.activation(h02[s][:, :], ps_h[s % 2][:, :], ACT.Copy, scale=0.2).then_inc(h02_ready, 1)

            def clear(b, s):
                nc.scalar.activation(tab[:, bass.ds(b * AW, D)], zero[:, 0:1].broadcast_to([P, D]), ACT.Copy)

            skewed(act, [(2, copy_msg_t), (2, clear), (4, sqrt(0)), (8, fifth), (4, normalise(0)), (6, copy_x1_t), (5, sqrt(1)), (5, normalise(1))])

        @block.tensor
        def _(pe):
            pe.wait_ge(weights_in, 12 * 16)
            pe.wait_ge(b_parts_in, 3 * 16)

            def turn_x1(b, s):
                pe.wait_ge(normed[1], b + 1)
                if not early(b, 1):
                    pe.wait_ge(x1_t_ready, b)
                for c in range(2):
                    last = nc.tensor.transpose(ps_t[1][:, c, :], x1[s][:, c * P:(c + 1) * P], ident[:, :])
                last.then_inc(x1_turned, 1)

            def turn_msg(b, s):
                pe.wait_ge(msg_ready, b + 1)
                if not early(b, 1):
                    pe.wait_ge(msg_t_ready, b)
                for c in range(2):
                    last = nc.tensor.transpose(ps_t[0][:, c, :], msg[s][:, c * P:(c + 1) * P], ident[:, :])
                last.then_inc(msg_turned, 1)

            def project_x1(b, s):
                pe.wait_ge(x1_t_ready, b + 1)
                if not early(b):
                    pe.wait_ge(xj_ready, b - 1)
                for c in range(2):
                    nc.tensor.matmul(ps_h[s % 2][:, :], x1_t[s][:, c, :], w_12[:, c, :], start=(c == 0), stop=False)
                nc.tensor.matmul(ps_h[s % 2][:, :], ones_h[0:3, :], b_parts[:, D:3 * D], start=False, stop=True).then_inc(h_ready, 1)

            def project_msg(b, s):
                pe.wait_ge(msg_t_ready, b + 1)
                if not early(b):
                    pe.wait_ge(var_ready[0], b - 1)
                for c in range(2):
                    nc.tensor.matmul(ps_o[s % 2][:, :], msg_t[s][:, c, :], w_o[:, c, :], start=(c == 0), stop=False)
                nc.tensor.matmul(ps_o[s % 2][:, :], ones_h[0:3, :], b_parts[:, 0:D], start=False, stop=True).then_inc(o_ready, 1)

            skewed(pe, [(2, turn_msg), (3, project_msg), (6, turn_x1), (7, project_x1)])

        @block.vector
        def _(dve):
            step = Serial(dve, dve_step, 4 * 10)
            dve.wait_ge(weights_in, 12 * 16)
            dve.wait_ge(pads_set, 6)

            def stats(k):
                def f(b, s):
                    v, m = (y, z)[k][s], small[s]
                    if k == 0:
                        dve.wait_ge(o_ready, b + 1)
                        dve.wait_ge(x_loaded[s], (b - s) * 4 + 16 if not isinstance(b, int) else 16 * (b // 4 + 1))
                        step(dve.tensor_tensor(v[:, :], ps_o[s % 2][:, :], x_in[s][:, :], ALU.add))
                    else:
                        dve.wait_ge(z_ready, b + 1)
                    step(dve.bn_stats(m[:, 24:30], v[:, :]))
                    dve.sem_inc(dve_turn, 1)
                    dve.bn_aggr(m[:, 8 + 2 * k:10 + 2 * k], m[:, 24:30]).then_inc(var_ready[k], 1)
                return f

            def scale(k):
                def f(b, s):
                    m = small[s]
                    dve.wait_ge(std_ready[k], b + 1)
                    step(dve.reciprocal(m[:, 20 + 2 * k:21 + 2 * k], m[:, 16 + k:17 + k]))
                    dve.scalar_tensor_tensor(m[:, 21 + 2 * k:22 + 2 * k], m[:, 8 + 2 * k:9 + 2 * k], -1.0, m[:, 20 + 2 * k:21 + 2 * k],
                                             ALU.mult, ALU.mult).then_inc(scale_ready[k], 1)
                return f

            def message(b, s):
                m, acc = small[s], tab[:, bass.ds(b * AW, D)]
                den = tab[:, bass.ds(b * AW + D, H)]
                dve.wait_ge(v_loaded[s], (b - s) * 4 + 16 if not isinstance(b, int) else 16 * (b // 4 + 1))
                dve.tensor_scalar(m[:, 0:H], den, 0.0, None, ALU.is_equal)
                step(dve.tensor_scalar(m[:, H:2 * H], den, 0.5, None, ALU.max))
                step(dve.reciprocal(m[:, H:2 * H], m[:, H:2 * H]))
                step(dve.tensor_tensor(msg[s][:, :].rearrange("p (h d) -> p h d", h=H), acc.rearrange("p (h d) -> p h d", h=H),
                                       m[:, H:2 * H].unsqueeze(2).broadcast_to([P, H, DH]), ALU.mult))
                dve.scalar_tensor_tensor(msg[s][:, :], v_in[s][:, :], m[:, 0:1], msg[s][:, :], ALU.mult, ALU.add).then_inc(msg_ready, 1)

            def scores(b, s):
                dve.wait_ge(h02_ready, b + 1)
                if not early(b, 4):
                    dve.wait_ge(xj_stored[s], (b - s) * 4 if not isinstance(b, int) else 16 * (b // 4))
                dve.tensor_tensor(h02[s][:, 0:D], ps_h[s % 2][:, 0:D], h02[s][:, 0:D], ALU.max)
                step(dve.tensor_tensor(xj[s][:, 0:D], ps_h[s % 2][:, D:2 * D], h02[s][:, D:2 * D], ALU.max))
                dve.tensor_tensor_reduce(junk[:, :], h02[s][:, 0:D], wide["wa1"][:, :], 1.0, 0.0, ALU.mult, ALU.add, small[s][:, 32:33])
                step(dve.tensor_tensor_reduce(h02[s][:, D:2 * D], xj[s][:, 0:D], wide["wa2"][:, :], 1.0, 0.0, ALU.mult, ALU.add, small[s][:, 33:34]))
                dve.tensor_tensor(t["a1_tab"][:, bass.ds(b, 1)], small[s][:, 32:33], ba[:, 0:1], ALU.add)
                dve.tensor_tensor(xj[s][:, D:D + 1], small[s][:, 33:34], ba[:, 1:2], ALU.add).then_inc(xj_ready, 1)

            skewed(dve, [(4, stats(0)), (1, message), (4, scale(0)), (5, stats(1)), (8, scores), (5, scale(1))], step)
            dve.wait_ge(xj_ready, NB)


def attend(nc, t):
    with ExitStack() as ctx:
        def sb(name, shape, dt=fp32):
            return ctx.enter_context(nc.sbuf_tensor(name, shape, dt))

        def sem(name):
            return ctx.enter_context(nc.semaphore(name))

        tab = t["node_tab"]
        index = [sb(f"t_index{u}", [P, U], i32) for u in range(V)]
        rows = [sb(f"t_rows{u}", [P, U, XW]) for u in range(V)]
        hot = [sb(f"t_hot{u}", [P, U, P]) for u in range(4)]
        node_hot = [sb(f"t_node_hot{u}", [P, U, P]) for u in range(2)]
        hot_att = [sb(f"t_hot_att{u}", [P, U, P]) for u in range(2)]
        logit = [sb(f"t_logit{u}", [P, U]) for u in range(2)]
        att = [sb(f"t_att{u}", [P, U]) for u in range(2)]
        ps_hot = ctx.enter_context(nc.psum_tensor("ps_hot", [P, U, P], fp32))
        ps_a1 = [ctx.enter_context(nc.psum_tensor(f"ps_a1{u}", [P, U], fp32)) for u in range(2)]
        ps_sum = [ctx.enter_context(nc.psum_tensor(f"ps_xsum{u}", [P, U, D], fp32)) for u in range(2)]
        index_ready, rows_in = sem("t_index_ready"), [sem(f"t_rows_in{u}") for u in range(V)]
        hot_ready, turned, turned_copied, a1_ready = sem("t_hot_ready"), sem("t_turned"), sem("t_turned_copied"), sem("t_a1_ready")
        logit_ready, att_ready, hot_att_ready, summed, added = sem("logit_ready"), sem("att_ready"), sem("hot_att_ready"), sem("t_summed"), sem("t_added")
        pool_turn = sem("t_pool_turn")
        block = ctx.enter_context(nc.Block())

        @block.gpsimd
        def _(pool):
            def turn(i):
                for u in range(V):
                    g = V * i + u
                    pool.wait_ge(index_ready, g + 1)
                    if not early(i, 1):
                        pool.wait_ge(summed, g - V + 1)
                    pool.sem_inc(pool_turn, 1)
                    for k in range(U):
                        pool.indirect_dma_start(out=rows[u][:, k, :], out_offset=None, in_=t["xj_rows"],
                                                in_offset=bass.IndirectOffsetOnAxis(ap=index[u][:, k:k + 1], axis=0))\
                            .then_inc(rows_in[u], 16)

            group_turns(pool, turn)

        @block.scalar
        def _(act):
            def set_index(g, u, i):
                if not early(i, 1):
                    act.wait_ge(rows_in[u], 16 * U * i)
                nc.scalar.copy(index[u][:, :], t["other1"][:, bass.ds(g * U, U)]).then_inc(index_ready, 1)

            for g in range(AHEAD):
                set_index(g, g, 0)

            def turn(i):
                for u in range(V):
                    g = V * i + u
                    if not (isinstance(g, int) and g + AHEAD >= G):
                        set_index(g + AHEAD, (u + AHEAD) % V, i + (u + AHEAD) // V)
                    act.wait_ge(turned, g + 1)
                    if not early(g):
                        act.wait_ge(a1_ready, g - 1)
                    nc.scalar.copy(node_hot[u % 2][:, :, :], ps_hot[:, :, :]).then_inc(turned_copied, 1)
                    if not early(g, 1):
                        weigh(g - 1, u - 1)

            def weigh(g, u):
                act.wait_ge(logit_ready, g + 1)
                nc.scalar.activation(att[u % 2][:, :], logit[u % 2][:, :], ACT.Sigmoid).then_inc(att_ready, 1)
                act.wait_ge(att_ready, g + 1)
                if not early(g):
                    act.wait_ge(summed, g - 1)
                for k in range(U):
                    last = nc.scalar.activation(hot_att[u % 2][:, k, :], hot[u % 4][:, k, :], ACT.Copy, scale=att[u % 2][:, k:k + 1])
                last.then_inc(hot_att_ready, 1)

            group_turns(act, turn)
            weigh(G - 1, V - 1)

        @block.vector
        def _(dve):
            def encode(g, u):
                if not early(g, 4):
                    dve.wait_ge(hot_att_ready, g - 3)
                local = t["local1"][:, bass.ds(g * U, U)].unsqueeze(2).broadcast_to([P, U, P])
                dve.tensor_tensor(hot[u % 4][:, :, :], t["iota"][:, :].unsqueeze(1).broadcast_to([P, U, P]), local, ALU.is_equal)\
                    .then_inc(hot_ready, 1)

            def add_logits(g, u, i):
                dve.wait_ge(rows_in[u], 16 * U * (i + 1))
                dve.wait_ge(a1_ready, g + 1)
                dve.tensor_tensor(logit[u % 2][:, :], ps_a1[u % 2][:, :], rows[u][:, :, D], ALU.add).then_inc(logit_ready, 1)

            def add(g, u, places):
                for k in range(U):
                    dve.compute_val(places[k])
                dve.wait_ge(summed, g + 1)
                for k in range(U):
                    acc = tab[:, bass.ds(places[k], D)]
                    if not (isinstance(g, int) and g == 0 and k == 0):
                        dve.wait_ge(added, g * U + k)
                    dve.tensor_tensor(acc, acc, ps_sum[u % 2][:, k, :], ALU.add).then_inc(added, 1)

            def turn(i):
                places = places_of(dve, t["packed_late1"], i, AW)
                for u in range(V):
                    g = V * i + u
                    if not (isinstance(g, int) and g + 2 >= G):
                        encode(g + 2, u + 2)
                    add_logits(g, u, i)
                    if not early(g, LAG):
                        add(g - LAG, u - LAG, places[u * U:])

            encode(0, 0)
            encode(1, 1)
            group_turns(dve, turn)
            places = places_of(dve, t["packed_late1"], G // V, AW)
            for k in range(LAG):
                add(G - LAG + k, k, places[k * U:])
            dve.wait_ge(added, G * U)

        @block.tensor
        def _(pe):
            def turn_hot(g, u):
                pe.wait_ge(hot_ready, g + 1)
                if not early(g, 1):
                    pe.wait_ge(turned_copied, g)
                for k in range(U):
                    last = nc.tensor.transpose(ps_hot[:, k, :], hot[u % 4][:, k, :], t["ident"][:, :])
                last.then_inc(turned, 1)

            def sum_up(g, u):
                pe.wait_ge(hot_att_ready, g + 1)
                if not early(g):
                    pe.wait_ge(added, (g - 1) * U)
                for k in range(U):
                    last = nc.tensor.matmul(ps_sum[u % 2][:, k, :], hot_att[u % 2][:, k, :], rows[u % V][:, k, 0:D], start=True, stop=True)
                last.then_inc(summed, 1)

            def turn(i):
                places = places_of(pe, t["packed1"], i, 1)
                for u in range(V):
                    g = V * i + u
                    if not (isinstance(g, int) and g == G - 1):
                        turn_hot(g + 1, u + 1)
                    pe.wait_ge(turned_copied, g + 1)
                    if not early(g):
                        pe.wait_ge(logit_ready, g - 1)
                    for k in range(U):
                        last = nc.tensor.matmul(ps_a1[u % 2][:, k:k + 1], node_hot[u % 2][:, k, :],
                                                t["a1_tab"][:, bass.ds(places[u * U + k], 1)], start=True, stop=True)
                    last.then_inc(a1_ready, 1)
                    if not early(g, 1):
                        sum_up(g - 1, u - 1)

            turn_hot(0, 0)
            group_turns(pe, turn)
            sum_up(G - 1, V - 1)


def finish(nc, t):
    with ExitStack() as ctx:
        def ring(name, shape):
            return [ctx.enter_context(nc.sbuf_tensor(f"{name}{u}", shape, fp32)) for u in range(4)]

        def sem(name):
            return ctx.enter_context(nc.semaphore(name))

        tab = t["node_tab"]
        x1, y, small = ring("f_x1", [P, D]), ring("f_y", [P, D]), ring("f_small", [P, 16])
        eps, eps_set = ctx.enter_context(nc.sbuf_tensor("f_eps", [P, 1], fp32)), sem("f_eps_set")
        loaded, stored = [sem(f"f_loaded{u}") for u in range(4)], [sem(f"f_stored{u}") for u in range(4)]
        var_ready, std_ready, scale_ready, normed, dve_step = sem("f_var"), sem("f_std"), sem("f_scale"), sem("f_normed"), sem("f_dve_step")
        dve_turn = sem("f_turn")
        block = ctx.enter_context(nc.Block())

        @block.sync
        def _(sp):
            def load(b, s):
                if not early(b, 4):
                    sp.wait_ge(var_ready, b - 3)
                r = rows_of(b)
                sp.dma_start(x1[s][0:r, :], t["x1_rows"][bass.ds(b * P, r), :]).then_inc(loaded[s], 16)

            def store(b, s):
                r = rows_of(b)
                sp.wait_ge(normed, b + 1)
                sp.dma_start(t["out"][bass.ds(b * P, r), :], y[s][0:r, :]).then_inc(stored[s], 16)

            skewed(sp, [(0, load), (4, store)])
            for s in range(4):
                sp.wait_ge(stored[s], 16 * len(range(s, NB, 4)))

        @block.scalar
        def _(act):
            act.wait_ge(eps_set, 1)

            def sqrt(b, s):
                act.wait_ge(var_ready, b + 1)
                nc.scalar.activation(small[s][:, 8:9], small[s][:, 7:8], ACT.Sqrt, bias=eps[:, 0:1]).then_inc(std_ready, 1)

            def normalise(b, s):
                act.wait_ge(scale_ready, b + 1)
                nc.scalar.activation(y[s][:, :], y[s][:, :], ACT.Identity, scale=small[s][:, 9:10], bias=small[s][:, 10:11]).then_inc(normed, 1)

            skewed(act, [(3, normalise), (2, sqrt)])

        @block.vector
        def _(dve):
            dve.memset(eps[:, :], EPS).then_inc(eps_set, 1)
            step = Serial(dve, dve_step, 4 * 3)

            def stats(b, s):
                m = small[s]
                dve.wait_ge(loaded[s], (b - s) * 4 + 16 if not isinstance(b, int) else 16 * (b // 4 + 1))
                if not early(b, 4):
                    dve.wait_ge(stored[s], (b - s) * 4 if not isinstance(b, int) else 16 * (b // 4))
                step(dve.scalar_tensor_tensor(y[s][:, :], x1[s][:, :], 2.0, tab[:, bass.ds(b * AW, D)], ALU.mult, ALU.add))
                step(dve.bn_stats(m[:, 0:6], y[s][:, :]))
                dve.sem_inc(dve_turn, 1)
                dve.bn_aggr(m[:, 6:8], m[:, 0:6]).then_inc(var_ready, 1)

            def scale(b, s):
                m = small[s]
                dve.wait_ge(std_ready, b + 1)
                step(dve.reciprocal(m[:, 9:10], m[:, 8:9]))
                dve.scalar_tensor_tensor(m[:, 10:11], m[:, 6:7], -1.0, m[:, 9:10], ALU.mult, ALU.mult).then_inc(scale_ready, 1)

            skewed(dve, [(2, stats), (3, scale)], step)


_INS = ["x", "src", "dst", "edge_type_64", "L0_gnn_query_emb", "L0_gnn_Wq", "L0_gnn_bq", "L0_gnn_Wk", "L0_gnn_bk",
        "L0_gnn_Wv", "L0_gnn_bv", "L0_gnn_rel_w", "L0_gnn_Wo", "L0_gnn_bo", "L0_gnn_gamma", "L0_gnn_beta",
        "L1_gnn_W1", "L1_gnn_b1", "L1_gnn_W2", "L1_gnn_b2", "L1_gnn_wa1", "L1_gnn_ba1", "L1_gnn_wa2", "L1_gnn_ba2"]


def kernel(**inputs):
    import numpy as _np
    import concourse.bacc as _bacc
    from concourse.bass_utils import run_bass_kernel_spmd as _run

    nc = _bacc.Bacc("TRN2", target_bir_lowering=False, num_devices=1)
    arrays, args = {}, []
    for name in _INS:
        a = _np.ascontiguousarray(inputs[name])
        arrays[f"in_{name}"] = a
        args.append(nc.dram_tensor(f"in_{name}", a.shape, mybir.dt.from_np(a.dtype), kind="ExternalInput").ap())
    out = nc.dram_tensor("out", (N, D), fp32, kind="ExternalOutput").ap()
    gnn_kernel(nc, *args, out)
    r = _run(nc, [arrays], core_ids=[0])
    return r.results[0]["out"]
```
